# Optimizing a Trainium2 kernel written in Bass

```python
import numpy as np
import jax
import jax.numpy as jnp

def _softmax(x, axis=-1):
    return jax.nn.softmax(x, axis=axis)

def _gelu(x):
    return jax.nn.gelu(x, approximate=True)

def _silu(x):
    return jax.nn.silu(x)

def _sigmoid(x):
    return jax.nn.sigmoid(x)

def _layernorm(x, axis=-1, eps=1e-05):
    m = jnp.mean(x, axis=axis, keepdims=True)
    v = jnp.var(x, axis=axis, keepdims=True)
    return (x - m) / jnp.sqrt(v + eps)

def _scatter_add(tgt, idx, src, axis=0):
    return tgt.at[idx].add(src)

def _segment_sum(src, seg, n):
    return jax.ops.segment_sum(src, seg, n)
kernel_name = 'mk_vit_tower_cls_d4_tok_img256_r4_79922d'

def setup_inputs(seed: int=0):
    np.random.seed(seed)
    _w = jnp.asarray

    def _rec_inputs():
        import jax
        import jax.numpy as jnp
        _rk = jax.random.key(seed)
        x = -0.00040386 + 0.999972 * jax.random.normal(jax.random.fold_in(_rk, 1), (64, 128, 64, 3), jnp.float32)
        cls_tok = 0.02 * jax.random.normal(jax.random.fold_in(_rk, 5), (1, 1, 64), jnp.float32)
        return (x, cls_tok)
    x, cls_tok = _rec_inputs()

    def _L0_tok_setup():
        import jax, jax.numpy as jnp
        import numpy as np
        B, T, J, LAT = (128, 128, 64, 64)
        EPS = 1e-05

        def layernorm(x, g, b):
            m = jnp.mean(x, axis=-1, keepdims=True)
            v = jnp.var(x, axis=-1, keepdims=True)
            return (x - m) * jax.lax.rsqrt(v + EPS) * g + b

        def conv2d(x, w, b, pad):
            y = jax.lax.conv_general_dilated(x, w, window_strides=(1, 1), padding=pad, dimension_numbers=('NCHW', 'OIHW', 'NCHW'))
            return y + b[None, :, None, None]
        key = jax.random.key(seed)
        ks = jax.random.split(key, 10)
        s = 0.02
        return {'x': jax.random.normal(ks[0], (B, T, J, 3), dtype=jnp.float32), 'ln0_g': jnp.ones((J * 3,), jnp.float32), 'ln0_b': jnp.zeros((J * 3,), jnp.float32), 'ln1_g': jnp.ones((J * 2,), jnp.float32), 'ln1_b': jnp.zeros((J * 2,), jnp.float32), 'conv1_w': jax.random.normal(ks[1], (T, T, 5, 3), jnp.float32) * s, 'conv1_b': jnp.zeros((T,), jnp.float32), 'conv2_w': jax.random.normal(ks[2], (T, T, 5, 2), jnp.float32) * s, 'conv2_b': jnp.zeros((T,), jnp.float32), 'conv3_w': jax.random.normal(ks[3], (2 * T, T, 5, 2), jnp.float32) * s, 'conv3_b': jnp.zeros((2 * T,), jnp.float32), 'out_w': jax.random.normal(ks[4], (2 * J, LAT), jnp.float32) * s, 'out_b': jnp.zeros((LAT,), jnp.float32)}
    _L0_tok_all = _L0_tok_setup()
    _L0_tok_in = {k: v for k, v in _L0_tok_all.items() if k in ('ln0_g', 'ln0_b', 'ln1_g', 'ln1_b', 'conv1_w', 'conv1_b', 'conv2_w', 'conv2_b', 'conv3_w', 'conv3_b', 'out_w', 'out_b')}
    del _L0_tok_all

    def _L0_attn_setup():
        import jax, jax.numpy as jnp
        import numpy as np
        IN_CHANNELS = 64
        SCALE = IN_CHANNELS ** (-0.5)
        key = jax.random.key(seed)
        k_x, k_we, k_wo = jax.random.split(key, 3)
        B, M, C, H3, NH = (4, 3072, 64, 192, 3)
        x = jax.random.normal(k_x, (B, M, C), dtype=jnp.float32)
        W_embed = jax.random.normal(k_we, (NH, H3, C), dtype=jnp.float32) * 0.01
        b_embed = jnp.zeros((NH, H3), dtype=jnp.float32)
        W_out = jax.random.normal(k_wo, (C, H3), dtype=jnp.float32) * 0.01
        b_out = jnp.zeros((C,), dtype=jnp.float32)
        return {'x': x, 'W_embed': W_embed, 'b_embed': b_embed, 'W_out': W_out, 'b_out': b_out}
    _L0_attn_all = _L0_attn_setup()
    _L0_attn_in = {k: v for k, v in _L0_attn_all.items() if k in ('W_embed', 'b_embed', 'W_out', 'b_out')}
    del _L0_attn_all

    def _L0_ffn_setup():
        import jax, jax.numpy as jnp
        import numpy as np
        B, S, D, E, H, K = (4, 1024, 64, 8, 128, 2)
        key = jax.random.key(seed)
        ks = jax.random.split(key, 6)
        x = jax.random.normal(ks[0], (B, S, D), jnp.float32)
        Wg = jax.random.normal(ks[1], (D, E), jnp.float32) * 0.02
        bg = jnp.zeros((E,), jnp.float32)
        W1 = jax.random.normal(ks[2], (E, D, H), jnp.float32) * 0.02
        b1 = jnp.zeros((E, H), jnp.float32)
        W2 = jax.random.normal(ks[3], (E, H, D), jnp.float32) * 0.02
        b2 = jnp.zeros((E, D), jnp.float32)
        return {'x': x, 'Wg': Wg, 'bg': bg, 'W1': W1, 'b1': b1, 'W2': W2, 'b2': b2}
    _L0_ffn_all = _L0_ffn_setup()
    _L0_ffn_in = {k: v for k, v in _L0_ffn_all.items() if k in ('Wg', 'bg', 'W1', 'b1', 'W2', 'b2')}
    del _L0_ffn_all

    def _L1_attn_setup():
        import jax, jax.numpy as jnp
        import numpy as np
        D, H, L, S_MAX = (64, 8, 4, 1024)
        DH = D // H
        FF = 4 * D
        B, S = (16, 1024)

        def _pe(seq_len, d):
            pos = jnp.arange(seq_len, dtype=jnp.float32)[:, None]
            div = jnp.exp(jnp.arange(0, d, 2, dtype=jnp.float32) * (-jnp.log(10000.0) / d))
            pe = jnp.zeros((seq_len, d), dtype=jnp.float32)
            pe = pe.at[:, 0::2].set(jnp.sin(pos * div))
            pe = pe.at[:, 1::2].set(jnp.cos(pos * div))
            return pe

        def _ln(x, g, b, eps=1e-05):
            mu = jnp.mean(x, axis=-1, keepdims=True)
            var = jnp.var(x, axis=-1, keepdims=True)
            return (x - mu) * jax.lax.rsqrt(var + eps) * g + b
        key = jax.random.key(seed)
        ks = jax.random.split(key, 12)
        s = 0.02
        return {'x': jax.random.normal(ks[0], (B, S, D), dtype=jnp.float32), 'Wq': jax.random.normal(ks[1], (L, D, D), dtype=jnp.float32) * s, 'Wk': jax.random.normal(ks[2], (L, D, D), dtype=jnp.float32) * s, 'Wv': jax.random.normal(ks[3], (L, D, D), dtype=jnp.float32) * s, 'Wo': jax.random.normal(ks[4], (L, D, D), dtype=jnp.float32) * s, 'bo': jnp.zeros((L, D), dtype=jnp.float32), 'g1': jnp.ones((L, D), dtype=jnp.float32), 'b1': jnp.zeros((L, D), dtype=jnp.float32), 'W1': jax.random.normal(ks[5], (L, D, FF), dtype=jnp.float32) * s, 'bf1': jnp.zeros((L, FF), dtype=jnp.float32), 'W2': jax.random.normal(ks[6], (L, FF, D), dtype=jnp.float32) * s, 'bf2': jnp.zeros((L, D), dtype=jnp.float32), 'g2': jnp.ones((L, D), dtype=jnp.float32), 'b2': jnp.zeros((L, D), dtype=jnp.float32)}
    _L1_attn_all = _L1_attn_setup()
    _L1_attn_in = {k: v for k, v in _L1_attn_all.items() if k in ('Wq', 'Wk', 'Wv', 'Wo', 'bo', 'g1', 'b1', 'W1', 'bf1', 'W2', 'bf2', 'g2', 'b2')}
    del _L1_attn_all

    def _L1_ffn_setup():
        import jax, jax.numpy as jnp
        import numpy as np
        B, S, D = (8, 1024, 64)
        H = 4 * D
        CAPACITY = 0.5
        key = jax.random.key(seed)
        ks = jax.random.split(key, 6)
        x = jax.random.normal(ks[0], (B, S, D), dtype=jnp.float32)
        attention_mask = jnp.zeros((B, 1, 1, S), dtype=jnp.float32)
        wr = jax.random.normal(ks[1], (D, 1), dtype=jnp.float32) * 0.02
        br = jnp.zeros((1,), dtype=jnp.float32)
        w1 = jax.random.normal(ks[2], (D, H), dtype=jnp.float32) * 0.02
        b1 = jnp.zeros((H,), dtype=jnp.float32)
        w2 = jax.random.normal(ks[3], (H, D), dtype=jnp.float32) * 0.02
        b2 = jnp.zeros((D,), dtype=jnp.float32)
        return {'x': x, 'attention_mask': attention_mask, 'wr': wr, 'br': br, 'w1': w1, 'b1': b1, 'w2': w2, 'b2': b2}
    _L1_ffn_all = _L1_ffn_setup()
    _L1_ffn_in = {k: v for k, v in _L1_ffn_all.items() if k in ('attention_mask', 'wr', 'br', 'w1', 'b1', 'w2', 'b2')}
    del _L1_ffn_all

    def _L2_attn_setup():
        import jax, jax.numpy as jnp
        import numpy as np
        DIM = 64
        HEADS = 4
        HEAD_DIM = DIM // HEADS
        SCALE = HEAD_DIM ** (-0.5)
        key = jax.random.key(seed)
        ks = jax.random.split(key, 9)
        B, N, C = (2, 1024, DIM)
        x = jax.random.normal(ks[0], (B, N, C), dtype=jnp.float32)
        lim = np.sqrt(6.0 / (C + C)).astype(np.float32)

        def w(k):
            return jax.random.uniform(k, (C, C), dtype=jnp.float32, minval=-lim, maxval=lim)
        return {'x': x, 'Wq': w(ks[1]), 'bq': jnp.zeros((C,), jnp.float32), 'Wk': w(ks[2]), 'bk': jnp.zeros((C,), jnp.float32), 'Wv': w(ks[3]), 'bv': jnp.zeros((C,), jnp.float32), 'Wo': w(ks[4]), 'bo': jnp.zeros((C,), jnp.float32)}
    _L2_attn_all = _L2_attn_setup()
    _L2_attn_in = {k: v for k, v in _L2_attn_all.items() if k in ('Wq', 'bq', 'Wk', 'bk', 'Wv', 'bv', 'Wo', 'bo')}
    del _L2_attn_all

    def _L2_ffn_setup():
        import jax, jax.numpy as jnp
        import numpy as np
        B, T, C = (64, 96, 64)
        NH, NKV = (4, 2)
        HD = C // NH
        NREP = NH // NKV
        NE, TOPK = (8, 2)
        HID = int(8 / 3 * C)
        EPS_RMS = 1e-06

        def _rope_tables(t_len):
            inv_freq = 1.0 / 10000.0 ** (np.arange(0, HD, 2, dtype=np.float32) / HD)
            t = np.arange(t_len, dtype=np.float32)
            freqs = np.outer(t, inv_freq)
            emb = np.concatenate([freqs, freqs], axis=-1)
            return (jnp.asarray(np.cos(emb)), jnp.asarray(np.sin(emb)))

        def _rotate_half(x):
            h = x.shape[-1] // 2
            return jnp.concatenate([-x[..., h:], x[..., :h]], axis=-1)

        def _rmsnorm(v, w):
            return v * jax.lax.rsqrt(jnp.mean(v * v, axis=-1, keepdims=True) + EPS_RMS) * w
        key = jax.random.key(seed)
        ks = jax.random.split(key, 10)
        s = lambda k, shape: jax.random.normal(k, shape, jnp.float32) * 0.02
        return {'x': jax.random.normal(ks[0], (B, T, C), jnp.float32), 'ln1_w': jnp.ones((C,), jnp.float32), 'ln2_w': jnp.ones((C,), jnp.float32), 'wq': s(ks[1], (NH * HD, C)), 'wk': s(ks[2], (NKV * HD, C)), 'wv': s(ks[3], (NKV * HD, C)), 'wo': s(ks[4], (C, C)), 'router_w': s(ks[5], (NE, C)), 'w1': s(ks[6], (NE, HID, C)), 'w2': s(ks[7], (NE, C, HID)), 'w3': s(ks[8], (NE, HID, C))}
    _L2_ffn_all = _L2_ffn_setup()
    _L2_ffn_in = {k: v for k, v in _L2_ffn_all.items() if k in ('ln1_w', 'ln2_w', 'wq', 'wk', 'wv', 'wo', 'router_w', 'w1', 'w2', 'w3')}
    del _L2_ffn_all

    def _L3_attn_setup():
        import jax, jax.numpy as jnp
        import numpy as np
        import math
        B, T, D_MODEL = (1, 512, 64)
        N_Q, N_KV = (16, 1)
        D_HEAD = D_MODEL // N_KV
        QPG = N_Q // N_KV
        ROPE_BASE = 10000.0
        WINDOW = 128
        EPS = 1.1920929e-07
        NEG = -1e+30

        def _rope(x, base=ROPE_BASE):
            t, d = (x.shape[-2], x.shape[-1])
            freqs = base ** (-2.0 * jnp.arange(d // 2, dtype=jnp.float32) / d)
            theta = jnp.arange(t, dtype=jnp.float32)[:, None] * freqs[None, :]
            cos, sin = (jnp.cos(theta), jnp.sin(theta))
            x1, x2 = (x[..., 0::2], x[..., 1::2])
            r1 = x1 * cos - x2 * sin
            r2 = x1 * sin + x2 * cos
            return jnp.stack([r1, r2], axis=-1).reshape(x.shape)

        def _rmsnorm(x, w):
            return x * jax.lax.rsqrt(jnp.mean(x * x, axis=-1, keepdims=True) + EPS) * w
        key = jax.random.key(seed)
        k0, k1, k2, k3 = jax.random.split(key, 4)
        x = jax.random.normal(k0, (B, T, D_MODEL), dtype=jnp.float32)
        wq = jax.random.normal(k1, (QPG * N_KV * D_HEAD, D_MODEL), dtype=jnp.float32) * 0.02
        wkv = jax.random.normal(k2, (2 * D_HEAD * N_KV, D_MODEL), dtype=jnp.float32) * 0.02
        wo = jax.random.normal(k3, (D_MODEL, D_HEAD * N_Q * N_KV), dtype=jnp.float32) * 0.02
        q_norm_w = jnp.ones((D_HEAD,), dtype=jnp.float32)
        k_norm_w = jnp.ones((D_HEAD,), dtype=jnp.float32)
        return {'x': x, 'wq': wq, 'wkv': wkv, 'wo': wo, 'q_norm_w': q_norm_w, 'k_norm_w': k_norm_w}
    _L3_attn_all = _L3_attn_setup()
    _L3_attn_in = {k: v for k, v in _L3_attn_all.items() if k in ('wq', 'wkv', 'wo', 'q_norm_w', 'k_norm_w')}
    del _L3_attn_all

    def _L3_ffn_setup():
        import math
        import jax, jax.numpy as jnp
        import numpy as np
        CAPACITY_FACTOR = 1.25
        key = jax.random.key(seed)
        ks = jax.random.split(key, 5)
        B, L, D, F, E = (8, 2048, 64, 256, 8)
        h = jax.random.normal(ks[0], (B, L, D), dtype=jnp.float32)
        gate_w = jax.random.normal(ks[1], (D, E), dtype=jnp.float32) * 0.02
        gate_b = jnp.zeros((E,), dtype=jnp.float32)
        w1 = jax.random.normal(ks[2], (E, D, F), dtype=jnp.float32) * (1.0 / math.sqrt(D))
        b1 = jnp.zeros((E, F), dtype=jnp.float32)
        w2 = jax.random.normal(ks[3], (E, F, D), dtype=jnp.float32) * (1.0 / math.sqrt(F))
        b2 = jnp.zeros((E, D), dtype=jnp.float32)
        return {'h': h, 'gate_w': gate_w, 'gate_b': gate_b, 'w1': w1, 'b1': b1, 'w2': w2, 'b2': b2}
    _L3_ffn_all = _L3_ffn_setup()
    _L3_ffn_in = {k: v for k, v in _L3_ffn_all.items() if k in ('gate_w', 'gate_b', 'w1', 'b1', 'w2', 'b2')}
    del _L3_ffn_all
    return {'x': x, 'cls_tok': cls_tok, 'L0_tok_ln0_g': _L0_tok_in['ln0_g'], 'L0_tok_ln0_b': _L0_tok_in['ln0_b'], 'L0_tok_ln1_g': _L0_tok_in['ln1_g'], 'L0_tok_ln1_b': _L0_tok_in['ln1_b'], 'L0_tok_conv1_w': _L0_tok_in['conv1_w'], 'L0_tok_conv1_b': _L0_tok_in['conv1_b'], 'L0_tok_conv2_w': _L0_tok_in['conv2_w'], 'L0_tok_conv2_b': _L0_tok_in['conv2_b'], 'L0_tok_conv3_w': _L0_tok_in['conv3_w'], 'L0_tok_conv3_b': _L0_tok_in['conv3_b'], 'L0_tok_out_w': _L0_tok_in['out_w'], 'L0_tok_out_b': _L0_tok_in['out_b'], 'L0_attn_W_embed': _L0_attn_in['W_embed'], 'L0_attn_b_embed': _L0_attn_in['b_embed'], 'L0_attn_W_out': _L0_attn_in['W_out'], 'L0_attn_b_out': _L0_attn_in['b_out'], 'L0_ffn_Wg': _L0_ffn_in['Wg'], 'L0_ffn_bg': _L0_ffn_in['bg'], 'L0_ffn_W1': _L0_ffn_in['W1'], 'L0_ffn_b1': _L0_ffn_in['b1'], 'L0_ffn_W2': _L0_ffn_in['W2'], 'L0_ffn_b2': _L0_ffn_in['b2'], 'L1_attn_Wq': _L1_attn_in['Wq'], 'L1_attn_Wk': _L1_attn_in['Wk'], 'L1_attn_Wv': _L1_attn_in['Wv'], 'L1_attn_Wo': _L1_attn_in['Wo'], 'L1_attn_bo': _L1_attn_in['bo'], 'L1_attn_g1': _L1_attn_in['g1'], 'L1_attn_b1': _L1_attn_in['b1'], 'L1_attn_W1': _L1_attn_in['W1'], 'L1_attn_bf1': _L1_attn_in['bf1'], 'L1_attn_W2': _L1_attn_in['W2'], 'L1_attn_bf2': _L1_attn_in['bf2'], 'L1_attn_g2': _L1_attn_in['g2'], 'L1_attn_b2': _L1_attn_in['b2'], 'L1_ffn_attention_mask': _L1_ffn_in['attention_mask'], 'L1_ffn_wr': _L1_ffn_in['wr'], 'L1_ffn_br': _L1_ffn_in['br'], 'L1_ffn_w1': _L1_ffn_in['w1'], 'L1_ffn_b1': _L1_ffn_in['b1'], 'L1_ffn_w2': _L1_ffn_in['w2'], 'L1_ffn_b2': _L1_ffn_in['b2'], 'L2_attn_Wq': _L2_attn_in['Wq'], 'L2_attn_bq': _L2_attn_in['bq'], 'L2_attn_Wk': _L2_attn_in['Wk'], 'L2_attn_bk': _L2_attn_in['bk'], 'L2_attn_Wv': _L2_attn_in['Wv'], 'L2_attn_bv': _L2_attn_in['bv'], 'L2_attn_Wo': _L2_attn_in['Wo'], 'L2_attn_bo': _L2_attn_in['bo'], 'L2_ffn_ln1_w': _L2_ffn_in['ln1_w'], 'L2_ffn_ln2_w': _L2_ffn_in['ln2_w'], 'L2_ffn_wq': _L2_ffn_in['wq'], 'L2_ffn_wk': _L2_ffn_in['wk'], 'L2_ffn_wv': _L2_ffn_in['wv'], 'L2_ffn_wo': _L2_ffn_in['wo'], 'L2_ffn_router_w': _L2_ffn_in['router_w'], 'L2_ffn_w1': _L2_ffn_in['w1'], 'L2_ffn_w2': _L2_ffn_in['w2'], 'L2_ffn_w3': _L2_ffn_in['w3'], 'L3_attn_wq': _L3_attn_in['wq'], 'L3_attn_wkv': _L3_attn_in['wkv'], 'L3_attn_wo': _L3_attn_in['wo'], 'L3_attn_q_norm_w': _L3_attn_in['q_norm_w'], 'L3_attn_k_norm_w': _L3_attn_in['k_norm_w'], 'L3_ffn_gate_w': _L3_ffn_in['gate_w'], 'L3_ffn_gate_b': _L3_ffn_in['gate_b'], 'L3_ffn_w1': _L3_ffn_in['w1'], 'L3_ffn_b1': _L3_ffn_in['b1'], 'L3_ffn_w2': _L3_ffn_in['w2'], 'L3_ffn_b2': _L3_ffn_in['b2']}

def reference(x, cls_tok, L0_tok_ln0_g, L0_tok_ln0_b, L0_tok_ln1_g, L0_tok_ln1_b, L0_tok_conv1_w, L0_tok_conv1_b, L0_tok_conv2_w, L0_tok_conv2_b, L0_tok_conv3_w, L0_tok_conv3_b, L0_tok_out_w, L0_tok_out_b, L0_attn_W_embed, L0_attn_b_embed, L0_attn_W_out, L0_attn_b_out, L0_ffn_Wg, L0_ffn_bg, L0_ffn_W1, L0_ffn_b1, L0_ffn_W2, L0_ffn_b2, L1_attn_Wq, L1_attn_Wk, L1_attn_Wv, L1_attn_Wo, L1_attn_bo, L1_attn_g1, L1_attn_b1, L1_attn_W1, L1_attn_bf1, L1_attn_W2, L1_attn_bf2, L1_attn_g2, L1_attn_b2, L1_ffn_attention_mask, L1_ffn_wr, L1_ffn_br, L1_ffn_w1, L1_ffn_b1, L1_ffn_w2, L1_ffn_b2, L2_attn_Wq, L2_attn_bq, L2_attn_Wk, L2_attn_bk, L2_attn_Wv, L2_attn_bv, L2_attn_Wo, L2_attn_bo, L2_ffn_ln1_w, L2_ffn_ln2_w, L2_ffn_wq, L2_ffn_wk, L2_ffn_wv, L2_ffn_wo, L2_ffn_router_w, L2_ffn_w1, L2_ffn_w2, L2_ffn_w3, L3_attn_wq, L3_attn_wkv, L3_attn_wo, L3_attn_q_norm_w, L3_attn_k_norm_w, L3_ffn_gate_w, L3_ffn_gate_b, L3_ffn_w1, L3_ffn_b1, L3_ffn_w2, L3_ffn_b2):
    import jax
    import jax.numpy as jnp

    def _L0_tok_ref(x, ln0_g, ln0_b, ln1_g, ln1_b, conv1_w, conv1_b, conv2_w, conv2_b, conv3_w, conv3_b, out_w, out_b):
        import jax, jax.numpy as jnp
        import numpy as np
        B, T, J, LAT = (128, 128, 64, 64)
        EPS = 1e-05

        def layernorm(x, g, b):
            m = jnp.mean(x, axis=-1, keepdims=True)
            v = jnp.var(x, axis=-1, keepdims=True)
            return (x - m) * jax.lax.rsqrt(v + EPS) * g + b

        def conv2d(x, w, b, pad):
            y = jax.lax.conv_general_dilated(x, w, window_strides=(1, 1), padding=pad, dimension_numbers=('NCHW', 'OIHW', 'NCHW'))
            return y + b[None, :, None, None]
        b, t, j, d = x.shape
        h = layernorm(x.reshape(b, t, j * 3), ln0_g, ln0_b).reshape(b, t, j, 3)
        h = jax.nn.relu(conv2d(h, conv1_w, conv1_b, ((2, 2), (1, 1))))
        h = layernorm(h.reshape(b, t, j * 3), ln0_g, ln0_b).reshape(b, t, j, 3)
        h = jax.nn.relu(conv2d(h, conv2_w, conv2_b, ((2, 2), (0, 0))))
        h = layernorm(h.reshape(b, t, j * 2), ln1_g, ln1_b).reshape(b, t, j, 2)
        h = jax.nn.relu(conv2d(h, conv3_w, conv3_b, ((2, 2), (0, 0))))
        h = h.reshape(b, 2 * t, j)
        res = jnp.concatenate([h[:, :t, :], h[:, t:, :]], axis=2)
        res = layernorm(res, ln1_g, ln1_b)
        return res @ out_w + out_b

    def _L0_attn_ref(x, W_embed, b_embed, W_out, b_out):
        import jax, jax.numpy as jnp
        import numpy as np
        IN_CHANNELS = 64
        SCALE = IN_CHANNELS ** (-0.5)

        def head(W, b):
            e = jnp.einsum('bmc,hc->bmh', x, W) + b
            q, k, v = jnp.split(e, 3, axis=1)
            attn = jax.nn.softmax(jnp.einsum('bmd,bnd->bmn', q, k) * SCALE, axis=-1)
            return jnp.einsum('bmn,bnd->bmd', attn, v)
        outs = jax.vmap(head)(W_embed, b_embed)
        qkv = jnp.concatenate([outs[i] for i in range(outs.shape[0])], axis=1)
        out = jnp.einsum('bmd,cd->bmc', qkv, W_out) + b_out
        return out + x

    def _L0_ffn_ref(x, Wg, bg, W1, b1, W2, b2):
        import jax, jax.numpy as jnp
        import numpy as np
        B, S, D, E, H, K = (4, 1024, 64, 8, 128, 2)
        Bv, Sv, Dv = x.shape
        gate_scores = x @ Wg + bg
        _, idx = jax.lax.top_k(gate_scores, K)
        mask = jax.nn.one_hot(idx, E, dtype=x.dtype).sum(axis=-2)
        xf = x.reshape(-1, Dv)
        mf = mask.reshape(-1, E)
        h = jax.nn.gelu(jnp.einsum('td,edh->teh', xf, W1) + b1[None], approximate=False)
        y = jnp.einsum('teh,ehd->ted', h, W2) + b2[None]
        out = jnp.einsum('ted,te->td', y, mf)
        return out.reshape(Bv, Sv, Dv)

    def _L1_attn_ref(x, Wq, Wk, Wv, Wo, bo, g1, b1, W1, bf1, W2, bf2, g2, b2):
        import jax, jax.numpy as jnp
        import numpy as np
        D, H, L, S_MAX = (64, 8, 4, 1024)
        DH = D // H
        FF = 4 * D
        B, S = (16, 1024)

        def _pe(seq_len, d):
            pos = jnp.arange(seq_len, dtype=jnp.float32)[:, None]
            div = jnp.exp(jnp.arange(0, d, 2, dtype=jnp.float32) * (-jnp.log(10000.0) / d))
            pe = jnp.zeros((seq_len, d), dtype=jnp.float32)
            pe = pe.at[:, 0::2].set(jnp.sin(pos * div))
            pe = pe.at[:, 1::2].set(jnp.cos(pos * div))
            return pe

        def _ln(x, g, b, eps=1e-05):
            mu = jnp.mean(x, axis=-1, keepdims=True)
            var = jnp.var(x, axis=-1, keepdims=True)
            return (x - mu) * jax.lax.rsqrt(var + eps) * g + b
        b, s, d = x.shape
        x = x + _pe(s, d)[None, :, :]
        scale = DH ** (-0.5)
        for l in range(L):
            h = _ln(x, g1[l], b1[l])
            q = (h @ Wq[l]).reshape(b, s, H, DH).transpose(0, 2, 1, 3)
            k = (h @ Wk[l]).reshape(b, s, H, DH).transpose(0, 2, 1, 3)
            v = (h @ Wv[l]).reshape(b, s, H, DH).transpose(0, 2, 1, 3)
            q = jax.nn.softmax(q, axis=-1) * scale
            k = jax.nn.softmax(k, axis=-2)
            ctx = jnp.einsum('bhnd,bhne->bhde', k, v)
            attn = jnp.einsum('bhnd,bhde->bhne', q, ctx)
            attn = attn.transpose(0, 2, 1, 3).reshape(b, s, d)
            x = x + attn @ Wo[l] + bo[l]
            h = _ln(x, g2[l], b2[l])
            x = x + jax.nn.gelu(h @ W1[l] + bf1[l], approximate=False) @ W2[l] + bf2[l]
        return x

    def _L1_ffn_ref(x, attention_mask, wr, br, w1, b1, w2, b2):
        import jax, jax.numpy as jnp
        import numpy as np
        B, S, D = (8, 1024, 64)
        H = 4 * D
        CAPACITY = 0.5
        b, s, d = x.shape
        weights = (jnp.einsum('bsd,do->bso', x, wr) + br)[..., 0]
        k = max(1, int(CAPACITY * s))
        kk = k - 1 if k > 1 else 1
        _, idx = jax.lax.top_k(weights, k)
        sel_idx = idx[:, :kk]
        sel = jnp.take_along_axis(x, sel_idx[:, :, None], axis=1)
        h = jax.nn.gelu(jnp.einsum('bkd,dh->bkh', sel, w1) + b1)
        y = jnp.einsum('bkh,hd->bkd', h, w2) + b2
        w_sel = jnp.take_along_axis(weights, sel_idx, axis=1)
        y = y * w_sel[..., None]
        batch_idx = jnp.arange(b)[:, None]
        processed = jnp.zeros_like(x).at[batch_idx, sel_idx].set(y)
        return processed + x

    def _L2_attn_ref(x, Wq, bq, Wk, bk, Wv, bv, Wo, bo):
        import jax, jax.numpy as jnp
        import numpy as np
        DIM = 64
        HEADS = 4
        HEAD_DIM = DIM // HEADS
        SCALE = HEAD_DIM ** (-0.5)
        B, N, C = x.shape
        x = jnp.clip(x, -10000.0, 10000.0)

        def heads(t):
            return t.reshape(B, N, HEADS, HEAD_DIM).transpose(0, 2, 1, 3)
        q = heads((x @ Wq.T + bq).astype(jnp.float32))
        k = heads((x @ Wk.T + bk).astype(jnp.float32))
        v = heads((x @ Wv.T + bv).astype(jnp.float32))
        attn = jnp.einsum('bhnd,bhmd->bhnm', q, k) * SCALE
        attn = jax.nn.softmax(attn, axis=-1)
        out = jnp.einsum('bhnm,bhmd->bhnd', attn, v)
        out = out.transpose(0, 2, 1, 3).reshape(B, N, C)
        out = out.astype(jnp.bfloat16).astype(jnp.float32)
        return out @ Wo.T + bo

    def _L2_ffn_ref(x, ln1_w, ln2_w, wq, wk, wv, wo, router_w, w1, w2, w3):
        import jax, jax.numpy as jnp
        import numpy as np
        B, T, C = (64, 96, 64)
        NH, NKV = (4, 2)
        HD = C // NH
        NREP = NH // NKV
        NE, TOPK = (8, 2)
        HID = int(8 / 3 * C)
        EPS_RMS = 1e-06

        def _rope_tables(t_len):
            inv_freq = 1.0 / 10000.0 ** (np.arange(0, HD, 2, dtype=np.float32) / HD)
            t = np.arange(t_len, dtype=np.float32)
            freqs = np.outer(t, inv_freq)
            emb = np.concatenate([freqs, freqs], axis=-1)
            return (jnp.asarray(np.cos(emb)), jnp.asarray(np.sin(emb)))

        def _rotate_half(x):
            h = x.shape[-1] // 2
            return jnp.concatenate([-x[..., h:], x[..., :h]], axis=-1)

        def _rmsnorm(v, w):
            return v * jax.lax.rsqrt(jnp.mean(v * v, axis=-1, keepdims=True) + EPS_RMS) * w
        Bx, Tx, Cx = x.shape
        h = _rmsnorm(x, ln1_w)
        q = (h @ wq.T).reshape(Bx, Tx, NH, HD).transpose(0, 2, 1, 3)
        k = (h @ wk.T).reshape(Bx, Tx, NKV, HD).transpose(0, 2, 1, 3)
        v = (h @ wv.T).reshape(Bx, Tx, NKV, HD).transpose(0, 2, 1, 3)
        cos, sin = _rope_tables(Tx)
        cos, sin = (cos[None, None], sin[None, None])
        q = q * cos + _rotate_half(q) * sin
        k = k * cos + _rotate_half(k) * sin
        k = jnp.repeat(k, NREP, axis=1)
        v = jnp.repeat(v, NREP, axis=1)
        scores = jnp.einsum('bhtd,bhsd->bhts', q, k) / jnp.sqrt(jnp.float32(HD))
        causal = jnp.tril(jnp.ones((Tx, Tx), dtype=bool))
        scores = jnp.where(causal[None, None], scores, jnp.float32(-1e+30))
        att = jax.nn.softmax(scores, axis=-1)
        y = jnp.einsum('bhts,bhsd->bhtd', att, v).transpose(0, 2, 1, 3).reshape(Bx, Tx, Cx)
        x = x + y @ wo.T
        flat = _rmsnorm(x, ln2_w).reshape(-1, Cx)
        probs = jax.nn.softmax(flat @ router_w.T, axis=-1)
        tp, ti = jax.lax.top_k(probs, TOPK)
        tp = tp / (jnp.sum(tp, axis=-1, keepdims=True) + 1e-09)
        weights = jnp.sum(tp[..., None] * jax.nn.one_hot(ti, NE, dtype=flat.dtype), axis=1)
        out = jnp.zeros_like(flat)
        for e in range(NE):
            hh = jax.nn.silu(flat @ w1[e].T) * (flat @ w3[e].T)
            out = out + weights[:, e:e + 1] * (hh @ w2[e].T)
        return x + out.reshape(Bx, Tx, Cx)

    def _L3_attn_ref(x, wq, wkv, wo, q_norm_w, k_norm_w):
        import jax, jax.numpy as jnp
        import numpy as np
        import math
        B, T, D_MODEL = (1, 512, 64)
        N_Q, N_KV = (16, 1)
        D_HEAD = D_MODEL // N_KV
        QPG = N_Q // N_KV
        ROPE_BASE = 10000.0
        WINDOW = 128
        EPS = 1.1920929e-07
        NEG = -1e+30

        def _rope(x, base=ROPE_BASE):
            t, d = (x.shape[-2], x.shape[-1])
            freqs = base ** (-2.0 * jnp.arange(d // 2, dtype=jnp.float32) / d)
            theta = jnp.arange(t, dtype=jnp.float32)[:, None] * freqs[None, :]
            cos, sin = (jnp.cos(theta), jnp.sin(theta))
            x1, x2 = (x[..., 0::2], x[..., 1::2])
            r1 = x1 * cos - x2 * sin
            r2 = x1 * sin + x2 * cos
            return jnp.stack([r1, r2], axis=-1).reshape(x.shape)

        def _rmsnorm(x, w):
            return x * jax.lax.rsqrt(jnp.mean(x * x, axis=-1, keepdims=True) + EPS) * w
        Bx, Tx, C = x.shape
        q = x @ wq.T
        kv = x @ wkv.T
        k, v = (kv[..., :N_KV * D_HEAD], kv[..., N_KV * D_HEAD:])
        q = q.reshape(Bx, Tx, QPG, N_KV, D_HEAD).transpose(0, 2, 3, 1, 4)
        k = k.reshape(Bx, Tx, 1, N_KV, D_HEAD).transpose(0, 2, 3, 1, 4)
        v = v.reshape(Bx, Tx, 1, N_KV, D_HEAD).transpose(0, 2, 3, 1, 4)
        q = _rmsnorm(_rope(q), q_norm_w)
        k = _rmsnorm(_rope(k), k_norm_w)
        rows = jnp.arange(Tx)[:, None]
        cols = jnp.arange(Tx)[None, :]
        mask = (cols <= rows) & (rows - cols <= WINDOW)
        scale = 1.0 / math.sqrt(D_HEAD)
        scores = jnp.einsum('bqgtd,bqgsd->bqgts', q, k) * scale
        scores = jnp.where(mask[None, None, None], scores, NEG)
        attn = jax.nn.softmax(scores, axis=-1)
        out = jnp.einsum('bqgts,bqgsd->bqgtd', attn, v)
        out = out.transpose(0, 3, 1, 2, 4).reshape(Bx, Tx, QPG * N_KV * D_HEAD)
        return out @ wo.T

    def _L3_ffn_ref(h, gate_w, gate_b, w1, b1, w2, b2):
        import math
        import jax, jax.numpy as jnp
        import numpy as np
        CAPACITY_FACTOR = 1.25
        B, L, D = h.shape
        E = gate_w.shape[1]
        T = B * L
        C = max(1, math.ceil(CAPACITY_FACTOR * T / E))
        x = h.reshape(T, D)
        logits = x @ gate_w + gate_b
        probs = jax.nn.softmax(logits, axis=-1)
        idx = jnp.argmax(probs, axis=-1)
        prb = jnp.take_along_axis(probs, idx[:, None], axis=1)[:, 0]
        one_hot = jax.nn.one_hot(idx, E, dtype=jnp.float32)
        pos = (jnp.cumsum(one_hot, axis=0) * one_hot).sum(-1).astype(jnp.int32) - 1
        kept = pos < C
        pos_safe = jnp.where(kept, pos, C)
        buf = jnp.zeros((E, C, D), dtype=h.dtype).at[idx, pos_safe].set(x, mode='drop')
        hmid = jax.nn.relu(jnp.einsum('ecd,edf->ecf', buf, w1) + b1[:, None, :])
        ybuf = jnp.einsum('ecf,efd->ecd', hmid, w2) + b2[:, None, :]
        pos_g = jnp.minimum(pos, C - 1)
        y_tok = ybuf[idx, pos_g] * (prb * kept)[:, None]
        y = y_tok.reshape(B, L, D)
        y = jnp.nan_to_num(y, nan=0.0, posinf=10000.0, neginf=-10000.0)
        return y
    h = _L0_tok_ref(x, L0_tok_ln0_g, L0_tok_ln0_b, L0_tok_ln1_g, L0_tok_ln1_b, L0_tok_conv1_w, L0_tok_conv1_b, L0_tok_conv2_w, L0_tok_conv2_b, L0_tok_conv3_w, L0_tok_conv3_b, L0_tok_out_w, L0_tok_out_b)
    h = jnp.concatenate([jnp.broadcast_to(cls_tok, (h.shape[0], 1, h.shape[2])), h], axis=1)
    h = h + _L0_attn_ref(_layernorm(h, axis=-1), L0_attn_W_embed, L0_attn_b_embed, L0_attn_W_out, L0_attn_b_out)
    h = h + _L0_ffn_ref(_layernorm(h, axis=-1), L0_ffn_Wg, L0_ffn_bg, L0_ffn_W1, L0_ffn_b1, L0_ffn_W2, L0_ffn_b2)
    h = h + _L1_attn_ref(_layernorm(h, axis=-1), L1_attn_Wq, L1_attn_Wk, L1_attn_Wv, L1_attn_Wo, L1_attn_bo, L1_attn_g1, L1_attn_b1, L1_attn_W1, L1_attn_bf1, L1_attn_W2, L1_attn_bf2, L1_attn_g2, L1_attn_b2)
    h = h + _L1_ffn_ref(_layernorm(h, axis=-1), L1_ffn_attention_mask, L1_ffn_wr, L1_ffn_br, L1_ffn_w1, L1_ffn_b1, L1_ffn_w2, L1_ffn_b2)
    h = h + _L2_attn_ref(_layernorm(h, axis=-1), L2_attn_Wq, L2_attn_bq, L2_attn_Wk, L2_attn_bk, L2_attn_Wv, L2_attn_bv, L2_attn_Wo, L2_attn_bo)
    h = h + _L2_ffn_ref(_layernorm(h, axis=-1), L2_ffn_ln1_w, L2_ffn_ln2_w, L2_ffn_wq, L2_ffn_wk, L2_ffn_wv, L2_ffn_wo, L2_ffn_router_w, L2_ffn_w1, L2_ffn_w2, L2_ffn_w3)
    h = h + _L3_attn_ref(_layernorm(h, axis=-1), L3_attn_wq, L3_attn_wkv, L3_attn_wo, L3_attn_q_norm_w, L3_attn_k_norm_w)
    h = h + _L3_ffn_ref(_layernorm(h, axis=-1), L3_ffn_gate_w, L3_ffn_gate_b, L3_ffn_w1, L3_ffn_b1, L3_ffn_w2, L3_ffn_b2)
    return h

_drawn_inputs = setup_inputs


def setup_inputs(seed=0):
    import zlib

    import numpy as np

    out = dict(_drawn_inputs(seed))
    spreads = {'L0_tok_ln0_g': (1.0, 0.2),
     'L0_tok_ln0_b': (0.0, 0.1),
     'L0_tok_ln1_g': (1.0, 0.2),
     'L0_tok_ln1_b': (0.0, 0.1),
     'L0_tok_conv1_b': (0.0, 0.1),
     'L0_tok_conv2_b': (0.0, 0.1),
     'L0_tok_conv3_b': (0.0, 0.1),
     'L0_tok_out_b': (0.0, 0.1),
     'L0_attn_b_embed': (0.0, 0.527),
     'L0_attn_b_out': (0.0, 0.1),
     'L0_ffn_bg': (0.0, 0.1),
     'L0_ffn_b1': (0.0, 0.638),
     'L0_ffn_b2': (0.0, 0.1),
     'L1_attn_bo': (0.0, 0.1),
     'L1_attn_g1': (1.0, 0.6),
     'L1_attn_b1': (0.0, 0.8),
     'L1_attn_bf1': (0.0, 0.463),
     'L1_attn_bf2': (0.0, 0.1),
     'L1_attn_g2': (1.0, 0.6),
     'L1_attn_b2': (0.0, 0.8),
     'L1_ffn_b1': (0.0, 0.8),
     'L1_ffn_b2': (0.0, 0.8),
     'L2_attn_bq': (0.0, 0.8),
     'L2_attn_bk': (0.0, 2.0),
     'L2_attn_bv': (0.0, 0.361),
     'L2_attn_bo': (0.0, 0.292),
     'L2_ffn_ln1_w': (1.0, 0.6),
     'L2_ffn_ln2_w': (1.0, 0.6),
     'L3_attn_q_norm_w': (1.0, 0.6),
     'L3_attn_k_norm_w': (1.0, 0.6),
     'L3_ffn_gate_b': (0.0, 0.407),
     'L3_ffn_b1': (0.0, 0.8),
     'L3_ffn_b2': (0.0, 2.0)}
    factors = {'L0_attn_W_embed': 7.717,
     'L0_attn_W_out': 3.879,
     'L0_ffn_W1': 2.84,
     'L1_attn_Wq': 8.0,
     'L1_attn_Wk': 8.0,
     'L1_attn_Wv': 8.0,
     'L1_attn_Wo': 8.0,
     'L1_ffn_wr': 8.0,
     'L1_ffn_w1': 8.0,
     'L1_ffn_w2': 8.0,
     'L2_ffn_wq': 8.0,
     'L2_ffn_wk': 8.0,
     'L2_ffn_wv': 8.0,
     'L2_ffn_wo': 8.0,
     'L2_ffn_router_w': 8.0,
     'L2_ffn_w1': 8.0,
     'L2_ffn_w2': 8.0,
     'L2_ffn_w3': 8.0,
     'L3_attn_wq': 8.0,
     'L3_attn_wkv': 4.485,
     'L3_attn_wo': 4.257,
     'L3_ffn_gate_w': 2.863,
     'L3_ffn_w1': 3.243,
     'L3_ffn_w2': 2.669}
    for name, (base, spread) in spreads.items():
        noise = np.random.default_rng([zlib.crc32(name.encode()), seed]).standard_normal(out[name].shape)
        drawn = base * np.exp(spread * noise) if base else spread * noise
        out[name] = jnp.asarray(drawn.astype(out[name].dtype))
    for name, factor in factors.items():
        out[name] = (out[name] * factor).astype(out[name].dtype)
    return out
```

```python
from contextlib import ExitStack, contextmanager

import numpy as np

import concourse.bass as bass
from concourse import mybir

F32 = mybir.dt.float32
BF16 = mybir.dt.bfloat16
ALU = mybir.AluOpType
ACT = mybir.ActivationFunctionType
AX = mybir.AxisListType.X

P = 128
D = 64
HALVES = 2
PAIRS = 32
SEQ = 129
COLS = PAIRS * SEQ
TILE = 344
TILES = COLS // TILE
CHUNK = 96
CHUNKS = COLS // CHUNK
EXPERTS = 8
BANK = 512
CREDIT = 8
BIG = 1.0e30


class Signal:

    def __init__(self, handle):
        self.sem, self.base, self.total = handle, CREDIT, 0

    def at(self, k):
        return k + self.base


class Tower:

    def __init__(self, nc, dram, free_handles):
        self.nc, self.dram = nc, dram
        self.free = [Signal(handle) for handle in free_handles]
        self.phases = 0


class Phase:

    def __init__(self, tower, stack):
        self.tower, self.nc, self.stack = tower, tower.nc, stack
        self.tag = f"p{tower.phases}"
        self.used = []
        tower.phases += 1

    def sb(self, name, shape, dtype=F32):
        return self.stack.enter_context(self.nc.sbuf_tensor(f"{self.tag}_{name}", shape, dtype))

    def ps(self, name, shape=(P, BANK), dtype=F32):
        return self.stack.enter_context(self.nc.psum_tensor(f"{self.tag}_{name}_ps", list(shape), dtype))

    def counts(self, total):
        s = self.tower.free.pop(0)
        s.total = total
        self.used.append(s)
        return s


@contextmanager
def phase(tower):
    with ExitStack() as stack:
        ph = Phase(tower, stack)
        yield ph
    for s in ph.used:
        s.base += s.total
        tower.free.append(s)



def norm_phase(tower, src, dst, eps, center=True, gamma=None, beta=None):
    nc, n2 = tower.nc, TILES // 2
    with phase(tower) as ph:
        centered_ps = [ph.ps(f"centered{u}") for u in range(2)]
        var_ps = [ph.ps(f"var{u}") for u in range(2)]
        square = [ph.sb(f"square{u}", [P, TILE]) for u in range(2)]
        rstd = [ph.sb(f"rstd{u}", [P, TILE]) for u in range(2)]
        centered = [ph.counts(n2) for _ in range(2)]
        squared = [ph.counts(n2) for _ in range(2)]
        var_ready = [ph.counts(n2) for _ in range(2)]
        logged = [ph.counts(n2) for _ in range(2)]
        rstd_ready = [ph.counts(n2) for _ in range(2)]
        scaled = [ph.counts(n2) for _ in range(2)]
        written = [ph.counts(n2) for _ in range(2)]
        affine = gamma is not None
        eps_col = tower.eps[eps]

        def cols(i, u):
            return bass.ds((2 * i + u) * TILE, TILE)

        with nc.Block() as block:
            @block.tensor
            def _(pe):
                with pe.Fori(0, n2) as i:
                    if center:
                        for u in range(2):
                            pe.wait_ge(scaled[u].sem, scaled[u].at(i))
                            pe.matmul(centered_ps[u][:, 0:TILE], tower.center[:], src[:, cols(i, u)],
                                      start=True, stop=True).then_inc(centered[u].sem, 1)
                    for u in range(2):
                        pe.wait_ge(squared[u].sem, squared[u].at(i + 1))
                        pe.wait_ge(logged[u].sem, logged[u].at(i))
                        pe.matmul(var_ps[u][:, 0:TILE], tower.average[:], square[u][:],
                                  start=True, stop=True).then_inc(var_ready[u].sem, 1)

            @block.scalar
            def _(act):
                act.preload_act_table_set("natural_log_exp_and_others")
                with act.Fori(0, n2) as i:
                    for u in range(2):
                        act.wait_ge(var_ready[u].sem, var_ready[u].at(i))
                        if center:
                            act.wait_ge(centered[u].sem, centered[u].at(i + 1))
                            act.activation(square[u][:], centered_ps[u][:, 0:TILE],
                                           ACT.Square).then_inc(squared[u].sem, 1)
                        else:
                            act.activation(square[u][:], src[:, cols(i, u)],
                                           ACT.Square).then_inc(squared[u].sem, 1)
                    for u in range(2):
                        act.wait_ge(var_ready[u].sem, var_ready[u].at(i + 1))
                        act.wait_ge(scaled[u].sem, scaled[u].at(i))
                        act.activation(rstd[u][:], var_ps[u][:, 0:TILE], ACT.Ln,
                                       bias=eps_col).then_inc(logged[u].sem, 1)
                    for u in range(2):
                        act.wait_ge(logged[u].sem, logged[u].at(i + 1))
                        act.activation(rstd[u][:], rstd[u][:], ACT.Exp,
                                       scale=-0.5).then_inc(rstd_ready[u].sem, 1)

            @block.vector
            def _(dve):
                with dve.Fori(0, n2) as i:
                    for u in range(2):
                        dve.wait_ge(rstd_ready[u].sem, rstd_ready[u].at(i + 1))
                        x = centered_ps[u][:, 0:TILE] if center else src[:, cols(i, u)]
                        dve.tensor_tensor(dst[:, cols(i, u)], x, rstd[u][:],
                                          ALU.mult).then_inc(scaled[u].sem, 1)
                    for u in range(2 if affine else 0):
                        dve.wait_ge(scaled[u].sem, scaled[u].at(i + 1))
                        if beta is None:
                            dve.tensor_scalar(dst[:, cols(i, u)], dst[:, cols(i, u)], gamma, None,
                                              ALU.mult).then_inc(written[u].sem, 1)
                        else:
                            dve.tensor_scalar(dst[:, cols(i, u)], dst[:, cols(i, u)], gamma, beta,
                                              ALU.mult, ALU.add).then_inc(written[u].sem, 1)
        if not affine:
            for s in written:
                s.total = 0
        if not center:
            for s in centered:
                s.total = 0



def gate_phase(tower, x, gate_w, gate_b, top, weighted, rows_t):
    nc = tower.nc
    per_bank = BANK // (HALVES * EXPERTS)
    groups = [(c, min(5, CHUNKS - c)) for c in range(0, CHUNKS, 5)]
    with phase(tower) as ph:
        gw = ph.sb("gate_w", [P, HALVES * EXPERTS])
        gb = ph.sb("gate_b", [CHUNK, HALVES * EXPERTS])
        logit_ps = [ph.ps(f"logit{u}") for u in range(2)]
        turn_ps = [ph.ps(f"turn{u}", (64, BANK)) for u in range(4)]
        shape = [CHUNK, CHUNKS, HALVES, EXPERTS]
        logit = ph.sb("logit", shape)
        eq = ph.sb("eq", shape)
        mark = ph.sb("mark", shape)
        second = ph.sb("second", shape)
        e_x = ph.sb("e_x", shape)
        best = ph.sb("best", [CHUNK, CHUNKS * HALVES])
        place = ph.sb("place", [CHUNK, CHUNKS * HALVES])
        total = ph.sb("total", [CHUNK, CHUNKS * HALVES])
        wide = ph.sb("wide", [CHUNK, CHUNKS, HALVES, 32])
        loaded = ph.counts(32)
        logits = ph.counts(1)
        v = ph.counts(0)
        exped = ph.counts(1)
        cleared = ph.counts(1)
        marked = ph.counts(1)
        turned = ph.counts(len(groups))
        copied = ph.counts(len(groups))

        def flat(t):
            return t[:].rearrange("p c g e -> p (c g) e")

        def wide_to(t):
            return t[:, :, None].to_broadcast([CHUNK, CHUNKS * HALVES, EXPERTS])

        rank = tower.rank8[0:CHUNK, :]
        rank_all = rank[:, None, :].to_broadcast([CHUNK, CHUNKS * HALVES, EXPERTS])
        with nc.Block() as block:
            @block.sync
            def _(sp):
                sp.dma_start(gw[:], tower.dram[gate_w]).then_inc(loaded.sem, 16)
                sp.dma_start(gb[:], tower.dram[gate_b]).then_inc(loaded.sem, 16)

            @block.gpsimd
            def _(pool):
                pool.memset(wide[:], 0.0).then_inc(cleared.sem, 1)

            @block.tensor
            def _(pe):
                pe.wait_ge(loaded.sem, loaded.at(32))
                for c in range(CHUNKS):
                    at = (c % per_bank) * HALVES * EXPERTS
                    mm = pe.matmul(logit_ps[c // per_bank][0:CHUNK, at:at + HALVES * EXPERTS],
                                   x[:, c * CHUNK:(c + 1) * CHUNK], gw[:], start=True, stop=True)
                mm.then_inc(logits.sem, 1)
                pe.wait_ge(marked.sem, marked.at(1))
                for n, (c0, k) in enumerate(groups):
                    pe.wait_ge(copied.sem, copied.at(n - 3))
                    for c in range(c0, c0 + k):
                        at = (c - c0) * CHUNK
                        mm = pe.transpose(turn_ps[n % 4][0:64, at:at + CHUNK],
                                          wide[:, c, :, :].rearrange("p g e -> p (g e)"),
                                          tower.ident[0:CHUNK, 0:CHUNK])
                    mm.then_inc(turned.sem, 1)

            @block.scalar
            def _(act):
                if top == 1 or weighted:
                    act.wait_ge(v.sem, v.at(5))
                    act.activation(e_x[:], e_x[:], ACT.Exp).then_inc(exped.sem, 1)
                for n, (c0, k) in enumerate(groups):
                    act.wait_ge(turned.sem, turned.at(n + 1))
                    act.activation(rows_t[0:64, c0 * CHUNK:(c0 + k) * CHUNK], turn_ps[n % 4][0:64, 0:k * CHUNK],
                                   ACT.Copy).then_inc(copied.sem, 1)

            @block.vector
            def _(dve):
                done = [0]

                def step(ins):
                    done[0] += 1
                    ins.then_inc(v.sem, 1)
                    dve.wait_ge(v.sem, v.at(done[0]))

                if rows_t.shape[0] > 64:
                    dve.memset(rows_t[64:P, :], 0.0)
                dve.wait_ge(logits.sem, logits.at(1))
                for k in range(2):
                    n = min(per_bank, CHUNKS - k * per_bank)
                    step(dve.tensor_tensor(
                        logit[:, k * per_bank:k * per_bank + n, :, :].rearrange("p c g e -> p c (g e)"),
                        logit_ps[k][0:CHUNK, 0:n * 16].rearrange("p (c e) -> p c e", e=16),
                        gb[:, None, :].to_broadcast([CHUNK, n, 16]), ALU.add))

                def mark_first(out, values):
                    step(dve.tensor_reduce(best[:], flat(values), AX, ALU.max))
                    step(dve.tensor_tensor(flat(eq), flat(values), wide_to(best), ALU.is_equal))
                    if values is logit:
                        step(dve.tensor_tensor(flat(e_x), flat(values), wide_to(best), ALU.subtract))
                    step(dve.tensor_tensor(flat(eq), flat(eq), rank_all, ALU.mult))
                    step(dve.tensor_reduce(place[:], flat(eq), AX, ALU.max))
                    step(dve.tensor_tensor(flat(out), rank_all, wide_to(place), ALU.is_equal))

                mark_first(mark, logit)
                if top == 2:
                    step(dve.scalar_tensor_tensor(second[:], mark[:], -BIG, logit[:], ALU.mult, ALU.add))
                    mark_first(logit, second)
                    step(dve.tensor_tensor(mark[:], mark[:], logit[:], ALU.add))
                dve.wait_ge(cleared.sem, cleared.at(1))
                if weighted:
                    dve.wait_ge(exped.sem, exped.at(1))
                    for eps in (0.0, 1e-9):
                        step(dve.tensor_reduce(total[:], flat(e_x), AX, ALU.add))
                        step(dve.tensor_scalar(total[:], total[:], eps, None, ALU.add))
                        step(dve.reciprocal(total[:], total[:]))
                        if eps:
                            last = dve.tensor_tensor(wide[:, :, :, 0:8].rearrange("p c g e -> p (c g) e"),
                                                     flat(e_x), wide_to(total), ALU.mult)
                        else:
                            step(dve.tensor_tensor(flat(e_x), flat(e_x), wide_to(total), ALU.mult))
                            step(dve.tensor_tensor(e_x[:], e_x[:], mark[:], ALU.mult))
                    last.then_inc(marked.sem, 1)
                else:
                    if top == 1:
                        dve.wait_ge(exped.sem, exped.at(1))
                        step(dve.tensor_reduce(total[:], flat(e_x), AX, ALU.add))
                        step(dve.reciprocal(total[:], total[:]))
                        step(dve.tensor_tensor(wide[:, :, :, 8:16].rearrange("p c g e -> p (c g) e"),
                                               flat(mark), wide_to(total), ALU.mult))
                    dve.tensor_copy(wide[:, :, :, 0:8].rearrange("p c g e -> p (c g) e"),
                                    flat(mark)).then_inc(marked.sem, 1)
                v.total = done[0]
        if not (top == 1 or weighted):
            exped.total = 0


def spread_phase(tower, x, rows_t, aug):
    nc = tower.nc
    with phase(tower) as ph:
        cleared = ph.counts(1)
        with nc.Block() as block:
            @block.gpsimd
            def _(pool):
                pool.memset(aug[0][64:96, :], 0.0)
                pool.memset(aug[1][64:96, :], 0.0).then_inc(cleared.sem, 1)

            @block.scalar
            def _(act):
                for g in range(HALVES):
                    act.activation(aug[g][0:64, :], x[64 * g:64 * g + 64, :], ACT.Copy)

            @block.vector
            def _(dve):
                for g in range(HALVES):
                    dve.tensor_copy(aug[g][96:104, :], rows_t[32 * g:32 * g + 8, :])
                dve.wait_ge(cleared.sem, cleared.at(1))
                for g in range(HALVES):
                    dve.tensor_scalar(aug[g][64:72, :], rows_t[32 * g:32 * g + 8, :], -1.0, None, ALU.add)



def mlp_phase(tower, up, down, bias, blocks, func, rows, x_of, finish, load, extra=None,
              up_of=lambda b: b):
    nc, n2, ring = tower.nc, TILES // 2, 4
    lag = 2
    with phase(tower) as ph:
        n_up = tower.dram[up].shape[1]
        w_up = ph.sb("w_up", [rows, n_up, P])
        w_down = ph.sb("w_down", [P, blocks, P])
        b_up = ph.sb("b_up", [P, n_up])
        w_extra = ph.sb("w_extra", [extra[1], HALVES, P]) if extra else None
        hid_ps = [ph.ps(f"hid{r}") for r in range(ring)]
        y_ps = [ph.ps(f"y{u}") for u in range(2)]
        aux_ps = [ph.ps(f"aux{u}") for u in range(2)]
        hid = [ph.sb(f"hidden{r}", [P, TILE]) for r in range(ring)]
        n_load = 4 if extra else 3
        loaded = ph.counts(16 * n_load)
        up_done = ph.counts(2 * blocks * n2)
        act_done = ph.counts(2 * blocks * n2)
        down_done = ph.counts(2 * blocks * n2)
        y_done = [ph.counts(n2) for _ in range(2)]
        y_read = [ph.counts(n2) for _ in range(2)]
        per = 2 * blocks
        state = load(ph) if load else None
        aux_sb = [ph.sb(f"aux_sb{u}", [P, TILE]) for u in range(2)] if finish.broadcast else None
        aux_ready = [ph.counts(n2 if finish.broadcast else 0) for _ in range(2)]

        def cols(i, u):
            return bass.ds((2 * i + u) * TILE, TILE)

        with nc.Block() as block:
            @block.sync
            def _(sp):
                sp.dma_start(w_up[:], tower.dram[up]).then_inc(loaded.sem, 16)
                sp.dma_start(b_up[:], tower.dram[bias]).then_inc(loaded.sem, 16)
                sp.dma_start(w_down[:], tower.dram[down]).then_inc(loaded.sem, 16)
                if extra:
                    sp.dma_start(w_extra[:], tower.dram[extra[0]]).then_inc(loaded.sem, 16)

            @block.tensor
            def _(pe):
                pe.wait_ge(loaded.sem, loaded.at(16 * n_load))
                with pe.Fori(0, n2) as i:
                    for n in range(per + lag):
                        if n < per:
                            b, u = n % blocks, n // blocks
                            pe.wait_ge(act_done.sem, act_done.at(i * per + n - ring + 1))
                            pe.matmul(hid_ps[n % ring][:, 0:TILE], w_up[:, up_of(b), :],
                                      x_of(b)[0:rows, cols(i, u)],
                                      start=True, stop=True).then_inc(up_done.sem, 1)
                        if n >= lag:
                            m = n - lag
                            b, u = m % blocks, m // blocks
                            if b == 0:
                                pe.wait_ge(y_read[u].sem, y_read[u].at(i))
                            pe.wait_ge(act_done.sem, act_done.at(i * per + m + 1))
                            last = b == blocks - 1 and not extra
                            mm = pe.matmul(y_ps[u][:, 0:TILE], w_down[:, b, :], hid[m % ring][:],
                                           start=b == 0, stop=last)
                            mm.then_inc(down_done.sem, 1)
                            if b == blocks - 1:
                                if extra:
                                    for g in range(HALVES):
                                        mm = pe.matmul(y_ps[u][:, 0:TILE], w_extra[:, g, :],
                                                       extra[2][g][0:extra[1], cols(i, u)],
                                                       start=False, stop=g == 1)
                                if finish.broadcast:
                                    mm = finish.broadcast(pe, aux_ps[u], state, cols(i, u), u)
                                if extra or finish.broadcast:
                                    mm.then_inc(y_done[u].sem, 1)

            @block.scalar
            def _(act):
                act.wait_ge(loaded.sem, loaded.at(16 * n_load))
                with act.Fori(0, n2) as i:
                    for n in range(per):
                        act.wait_ge(up_done.sem, up_done.at(i * per + n + 1))
                        act.wait_ge(down_done.sem, down_done.at(i * per + n - ring + 1))
                        b = up_of(n % blocks)
                        act.activation(hid[n % ring][:], hid_ps[n % ring][:, 0:TILE], func,
                                       bias=b_up[:, b:b + 1]).then_inc(act_done.sem, 1)
                        if finish.broadcast and n % blocks == blocks - 1:
                            u = n // blocks
                            act.wait_ge(y_done[u].sem, y_done[u].at(i + 1))
                            act.wait_ge(y_read[u].sem, y_read[u].at(i))
                            act.activation(aux_sb[u][:], aux_ps[u][:, 0:TILE],
                                           ACT.Copy).then_inc(aux_ready[u].sem, 1)

            @block.vector
            def _(dve):
                with dve.Fori(0, n2) as i:
                    for u in range(2):
                        if extra or finish.broadcast:
                            dve.wait_ge(y_done[u].sem, y_done[u].at(i + 1))
                        else:
                            dve.wait_ge(down_done.sem, down_done.at(i * per + (u + 1) * blocks))
                        if finish.broadcast:
                            dve.wait_ge(aux_ready[u].sem, aux_ready[u].at(i + 1))
                        finish.vector(dve, y_ps[u][:, 0:TILE], aux_sb and aux_sb[u], state, cols(i, u), i, u).then_inc(
                            y_read[u].sem, 1)
        if not (extra or finish.broadcast):
            for s in y_done:
                s.total = 0


class AddTo:
    broadcast = None

    def __init__(self, acc, bias=None):
        self.acc, self.bias = acc, bias

    def vector(self, dve, y, aux, state, cols, i, u):
        if self.bias is None:
            return dve.tensor_tensor(self.acc[:, cols], y, self.acc[:, cols], ALU.add)
        return dve.scalar_tensor_tensor(self.acc[:, cols], y, self.bias, self.acc[:, cols], ALU.add, ALU.add)



class Attend:

    def __init__(self, name, heads, scale, causal=False, rope=False, norm=False, bias=False, bf16_out=False):
        self.name, self.heads, self.scale = name, heads, scale
        self.causal, self.rope, self.norm, self.bias, self.bf16_out = causal, rope, norm, bias, bf16_out


ATTENTION = {
    "L2a": Attend("L2a", heads=4, scale=16 ** -0.5, bias=True, bf16_out=True),
    "L2f": Attend("L2f", heads=4, scale=16 ** -0.5, causal=True, rope=True),
    "L3a": Attend("L3a", heads=16, scale=64 ** -0.5, causal=True, rope=True, norm=True),
}


def attention_phase(tower, src, acc, a, out_bias=None):
    nc = tower.nc
    rows = a.heads * SEQ
    n_q = a.heads // 2
    wide = 2 * SEQ
    full, rest = divmod(rows, P)
    tiles = full + 1
    banks = -(-tiles // 3)
    groups = n_q + 1
    both = HALVES * n_q
    with phase(tower) as ph:
        def w(name, shape, dtype=F32):
            loads.append((ph.sb(name, shape, dtype), f"{a.name}_{name}"))
            return loads[-1][0]

        loads = []
        wq, wk = w("wq", [P, a.heads, P]), w("wk", [P, P])
        wv, wo = w("wv", [P, P]), w("wo", [P, a.heads, P])
        if a.rope:
            wq_turned, wk_turned = w("wq_turned", [P, a.heads, P]), w("wk_turned", [P, P])
            cos, sin = w("cos", [P, SEQ]), w("sin", [P, SEQ])
        if a.norm:
            norm_w = w("norm_w", [P, 2])
        if a.bias:
            bias = w("bias", [P, a.heads + 2])
        if a.causal:
            later, place = tower.later, tower.place
        ones2 = tower.ones2

        xs = ph.sb("xs", [P, SEQ])
        k_t = ph.sb("k_t", [P, SEQ])
        q_t = ph.sb("q_t", [P, rows])
        turn_a = [ph.sb(f"turn_a{r}", [P, 2, SEQ]) for r in range(2)]
        turn_b = [ph.sb(f"turn_b{r}", [P, 2, SEQ]) for r in range(2)]
        square = [ph.sb(f"square{r}", [P, wide]) for r in range(2)]
        rstd = [ph.sb(f"rstd{r}", [P, wide]) for r in range(2)]
        val = [ph.sb(f"val{g}", [P, P]) for g in range(HALVES)]
        val_last = [ph.sb(f"val_last{g}", [1, P]) for g in range(HALVES)]
        peak = ph.sb("peak", [P, HALVES, tiles])
        peak_t = [ph.sb(f"peak_t{g}", [tiles, 2, P], BF16) for g in range(HALVES)]
        peak_row = [ph.sb(f"peak_row{g}", [2, tiles * P], BF16) for g in range(HALVES)]
        prob = [ph.sb(f"prob{r}", [P, wide]) for r in range(3)]
        n_last = 2 if a.causal else wide
        prob_last = [ph.sb(f"prob_last{r}", [1, n_last]) for r in range(3)]
        inv = [ph.sb(f"inv{r}", [P, wide]) for r in range(2)]
        mixed = ph.sb("mixed", [P, rows])
        narrow = ph.sb("narrow", [P, wide], BF16) if a.bf16_out else None
        raw = ph.sb("raw", [P, wide]) if a.bf16_out else None

        b = [ph.ps(f"bank{n}") for n in range(8)]
        proj_ps, turned_ps, avg_ps, score_ps, out_ps, st_ps = b[0:2], b[2:4], b[4:6], b[0:2], b[2:4], b[6:8]
        misc_ps = b[4]
        last_ps = [b[5][:, 0:n_last], b[0][:, 0:n_last]]

        loaded = ph.counts(16 * len(loads))
        filled = ph.counts(3)
        copied = ph.counts(PAIRS)
        projected = ph.counts(PAIRS * groups)
        squared = ph.counts(PAIRS * groups * a.norm)
        averaged = ph.counts(PAIRS * groups * a.norm)
        logged = ph.counts(PAIRS * groups * a.norm)
        rstd_ready = ph.counts(PAIRS * groups * a.norm)
        turns = 3 if a.norm else 2
        turned = ph.counts(PAIRS * groups * turns * a.rope)
        written = ph.counts(PAIRS * groups)
        values_made = ph.counts(PAIRS)
        values_ready = ph.counts(PAIRS)
        scored = ph.counts(PAIRS * HALVES * banks)
        peaked = ph.counts(PAIRS * HALVES * banks)
        peak_turned = ph.counts(PAIRS * HALVES)
        peak_high = ph.counts(PAIRS * HALVES)
        peak_split = ph.counts(PAIRS * HALVES)
        rows_landed = [ph.counts(PAIRS * 32) for _ in range(HALVES)]
        st_ready = ph.counts(PAIRS * both)
        exped = ph.counts(PAIRS * both)
        out_ready = ph.counts(PAIRS * both)
        sum_logged = ph.counts(PAIRS * both)
        inv_ready = ph.counts(PAIRS * both)
        rounding = ph.counts(PAIRS * both * 2 * a.bf16_out)
        out_read = ph.counts(PAIRS * both)
        y_ready = ph.counts(PAIRS)
        y_read = ph.counts(PAIRS)

        def half(g):
            return slice(D * g, D * g + D)

        def other(g):
            return half(1 - g)

        def q_cols(n):
            return slice((n - 1) * wide, n * wide)

        def last_cols(buf, gr):
            cut = buf[:, gr * wide:(gr + 1) * wide]
            return cut.rearrange("p (h t) -> p h t", h=2)[:, :, SEQ - 1] if a.causal else cut

        with nc.Block() as block:
            @block.sync
            def _(sp):
                for buf, name in loads:
                    sp.dma_start(buf[:], tower.dram[name]).then_inc(loaded.sem, 16)
                with sp.Fori(0, PAIRS) as j:
                    for g in range(HALVES):
                        sp.wait_ge(peak_split.sem, peak_split.at(j * HALVES + g + 1))
                        for part in range(2):
                            sp.dma_start(peak_row[g][part:part + 1, :].rearrange("a (i r) -> a i r", r=P),
                                         peak_t[g][:, part, :]).then_inc(rows_landed[g].sem, 16)

            @block.gpsimd
            def _(pool):
                for g in range(HALVES):
                    pool.memset(val[g][:], 1.0)
                    pool.memset(val_last[g][:], 1.0).then_inc(filled.sem, 1)
                pool.memset(peak[:], 0.0).then_inc(filled.sem, 1)
                with pool.Fori(0, PAIRS) as j:
                    pool.wait_ge(values_made.sem, values_made.at(j))
                    pool.tensor_copy(xs[:], src[:, bass.ds(j * SEQ, SEQ)]).then_inc(copied.sem, 1)

            @block.tensor
            def _(pe):
                pe.wait_ge(loaded.sem, loaded.at(16 * len(loads)))

                def project(j, n):
                    if n >= 2:
                        pe.wait_ge(written.sem, written.at(j * groups + n - 1))
                    if n == 0:
                        mm = pe.matmul(proj_ps[0][:, 0:SEQ], wk[:], xs[:], start=True, stop=True)
                        if a.rope:
                            mm = pe.matmul(turned_ps[0][:, 0:SEQ], wk_turned[:], xs[:], start=True, stop=True)
                    else:
                        for t in range(2):
                            head, at = 2 * (n - 1) + t, slice(t * SEQ, (t + 1) * SEQ)
                            mm = pe.matmul(proj_ps[n % 2][:, at], wq[:, head, :], xs[:], start=True, stop=True)
                            if a.rope:
                                mm = pe.matmul(turned_ps[n % 2][:, at], wq_turned[:, head, :], xs[:],
                                               start=True, stop=True)
                    mm.then_inc(projected.sem, 1)

                def average(j, n):
                    pe.wait_ge(squared.sem, squared.at(j * groups + n + 1))
                    size = wide if n else SEQ
                    pe.matmul(avg_ps[n % 2][:, 0:size], tower.average[:], square[n % 2][:, 0:size],
                              start=True, stop=True).then_inc(averaged.sem, 1)

                def score(j, g, m):
                    pe.wait_ge(peaked.sem, peaked.at((j * HALVES + g) * banks + m - 1))
                    for i in range(3 * m, min(3 * m + 3, tiles)):
                        size = P if i < full else rest
                        to = score_ps[m % 2][0:size, (i % 3) * SEQ:(i % 3 + 1) * SEQ]
                        mm = pe.matmul(to, q_t[half(g), i * P:i * P + size], k_t[half(g), :],
                                       start=True, stop=not a.causal)
                        if a.causal:
                            at = i * P % SEQ
                            mm = pe.matmul(to, place[:, at:at + size], later[:], start=False, stop=True)
                    mm.then_inc(scored.sem, 1)

                def turn_peak(j, g):
                    pe.wait_ge(peaked.sem, peaked.at((j * HALVES + g + 1) * banks))
                    pe.wait_ge(values_ready.sem, values_ready.at(j + 1))
                    pe.wait_ge(peak_split.sem, peak_split.at(j * HALVES + g))
                    pe.transpose(misc_ps[0:tiles, 0:P], peak[:, g, :], tower.ident[:]).then_inc(
                        peak_turned.sem, 1)

                def scores_t(j, n):
                    g, gr = n // n_q, n % n_q
                    if gr == 0:
                        pe.wait_ge(rows_landed[g].sem, rows_landed[g].at(j * 32 + 32))
                    pe.wait_ge(exped.sem, exped.at(j * both + n - 1))
                    at = slice(gr * wide, (gr + 1) * wide)
                    to = st_ps[n % 2][:, 0:wide]
                    pe.matmul(to, k_t[half(g), 0:P], q_t[half(g), at], start=True, stop=False)
                    pe.matmul(to, ones2[:], peak_row[g][:, at], start=False, stop=not a.causal)
                    if a.causal:
                        pe.matmul(to, later[:, 0:P], place[:, None, 0:SEQ].to_broadcast([P, 2, SEQ]),
                                  start=False, stop=True)
                    to = last_ps[n % 2][0:1, :]
                    pe.matmul(to, k_t[half(g), P:SEQ], last_cols(q_t[half(g), :], gr), start=True, stop=False)
                    pe.matmul(to, ones2[:, 0:1], last_cols(peak_row[g][:, 0:rows], gr),
                              start=False, stop=True).then_inc(st_ready.sem, 1)

                def mix(j, n):
                    g = n // n_q
                    pe.wait_ge(exped.sem, exped.at(j * both + n + 1))
                    pe.wait_ge(out_read.sem, out_read.at(j * both + n - 1))
                    to = out_ps[n % 2]
                    pe.matmul(to[:, 0:wide], val[g][:], prob[n % 3][:], start=True, stop=a.causal)
                    pe.matmul(last_cols(to[:, 0:wide], 0), val_last[g][:], prob_last[n % 3][:],
                              start=False, stop=True, skip_group_check=a.causal).then_inc(out_ready.sem, 1)

                with pe.Fori(0, PAIRS) as j:
                    pe.wait_ge(copied.sem, copied.at(j + 1))
                    pe.wait_ge(y_read.sem, y_read.at(j))
                    for n in range(groups + 1):
                        if n < groups:
                            project(j, n)
                        if a.norm and n:
                            average(j, n - 1)
                    pe.wait_ge(written.sem, written.at(j * groups + groups))
                    pe.matmul(misc_ps[:, 0:P], xs[:, 0:P], wv[:], start=True, stop=True)
                    pe.matmul(misc_ps[0:1, P:2 * P], xs[:, P:SEQ], wv[:],
                              start=True, stop=True).then_inc(values_made.sem, 1)
                    for m in range(banks):
                        score(j, 0, m)
                    for m in range(banks):
                        if m == 1:
                            turn_peak(j, 0)
                        score(j, 1, m)
                    for n in range(both + 1):
                        if n == 1:
                            turn_peak(j, 1)
                        if n < both:
                            scores_t(j, n)
                        if n:
                            mix(j, n - 1)
                    pe.wait_ge(out_read.sem, out_read.at(j * both + both))
                    for head in range(a.heads):
                        mm = pe.matmul(misc_ps[:, 0:SEQ], wo[:, head, :], mixed[:, head * SEQ:(head + 1) * SEQ],
                                       start=head == 0, stop=head == a.heads - 1)
                    mm.then_inc(y_ready.sem, 1)

            @block.scalar
            def _(act):
                act.preload_act_table_set("natural_log_exp_and_others")
                eps = tower.eps[1.1920929e-07]
                act.wait_ge(filled.sem, filled.at(3))

                def inverse_norm(j, n):
                    size = wide if n else SEQ
                    act.wait_ge(averaged.sem, averaged.at(j * groups + n + 1))
                    act.activation(rstd[n % 2][:, 0:size], avg_ps[n % 2][:, 0:size], ACT.Ln,
                                   bias=eps).then_inc(logged.sem, 1)
                    act.wait_ge(logged.sem, logged.at(j * groups + n + 1))
                    act.activation(rstd[n % 2][:, 0:size], rstd[n % 2][:, 0:size], ACT.Exp,
                                   scale=-0.5).then_inc(rstd_ready.sem, 1)

                def inverse_sum(j, n):
                    g = n // n_q
                    act.wait_ge(out_ready.sem, out_ready.at(j * both + n + 1))
                    act.wait_ge(out_read.sem, out_read.at(j * both + n - 1))
                    act.activation(inv[n % 2][half(g), :], out_ps[n % 2][other(g), 0:wide],
                                   ACT.Ln).then_inc(sum_logged.sem, 1)
                    act.wait_ge(sum_logged.sem, sum_logged.at(j * both + n + 1))
                    act.activation(inv[n % 2][half(g), :], inv[n % 2][half(g), :], ACT.Exp,
                                   scale=-1.0).then_inc(inv_ready.sem, 1)

                with act.Fori(0, PAIRS) as j:
                    for n in range(groups + 1 if a.norm else 0):
                        if n < groups:
                            size = wide if n else SEQ
                            act.wait_ge(projected.sem, projected.at(j * groups + n + 1))
                            act.activation(square[n % 2][:, 0:size], proj_ps[n % 2][:, 0:size],
                                           ACT.Square).then_inc(squared.sem, 1)
                        if n:
                            inverse_norm(j, n - 1)
                    act.wait_ge(values_made.sem, values_made.at(j + 1))
                    for g in range(HALVES):
                        act.activation(val[g][:, half(g)], misc_ps[:, D * g:D * g + D], ACT.Copy)
                        ins = act.activation(val_last[g][:, half(g)], misc_ps[0:1, P + D * g:P + D * g + D],
                                             ACT.Copy)
                    ins.then_inc(values_ready.sem, 1)
                    for n in range(both + 1):
                        if n < both:
                            act.wait_ge(st_ready.sem, st_ready.at(j * both + n + 1))
                            act.activation(prob[n % 3][:], st_ps[n % 2][:, 0:wide], ACT.Exp, scale=a.scale)
                            act.activation(prob_last[n % 3][:], last_ps[n % 2][0:1, :], ACT.Exp,
                                           scale=a.scale).then_inc(exped.sem, 1)
                        if n:
                            inverse_sum(j, n - 1)

            @block.vector
            def _(dve):
                dve.wait_ge(loaded.sem, loaded.at(16 * len(loads)))
                dve.wait_ge(filled.sem, filled.at(3))

                def write(j, n):
                    heads = 2 if n else 1
                    size = heads * SEQ
                    dst = q_t[:, q_cols(n)] if n else k_t[:, :]
                    step = j * groups + n
                    dve.wait_ge(projected.sem, projected.at(step + 1))
                    if not a.rope:
                        for t in range(heads):
                            at, col = slice(t * SEQ, (t + 1) * SEQ), 2 * n - 1 + t if n else 0
                            ins = dve.tensor_scalar(dst[:, at], proj_ps[n % 2][:, at], bias[:, col:col + 1],
                                                    None, ALU.add)
                        ins.then_inc(written.sem, 1)
                        return
                    if a.norm:
                        dve.wait_ge(squared.sem, squared.at(step + 1))
                    for to, ps, table in ((turn_a, proj_ps, cos), (turn_b, turned_ps, sin)):
                        dve.tensor_tensor(to[n % 2][:, 0:heads, :],
                                          ps[n % 2][:, 0:size].rearrange("p (h t) -> p h t", h=heads),
                                          table[:, None, :].to_broadcast([P, heads, SEQ]),
                                          ALU.mult).then_inc(turned.sem, 1)
                    dve.wait_ge(turned.sem, turned.at(step * turns + 2))
                    ins = dve.tensor_tensor(dst.rearrange("p (h t) -> p h t", h=heads),
                                            turn_a[n % 2][:, 0:heads, :], turn_b[n % 2][:, 0:heads, :], ALU.add)
                    if a.norm:
                        ins.then_inc(turned.sem, 1)
                        dve.wait_ge(turned.sem, turned.at(step * turns + 3))
                        dve.wait_ge(rstd_ready.sem, rstd_ready.at(step + 1))
                        col = 1 if n else 0
                        dve.scalar_tensor_tensor(dst, dst, norm_w[:, col:col + 1], rstd[n % 2][:, 0:size],
                                                 ALU.mult, ALU.mult).then_inc(written.sem, 1)
                    else:
                        ins.then_inc(written.sem, 1)

                def peaks(j, g, m):
                    dve.wait_ge(scored.sem, scored.at((j * HALVES + g) * banks + m + 1))
                    k = min(3, full - 3 * m)
                    bank = score_ps[m % 2]
                    ins = dve.tensor_reduce(peak[:, g, 3 * m:3 * m + k],
                                            bank[:, 0:k * SEQ].rearrange("p (i s) -> p i s", s=SEQ), AX, ALU.max)
                    if m == banks - 1:
                        ins = dve.tensor_reduce(peak[0:rest, g, full:full + 1],
                                                bank[0:rest, k * SEQ:(k + 1) * SEQ], AX, ALU.max)
                    ins.then_inc(peaked.sem, 1)

                def split_peak(j, g):
                    step = j * HALVES + g
                    dve.wait_ge(peak_turned.sem, peak_turned.at(step + 1))
                    dve.wait_ge(rows_landed[g].sem, rows_landed[g].at(j * 32))
                    dve.tensor_scalar(peak_t[g][:, 0, :], misc_ps[0:tiles, 0:P], -1.0, None,
                                      ALU.mult).then_inc(peak_high.sem, 1)
                    dve.wait_ge(peak_high.sem, peak_high.at(step + 1))
                    dve.scalar_tensor_tensor(peak_t[g][:, 1, :], misc_ps[0:tiles, 0:P], -1.0,
                                             peak_t[g][:, 0, :], ALU.mult, ALU.subtract).then_inc(
                        peak_split.sem, 1)

                def normalise(j, n):
                    g, gr = n // n_q, n % n_q
                    step = j * both + n
                    dst = mixed[half(g), gr * wide:(gr + 1) * wide]
                    dve.wait_ge(inv_ready.sem, inv_ready.at(step + 1))
                    sums = out_ps[n % 2][half(g), 0:wide]
                    if not a.bf16_out:
                        dve.tensor_tensor(dst, sums, inv[n % 2][half(g), :], ALU.mult).then_inc(out_read.sem, 1)
                        return
                    dve.tensor_tensor(raw[half(g), :], sums, inv[n % 2][half(g), :], ALU.mult).then_inc(
                        rounding.sem, 1)
                    dve.wait_ge(rounding.sem, rounding.at(2 * step + 1))
                    col = a.heads + 1
                    dve.tensor_scalar(narrow[half(g), :], raw[half(g), :], bias[half(g), col:col + 1], None,
                                      ALU.add).then_inc(rounding.sem, 1)
                    dve.wait_ge(rounding.sem, rounding.at(2 * step + 2))
                    dve.tensor_copy(dst, narrow[half(g), :]).then_inc(out_read.sem, 1)

                with dve.Fori(0, PAIRS) as j:
                    for n in range(groups):
                        write(j, n)
                    for m in range(banks):
                        peaks(j, 0, m)
                    for m in range(banks):
                        if m == 1:
                            split_peak(j, 0)
                        peaks(j, 1, m)
                    for n in range(both):
                        if n == 0:
                            split_peak(j, 1)
                        normalise(j, n)
                    dve.wait_ge(y_ready.sem, y_ready.at(j + 1))
                    at = bass.ds(j * SEQ, SEQ)
                    if out_bias is None:
                        ins = dve.tensor_tensor(acc[:, at], misc_ps[:, 0:SEQ], acc[:, at], ALU.add)
                    else:
                        ins = dve.scalar_tensor_tensor(acc[:, at], misc_ps[:, 0:SEQ], out_bias, acc[:, at],
                                                       ALU.add, ALU.add)
                    ins.then_inc(y_read.sem, 1)



def add_phase(tower, acc, x):
    with tower.nc.Block() as block:
        @block.vector
        def _(dve):
            dve.tensor_tensor(acc[:], acc[:], x[:], ALU.add)



GROUP = 8
GROUPS = COLS // GROUP


def query_softmax_phase(tower, hn, q, w_name):
    nc = tower.nc
    with phase(tower) as ph:
        wq = ph.sb("wq", [P, P])
        turned = ph.sb("turned", [P, COLS])
        stat = ph.sb("stat", [P, GROUPS])
        q_ps = [ph.ps(f"q{r}") for r in range(4)]
        loaded = ph.counts(16)
        made = ph.counts(TILES)
        copied = ph.counts(TILES)
        v = ph.counts(8)
        exped = ph.counts(1)
        grouped = turned[:].rearrange("p (n e) -> p n e", e=GROUP)
        spread = stat[:, :, None].to_broadcast([P, GROUPS, GROUP])
        with nc.Block() as block:
            @block.sync
            def _(sp):
                sp.dma_start(wq[:], tower.dram[w_name]).then_inc(loaded.sem, 16)

            @block.tensor
            def _(pe):
                pe.wait_ge(loaded.sem, loaded.at(16))
                for n in range(TILES):
                    pe.wait_ge(copied.sem, copied.at(n - 3))
                    pe.matmul(q_ps[n % 4][:, 0:TILE], wq[:], hn[:, n * TILE:(n + 1) * TILE],
                              start=True, stop=True).then_inc(made.sem, 1)

            @block.scalar
            def _(act):
                for n in range(TILES):
                    act.wait_ge(made.sem, made.at(n + 1))
                    act.activation(q[:, n * TILE:(n + 1) * TILE], q_ps[n % 4][:, 0:TILE],
                                   ACT.Copy).then_inc(copied.sem, 1)
                act.wait_ge(v.sem, v.at(3))
                act.activation(turned[:], turned[:], ACT.Exp).then_inc(exped.sem, 1)

            @block.vector
            def _(dve):
                dve.wait_ge(copied.sem, copied.at(TILES))
                dve.transpose(turned[:], q[:]).then_inc(v.sem, 1)
                dve.wait_ge(v.sem, v.at(1))
                dve.tensor_reduce(stat[:], grouped, AX, ALU.max).then_inc(v.sem, 1)
                dve.wait_ge(v.sem, v.at(2))
                dve.tensor_tensor(grouped, grouped, spread, ALU.subtract).then_inc(v.sem, 1)
                dve.wait_ge(exped.sem, exped.at(1))
                dve.tensor_reduce(stat[:], grouped, AX, ALU.add).then_inc(v.sem, 1)
                dve.wait_ge(v.sem, v.at(4))
                dve.reciprocal(stat[:], stat[:]).then_inc(v.sem, 1)
                dve.wait_ge(v.sem, v.at(5))
                dve.tensor_tensor(grouped, grouped, spread, ALU.mult).then_inc(v.sem, 1)
                dve.wait_ge(v.sem, v.at(6))
                dve.transpose(q[:], turned[:]).then_inc(v.sem, 2)


def linear_attention_phase(tower, hn, q, acc, names, out_bias):
    nc, n2 = tower.nc, PAIRS // 2
    cut = [slice(0, 65), slice(65, SEQ)]
    size = [65, 64]
    with phase(tower) as ph:
        wk, wv, wo = [ph.sb(n, [P, P]) for n in ("wk", "wv", "wo")]
        two = range(2)
        xs = [ph.sb(f"xs{u}", [P, SEQ]) for u in two]
        low = [ph.sb(f"low{u}", [P, 1]) for u in two]
        ek = [ph.sb(f"ek{u}", [P, SEQ]) for u in two]
        total = [ph.sb(f"total{u}", [P, 1]) for u in two]
        inv = [ph.sb(f"inv{u}", [P, 1]) for u in two]
        ek_t = [ph.sb(f"ek_t{u}", [65, 2, P]) for u in two]
        vt = [ph.sb(f"vt{u}", [65, 2, P]) for u in two]
        ctx = [ph.sb(f"ctx{u}", [P, P]) for u in two]
        at_s = [ph.sb(f"at{u}", [P, SEQ]) for u in two]
        k_ps = [ph.ps(f"k{u}") for u in two]
        v_ps = [ph.ps(f"v{u}") for u in two]
        t_ps = [ph.ps(f"t{u}") for u in two]
        c_ps = [ph.ps(f"c{u}") for u in two]
        sig = lambda k=1: [ph.counts(n2 * k) for _ in two]
        loaded = ph.counts(48)
        copied, k_made, v_made, lowest, exped, v_copied = sig(), sig(), sig(), sig(), sig(), sig()
        ek_turned, ek_copied, inverted, ctx_made, ctx_ready = sig(), sig(), sig(), sig(), sig()
        at_made, at_copied, y_made, y_read = sig(), sig(), sig(), sig()

        def cols(i, u):
            return bass.ds((2 * i + u) * SEQ, SEQ)

        with nc.Block() as block:
            @block.sync
            def _(sp):
                for buf, name in zip((wk, wv, wo), names):
                    sp.dma_start(buf[:], tower.dram[name]).then_inc(loaded.sem, 16)

            @block.gpsimd
            def _(pool):
                with pool.Fori(0, n2) as i:
                    for u in two:
                        pool.wait_ge(v_made[u].sem, v_made[u].at(i))
                        pool.tensor_copy(xs[u][:], hn[:, cols(i, u)]).then_inc(copied[u].sem, 1)

            @block.tensor
            def _(pe):
                pe.wait_ge(loaded.sem, loaded.at(48))
                with pe.Fori(0, n2) as i:
                    for u in two:
                        pe.wait_ge(copied[u].sem, copied[u].at(i + 1))
                        pe.wait_ge(at_copied[u].sem, at_copied[u].at(i))
                        pe.matmul(k_ps[u][:, 0:SEQ], wk[:], xs[u][:], start=True, stop=True).then_inc(
                            k_made[u].sem, 1)
                        pe.wait_ge(y_read[u].sem, y_read[u].at(i))
                        for c in two:
                            mm = pe.matmul(v_ps[u][0:size[c], c * P:(c + 1) * P], xs[u][:, cut[c]], wv[:],
                                           start=True, stop=True)
                        mm.then_inc(v_made[u].sem, 1)
                    for u in two:
                        pe.wait_ge(exped[u].sem, exped[u].at(i + 1))
                        pe.wait_ge(ek_copied[u].sem, ek_copied[u].at(i))
                        for c in two:
                            mm = pe.transpose(t_ps[u][0:size[c], c * P:(c + 1) * P], ek[u][:, cut[c]],
                                              tower.ident[:])
                        mm.then_inc(ek_turned[u].sem, 1)
                    for u in two:
                        pe.wait_ge(ek_copied[u].sem, ek_copied[u].at(i + 1))
                        pe.wait_ge(v_copied[u].sem, v_copied[u].at(i + 1))
                        pe.wait_ge(ctx_ready[u].sem, ctx_ready[u].at(i))
                        for c in two:
                            mm = pe.matmul(c_ps[u][:, 0:P], ek_t[u][0:size[c], c, :], vt[u][0:size[c], c, :],
                                           start=c == 0, stop=c == 1)
                        mm.then_inc(ctx_made[u].sem, 1)
                    for u in two:
                        pe.wait_ge(ctx_ready[u].sem, ctx_ready[u].at(i + 1))
                        pe.matmul(k_ps[u][:, 0:SEQ], ctx[u][:], q[:, cols(i, u)],
                                  start=True, stop=True).then_inc(at_made[u].sem, 1)
                    for u in two:
                        pe.wait_ge(at_copied[u].sem, at_copied[u].at(i + 1))
                        pe.matmul(v_ps[u][:, 0:SEQ], wo[:], at_s[u][:], start=True, stop=True).then_inc(
                            y_made[u].sem, 1)

            @block.scalar
            def _(act):
                with act.Fori(0, n2) as i:
                    for u in two:
                        act.wait_ge(v_made[u].sem, v_made[u].at(i + 1))
                        for c in two:
                            ins = act.activation(vt[u][0:size[c], c, :], v_ps[u][0:size[c], c * P:(c + 1) * P],
                                                 ACT.Copy)
                        ins.then_inc(v_copied[u].sem, 1)
                        act.wait_ge(lowest[u].sem, lowest[u].at(i + 1))
                        act.activation(ek[u][:], k_ps[u][:, 0:SEQ], ACT.Exp, bias=low[u][:, 0:1],
                                       accum_out=total[u][:, 0:1]).then_inc(exped[u].sem, 1)
                    for u in two:
                        act.wait_ge(at_made[u].sem, at_made[u].at(i + 1))
                        act.activation(at_s[u][:], k_ps[u][:, 0:SEQ], ACT.Copy).then_inc(at_copied[u].sem, 1)

            @block.vector
            def _(dve):
                with dve.Fori(0, n2) as i:
                    for u in two:
                        dve.wait_ge(k_made[u].sem, k_made[u].at(i + 1))
                        dve.tensor_reduce(low[u][:], k_ps[u][:, 0:SEQ], AX, ALU.max,
                                          negate=True).then_inc(lowest[u].sem, 1)
                    for u in two:
                        dve.wait_ge(ek_turned[u].sem, ek_turned[u].at(i + 1))
                        for c in two:
                            ins = dve.tensor_copy(ek_t[u][0:size[c], c, :], t_ps[u][0:size[c], c * P:(c + 1) * P])
                        ins.then_inc(ek_copied[u].sem, 1)
                        dve.reciprocal(inv[u][:], total[u][:]).then_inc(inverted[u].sem, 1)
                    for u in two:
                        dve.wait_ge(ctx_made[u].sem, ctx_made[u].at(i + 1))
                        dve.wait_ge(inverted[u].sem, inverted[u].at(i + 1))
                        dve.scalar_tensor_tensor(ctx[u][:], c_ps[u][:, 0:P], inv[u][:, 0:1],
                                                 tower.head_blocks[:], ALU.mult, ALU.mult).then_inc(
                            ctx_ready[u].sem, 1)
                    for u in two:
                        dve.wait_ge(y_made[u].sem, y_made[u].at(i + 1))
                        dve.scalar_tensor_tensor(acc[:, cols(i, u)], v_ps[u][:, 0:SEQ], out_bias,
                                                 acc[:, cols(i, u)], ALU.add, ALU.add).then_inc(
                            y_read[u].sem, 1)


def linear_tower(tower, nc, h, x, column):
    with ExitStack() as stack:
        hn = stack.enter_context(nc.sbuf_tensor("lin_hn", [P, COLS], F32))
        q = stack.enter_context(nc.sbuf_tensor("lin_q", [P, COLS], F32))
        with phase(tower) as ph:
            pos = ph.sb("pos", [P, SEQ])
            loaded = ph.counts(32)
            with nc.Block() as block:
                @block.sync
                def _(sp):
                    sp.dma_start(pos[:], tower.dram["L1_pos"]).then_inc(loaded.sem, 16)
                    sp.dma_start(tower.head_blocks[:], tower.dram["L1_blocks"]).then_inc(loaded.sem, 16)

                @block.vector
                def _(dve):
                    dve.wait_ge(loaded.sem, loaded.at(32))
                    xj = x[:].rearrange("p (j t) -> p j t", t=SEQ)
                    dve.tensor_tensor(xj, xj, pos[:, None, :].to_broadcast([P, PAIRS, SEQ]), ALU.add)
        for l in range(4):
            norm_phase(tower, x, hn, 1e-5, gamma=column(f"L1_g1{l}"), beta=column(f"L1_b1{l}"))
            query_softmax_phase(tower, hn, q, f"L1_wq{l}")
            linear_attention_phase(tower, hn, q, x, [f"L1_wk{l}", f"L1_wv{l}", f"L1_wo{l}"],
                                   column(f"L1_bo{l}"))
            norm_phase(tower, x, hn, 1e-5, gamma=column(f"L1_g2{l}"), beta=column(f"L1_b2{l}"))
            mlp_phase(tower, f"L1_up{l}", f"L1_down{l}", f"L1_up_b{l}", 4, ACT.Gelu, P,
                      lambda b: hn, AddTo(x, column(f"L1_bf2{l}")), None)
        add_phase(tower, h, x)



KEPT = max(1, int(0.5 * SEQ)) - 1


class WeightedAddTo:

    def __init__(self, tower, acc, bias, weight_rows, rows):
        self.acc, self.bias, self.weights, self.rows = acc, bias, weight_rows, rows
        self.tower = tower

    def load(self, ph):
        self.tmp = [ph.sb(f"weighted{u}", [P, TILE]) for u in range(2)]
        self.made = ph.counts(TILES)

    def broadcast(self, pe, aux, state, cols, u):
        return pe.matmul(aux[:, 0:TILE], self.tower.spread2[0:self.rows, :], self.weights[0:self.rows, cols],
                         start=True, stop=True)

    def vector(self, dve, y, aux, state, cols, i, u):
        dve.scalar_tensor_tensor(self.tmp[u][:], y, self.bias, aux[:], ALU.add,
                                 ALU.mult).then_inc(self.made.sem, 1)
        dve.wait_ge(self.made.sem, self.made.at(2 * i + u + 1))
        return dve.tensor_tensor(self.acc[:, cols], self.acc[:, cols], self.tmp[u][:], ALU.add)


def half_ffn(tower, nc, h, x, column):
    add_phase(tower, h, x)
    with ExitStack() as stack:
        rows = stack.enter_context(nc.sbuf_tensor("mod_rows", [HALVES, COLS], F32))
        with phase(tower) as ph:
            wr = ph.sb("wr", [P, HALVES])
            br = ph.sb("br", [HALVES, 1])
            weight = ph.sb("weight", [D, SEQ])
            race = ph.sb("race", [D, SEQ])
            top = ph.sb("top", [D, 8])
            w_ps = [ph.ps(f"w{r}") for r in range(4)]
            loaded = ph.counts(32)
            made = ph.counts(TILES)
            copied = ph.counts(TILES)
            turned = ph.counts(32)
            back = ph.counts(32)
            rounds = -(-KEPT // 8)
            v = ph.counts(2 * rounds + 3)
            with nc.Block() as block:
                @block.sync
                def _(sp):
                    sp.dma_start(wr[:], tower.dram["L1f_wr"]).then_inc(loaded.sem, 16)
                    sp.dma_start(br[:], tower.dram["L1f_br"]).then_inc(loaded.sem, 16)
                    sp.wait_ge(copied.sem, copied.at(TILES))
                    for g in range(HALVES):
                        sp.dma_start(weight[PAIRS * g:PAIRS * (g + 1), :],
                                     rows[g:g + 1, :].rearrange("a (j t) -> a j t", t=SEQ)).then_inc(
                            turned.sem, 16)
                    sp.wait_ge(v.sem, v.at(2 * rounds + 3))
                    for g in range(HALVES):
                        sp.dma_start(rows[g:g + 1, :].rearrange("a (j t) -> a j t", t=SEQ),
                                     race[PAIRS * g:PAIRS * (g + 1), :]).then_inc(back.sem, 16)
                    sp.wait_ge(back.sem, back.at(32))

                @block.tensor
                def _(pe):
                    pe.wait_ge(loaded.sem, loaded.at(32))
                    for n in range(TILES):
                        pe.wait_ge(copied.sem, copied.at(n - 3))
                        pe.matmul(w_ps[n % 4][0:HALVES, 0:TILE], wr[:], x[:, n * TILE:(n + 1) * TILE],
                                  start=True, stop=True).then_inc(made.sem, 1)

                @block.scalar
                def _(act):
                    for n in range(TILES):
                        act.wait_ge(made.sem, made.at(n + 1))
                        act.activation(rows[:, n * TILE:(n + 1) * TILE], w_ps[n % 4][0:HALVES, 0:TILE],
                                       ACT.Identity, bias=br[:, 0:1]).then_inc(copied.sem, 1)

                @block.vector
                def _(dve):
                    done = [0]

                    def step(ins):
                        done[0] += 1
                        ins.then_inc(v.sem, 1)
                        dve.wait_ge(v.sem, v.at(done[0]))

                    dve.wait_ge(turned.sem, turned.at(32))
                    step(dve.tensor_copy(race[:], weight[:]))
                    for r in range(rounds):
                        step(dve.max(top[:], race[:]))
                        if r == rounds - 1:
                            step(dve.memset(top[:, KEPT - 8 * r:8], 3.0e38))
                        step(dve.match_replace(race[:], top[:], race[:], -3.0e38))
                    step(dve.scalar_tensor_tensor(race[:], race[:], -3.0e38, weight[:], ALU.is_equal, ALU.mult))
                    v.total = done[0]
                    assert done[0] == 2 * rounds + 3
        finish = WeightedAddTo(tower, h, column("L1f_b2"), rows, HALVES)
        mlp_phase(tower, "L1f_up", "L1f_down", "L1f_up_b", 4, ACT.Gelu_apprx_tanh, P,
                  lambda b: x, finish, finish.load)



HIDDEN = int(8 / 3 * D)
SLAB = 2 * HIDDEN // 3 + 1
SLABS = 3


def gated_experts_phase(tower, hn, rows_t, acc):
    nc = tower.nc
    blocks = EXPERTS * SLABS
    lag = 2
    with phase(tower) as ph:
        w1 = ph.sb("w1", [P, blocks, SLAB])
        w3 = ph.sb("w3", [P, blocks, SLAB])
        w2 = ph.sb("w2", [SLAB, blocks, P])
        pick = ph.sb("pick", [P, EXPERTS, P])
        a_ps, c_ps = [[ph.ps(f"{n}{r}") for r in range(2)] for n in "ac"]
        weight_ps = [ph.ps(f"weight{r}") for r in range(2)]
        y_ps = [ph.ps(f"y{u}") for u in range(2)]
        weighted = [ph.sb(f"weighted{r}", [P, TILE]) for r in range(2)]
        silu = [ph.sb(f"silu{r}", [SLAB, TILE]) for r in range(2)]
        hid = [ph.sb(f"hid{r}", [SLAB, TILE]) for r in range(3)]
        n2 = TILES // 2
        per, per_e = 2 * blocks, 2 * EXPERTS
        loaded = ph.counts(64)
        weight_made = ph.counts(n2 * per_e)
        weighted_ready = ph.counts(n2 * per_e)
        up_made = ph.counts(n2 * per)
        silu_ready = ph.counts(n2 * per)
        hid_ready = ph.counts(n2 * per)
        down_made = ph.counts(n2 * per)
        y_read = [ph.counts(n2) for _ in range(2)]

        def cols(i, u):
            return bass.ds((2 * i + u) * TILE, TILE)

        with nc.Block() as block:
            @block.sync
            def _(sp):
                for buf, name in ((pick, "L2m_pick"), (w1, "L2m_w1"), (w3, "L2m_w3"), (w2, "L2m_w2")):
                    sp.dma_start(buf[:], tower.dram[name]).then_inc(loaded.sem, 16)

            @block.tensor
            def _(pe):
                pe.wait_ge(loaded.sem, loaded.at(64))

                def spread(i, x):
                    pe.wait_ge(weighted_ready.sem, weighted_ready.at(i * per_e + x - 1))
                    pe.matmul(weight_ps[x % 2][:, 0:TILE], pick[:, x % EXPERTS, :],
                              rows_t[:, cols(i, x // EXPERTS)], start=True, stop=True).then_inc(
                        weight_made.sem, 1)

                def up(i, n):
                    x, b, u = n // SLABS, n % blocks, n // blocks
                    pe.wait_ge(hid_ready.sem, hid_ready.at(i * per + n - 1))
                    pe.matmul(a_ps[n % 2][0:SLAB, 0:TILE], w1[:, b, :], hn[:, cols(i, u)],
                              start=True, stop=True)
                    pe.wait_ge(weighted_ready.sem, weighted_ready.at(i * per_e + x + 1))
                    pe.matmul(c_ps[n % 2][0:SLAB, 0:TILE], w3[:, b, :], weighted[x % 2][:],
                              start=True, stop=True).then_inc(up_made.sem, 1)

                def down(i, m):
                    b, u = m % blocks, m // blocks
                    if b == 0:
                        pe.wait_ge(y_read[u].sem, y_read[u].at(i))
                    pe.wait_ge(hid_ready.sem, hid_ready.at(i * per + m + 1))
                    pe.matmul(y_ps[u][:, 0:TILE], w2[:, b, :], hid[m % 3][:], start=b == 0,
                              stop=b == blocks - 1).then_inc(down_made.sem, 1)

                with pe.Fori(0, n2) as i:
                    spread(i, 0)
                    for n in range(per + lag):
                        if n < per and n % SLABS == 0 and n // SLABS + 1 < per_e:
                            spread(i, n // SLABS + 1)
                        if n < per:
                            up(i, n)
                        if n >= lag:
                            down(i, n - lag)

            @block.scalar
            def _(act):
                with act.Fori(0, n2) as i:
                    for n in range(per):
                        act.wait_ge(up_made.sem, up_made.at(i * per + n + 1))
                        act.wait_ge(hid_ready.sem, hid_ready.at(i * per + n - 1))
                        act.activation(silu[n % 2][:], a_ps[n % 2][0:SLAB, 0:TILE],
                                       ACT.Silu).then_inc(silu_ready.sem, 1)

            @block.vector
            def _(dve):
                def weigh(i, x):
                    dve.wait_ge(weight_made.sem, weight_made.at(i * per_e + x + 1))
                    dve.wait_ge(up_made.sem, up_made.at(i * per + (x - 1) * SLABS))
                    dve.tensor_tensor(weighted[x % 2][:], hn[:, cols(i, x // EXPERTS)],
                                      weight_ps[x % 2][:, 0:TILE], ALU.mult).then_inc(weighted_ready.sem, 1)

                def add_y(i, u):
                    dve.wait_ge(down_made.sem, down_made.at(i * per + (u + 1) * blocks))
                    dve.tensor_tensor(acc[:, cols(i, u)], acc[:, cols(i, u)], y_ps[u][:, 0:TILE],
                                      ALU.add).then_inc(y_read[u].sem, 1)

                with dve.Fori(0, n2) as i:
                    weigh(i, 0)
                    for n in range(per):
                        if n % SLABS == 0 and n // SLABS + 1 < per_e:
                            weigh(i, n // SLABS + 1)
                        dve.wait_ge(silu_ready.sem, silu_ready.at(i * per + n + 1))
                        dve.wait_ge(down_made.sem, down_made.at(i * per + n - 2))
                        dve.tensor_tensor(hid[n % 3][:], silu[n % 2][:], c_ps[n % 2][0:SLAB, 0:TILE],
                                          ALU.mult).then_inc(hid_ready.sem, 1)
                        if n == blocks + lag:
                            add_y(i, 0)
                    add_y(i, 1)


def routed_block(tower, nc, h, x, column):
    with ExitStack() as stack:
        hn = stack.enter_context(nc.sbuf_tensor("routed_hn", [P, COLS], F32))
        norm_phase(tower, x, hn, 1e-6, center=False, gamma=column("L2_ln1"))
        attention_phase(tower, hn, x, ATTENTION["L2f"])
        norm_phase(tower, x, hn, 1e-6, center=False, gamma=column("L2_ln2"))
        with ExitStack() as inner:
            rows_t = inner.enter_context(nc.sbuf_tensor("routed_rows", [P, COLS], F32))
            gate_phase(tower, hn, "L2_gate_w", "L2_gate_b", 2, True, rows_t)
            add_phase(tower, h, x)
            gated_experts_phase(tower, hn, rows_t, h)



TOKENS = HALVES * COLS
CAPACITY = max(1, -(-5 * TOKENS // (4 * EXPERTS)))


def capacity_phase(tower, rows_t, scale_rows):
    nc = tower.nc
    with phase(tower) as ph:
        before = ph.sb("before", [64, 1])
        count = ph.sb("count", [64, COLS])
        pick = ph.sb("pick", [64, 2, HALVES])
        kept = [ph.sb(f"kept{r}", [HALVES, TILE]) for r in range(2)]
        kept_ps = [ph.ps(f"kept_ps{r}") for r in range(2)]
        prob_ps = [ph.ps(f"prob_ps{r}") for r in range(2)]
        loaded = ph.counts(16)
        v = ph.counts(5)
        made = ph.counts(TILES)
        copied = ph.counts(TILES)
        scaled = ph.counts(TILES)
        with nc.Block() as block:
            @block.sync
            def _(sp):
                sp.dma_start(pick[:], tower.dram["L3_pick"]).then_inc(loaded.sem, 16)

            @block.vector
            def _(dve):
                dve.memset(before[:], 0.0).then_inc(v.sem, 1)
                dve.tensor_reduce(count[0:8, 0:1], rows_t[0:8, :], AX, ALU.add).then_inc(v.sem, 1)
                dve.wait_ge(v.sem, v.at(2))
                dve.tensor_copy(before[32:40, :], count[0:8, 0:1]).then_inc(v.sem, 1)
                dve.wait_ge(v.sem, v.at(3))
                dve.tensor_tensor_scan(count[:], rows_t[:], rows_t[:], before[:, 0:1], ALU.add,
                                       ALU.bypass).then_inc(v.sem, 1)
                dve.wait_ge(v.sem, v.at(4))
                dve.scalar_tensor_tensor(count[:], count[:], float(CAPACITY), rows_t[:], ALU.is_le,
                                         ALU.mult).then_inc(v.sem, 1)
                for n in range(TILES):
                    dve.wait_ge(copied.sem, copied.at(n + 1))
                    dve.tensor_tensor(scale_rows[:, n * TILE:(n + 1) * TILE], kept[n % 2][:],
                                      prob_ps[n % 2][0:HALVES, 0:TILE], ALU.mult).then_inc(scaled.sem, 1)

            @block.tensor
            def _(pe):
                pe.wait_ge(loaded.sem, loaded.at(16))
                pe.wait_ge(v.sem, v.at(5))
                for n in range(TILES):
                    pe.wait_ge(scaled.sem, scaled.at(n - 1))
                    at = slice(n * TILE, (n + 1) * TILE)
                    pe.matmul(kept_ps[n % 2][0:HALVES, 0:TILE], pick[:, 0, :], count[:, at],
                              start=True, stop=True)
                    pe.matmul(prob_ps[n % 2][0:HALVES, 0:TILE], pick[:, 1, :], rows_t[:, at],
                              start=True, stop=True).then_inc(made.sem, 1)

            @block.scalar
            def _(act):
                for n in range(TILES):
                    act.wait_ge(made.sem, made.at(n + 1))
                    act.wait_ge(scaled.sem, scaled.at(n - 1))
                    act.activation(kept[n % 2][:], kept_ps[n % 2][0:HALVES, 0:TILE],
                                   ACT.Copy).then_inc(copied.sem, 1)


def capacity_ffn(tower, nc, h, x):
    with ExitStack() as stack:
        scale_rows = stack.enter_context(nc.sbuf_tensor("cap_scale", [HALVES, COLS], F32))
        aug = [stack.enter_context(nc.sbuf_tensor(f"cap_aug{g}", [104, COLS], F32)) for g in range(HALVES)]
        with ExitStack() as inner:
            rows_t = inner.enter_context(nc.sbuf_tensor("cap_rows", [64, COLS], F32))
            gate_phase(tower, x, "L3_gate_w", "L3_gate_b", 1, False, rows_t)
            spread_phase(tower, x, rows_t, aug)
            capacity_phase(tower, rows_t, scale_rows)
        finish = WeightedAddTo(tower, h, 0.0, scale_rows, HALVES)
        mlp_phase(tower, "L3_up", "L3_down", "L3_up_b", 4 * EXPERTS, ACT.Relu, 72,
                  lambda b: aug[b % 2], finish, finish.load, extra=("L3_down_b", 104, aug),
                  up_of=lambda b: b // HALVES)



JOINTS = 64
TAPS_H = 5
ROWS_PADDED = JOINTS + TAPS_H - 1
TOKENS_IN = SEQ - 1


def tokenizer_phase(tower, h, column):
    nc, n2, two = tower.nc, PAIRS // 2, range(2)
    with phase(tower) as ph:
        c1w, c2w = ph.sb("c1w", [P, 15, P]), ph.sb("c2w", [P, 10, P])
        c3w, ow = ph.sb("c3w", [P, 10, 2, P]), ph.sb("ow", [P, HALVES, P])
        ln0 = ph.sb("ln0", [P, 2, 192])
        ln1 = ph.sb("ln1", [P, 2, 128])
        x_in = [ph.sb(f"x{u}", [P, HALVES, 192]) for u in two]
        pad1 = [ph.sb(f"pad1{u}", [P, HALVES, ROWS_PADDED, 5]) for u in two]
        pad2 = [ph.sb(f"pad2{u}", [P, HALVES, ROWS_PADDED, 3]) for u in two]
        pad3 = [ph.sb(f"pad3{u}", [P, HALVES, ROWS_PADDED, 2]) for u in two]
        act1 = [ph.sb(f"act1{u}", [P, HALVES, 192]) for u in two]
        act2 = [ph.sb(f"act2{u}", [P, HALVES, 128]) for u in two]
        act3 = [ph.sb(f"act3{u}", [P, HALVES, 128]) for u in two]
        normed = [ph.sb(f"normed{u}", [P, HALVES, 192]) for u in two]
        scaled_by = [ph.sb(f"scaled{u}", [P, HALVES, 192]) for u in two]
        last = [ph.sb(f"last{u}", [P, HALVES, 128]) for u in two]
        turned_s = [ph.sb(f"turned{u}", [P, HALVES, 128]) for u in two]
        stats = [ph.sb(f"stats{u}", [P, HALVES, 6]) for u in two]
        moments = [ph.sb(f"moments{u}", [P, HALVES, 2]) for u in two]
        rstd = [ph.sb(f"rstd{u}", [P, HALVES]) for u in two]
        held = ph.sb("held", [P, 1])
        c1_ps, c2_ps, c3_ps, y_ps = [[ph.ps(f"{n}{u}") for u in two] for n in ("c1", "c2", "c3", "y")]
        sig = lambda k=1: [ph.counts(n2 * k) for _ in two]
        loaded = ph.counts(16 * 6)
        cleared = ph.counts(1)
        landed = [ph.counts(n2 * 16) for _ in two]
        conv1, conv2, conv3, relu1, relu2, relu3 = sig(), sig(), sig(), sig(), sig(), sig()
        padded1, padded2, padded3, last_ready = sig(), sig(), sig(), sig()
        measured, rstd_ready, chain = sig(4), sig(4), sig(4 * 3)
        logged = sig(4)
        turned, turned_copied, y_made, y_written = sig(), sig(), sig(), sig()

        with nc.Block() as block:
            @block.sync
            def _(sp):
                for buf, name in ((ln0, "tok_ln0"), (c1w, "tok_c1w"), (c2w, "tok_c2w"), (ln1, "tok_ln1"),
                                  (c3w, "tok_c3w"), (ow, "tok_ow")):
                    sp.dma_start(buf[:], tower.dram[name]).then_inc(loaded.sem, 16)
                with sp.Fori(0, n2) as i:
                    for u in two:
                        sp.wait_ge(padded1[u].sem, padded1[u].at(i))
                        sp.dma_start(x_in[u][:], tower.dram["tok_x"][bass.ds(2 * i + u, 1), :, :, :]
                                     .rearrange("o p g n -> (o p) g n")).then_inc(landed[u].sem, 16)

            @block.gpsimd
            def _(pool):
                for pads in (pad1, pad2, pad3):
                    for u in two:
                        ins = pool.memset(pads[u][:], 0.0)
                ins.then_inc(cleared.sem, 1)

            @block.tensor
            def _(pe):
                pe.wait_ge(loaded.sem, loaded.at(96))

                def taps(to, pad, weights, kw_of, width):
                    n = TAPS_H * kw_of
                    for k in range(n):
                        kh, kw = k // kw_of, k % kw_of
                        mm = pe.matmul(to, weights(k), pad[:, :, kh:kh + JOINTS, kw:kw + width],
                                       start=k == 0, stop=k == n - 1)
                    return mm

                with pe.Fori(0, n2) as i:
                    for u in two:
                        pe.wait_ge(padded1[u].sem, padded1[u].at(i + 1))
                        pe.wait_ge(relu1[u].sem, relu1[u].at(i))
                        taps(c1_ps[u][:, 0:384], pad1[u], lambda k: c1w[:, k, :], 3, 3).then_inc(
                            conv1[u].sem, 1)
                    for u in two:
                        pe.wait_ge(padded2[u].sem, padded2[u].at(i + 1))
                        pe.wait_ge(relu2[u].sem, relu2[u].at(i))
                        taps(c2_ps[u][:, 0:256], pad2[u], lambda k: c2w[:, k, :], 2, 2).then_inc(
                            conv2[u].sem, 1)
                    for u in two:
                        pe.wait_ge(padded3[u].sem, padded3[u].at(i + 1))
                        pe.wait_ge(relu3[u].sem, relu3[u].at(i))
                        for part in range(2):
                            mm = taps(c3_ps[u][:, part * 128:part * 128 + 128], pad3[u],
                                      lambda k: c3w[:, k, part, :], 2, 1)
                        mm.then_inc(conv3[u].sem, 1)
                    for u in two:
                        pe.wait_ge(last_ready[u].sem, last_ready[u].at(i + 1))
                        pe.wait_ge(y_written[u].sem, y_written[u].at(i))
                        for g in range(HALVES):
                            mm = pe.transpose(y_ps[u][:, g * P:(g + 1) * P], last[u][:, g, :], tower.ident[:])
                        mm.then_inc(turned[u].sem, 1)
                    for u in two:
                        pe.wait_ge(turned_copied[u].sem, turned_copied[u].at(i + 1))
                        for g in range(HALVES):
                            mm = pe.matmul(y_ps[u][:, 256:384], ow[:, g, :], turned_s[u][:, g, :],
                                           start=g == 0, stop=g == 1)
                        mm.then_inc(y_made[u].sem, 1)

            @block.scalar
            def _(act):
                act.preload_act_table_set("natural_log_exp_and_others")
                eps = tower.eps[1e-5]

                def inverse(i, u, k):
                    at = 4 * i + k + 1
                    act.wait_ge(measured[u].sem, measured[u].at(at))
                    act.activation(rstd[u][:], moments[u][:, :, 1], ACT.Ln, bias=eps).then_inc(logged[u].sem, 1)
                    act.wait_ge(logged[u].sem, logged[u].at(at))
                    act.activation(rstd[u][:], rstd[u][:], ACT.Exp, scale=-0.5).then_inc(rstd_ready[u].sem, 1)

                with act.Fori(0, n2) as i:
                    for u in two:
                        inverse(i, u, 0)
                    for u in two:
                        act.wait_ge(conv1[u].sem, conv1[u].at(i + 1))
                        act.activation(act1[u][:], c1_ps[u][:, 0:384].rearrange("p (g n) -> p g n", g=2),
                                       ACT.Relu, bias=column("tok_c1b")).then_inc(relu1[u].sem, 1)
                        inverse(i, u, 1)
                    for u in two:
                        act.wait_ge(conv2[u].sem, conv2[u].at(i + 1))
                        act.activation(act2[u][:], c2_ps[u][:, 0:256].rearrange("p (g n) -> p g n", g=2),
                                       ACT.Relu, bias=column("tok_c2b")).then_inc(relu2[u].sem, 1)
                        inverse(i, u, 2)
                    for u in two:
                        act.wait_ge(conv3[u].sem, conv3[u].at(i + 1))
                        for part in range(2):
                            ins = act.activation(act3[u][:, :, part * 64:part * 64 + 64],
                                                 c3_ps[u][:, part * 128:part * 128 + 128]
                                                 .rearrange("p (g n) -> p g n", g=2),
                                                 ACT.Relu, bias=column(f"tok_c3b{part}"))
                        ins.then_inc(relu3[u].sem, 1)
                        inverse(i, u, 3)
                    for u in two:
                        act.wait_ge(turned[u].sem, turned[u].at(i + 1))
                        act.activation(turned_s[u][:], y_ps[u][:, 0:256].rearrange("p (g n) -> p g n", g=2),
                                       ACT.Copy).then_inc(turned_copied[u].sem, 1)
                    for u in two:
                        act.wait_ge(y_made[u].sem, y_made[u].at(i + 1))
                        act.activation(h[:, bass.ds((2 * i + u) * SEQ + 1, TOKENS_IN)], y_ps[u][:, 256:384],
                                       ACT.Identity, bias=column("tok_out_b")).then_inc(y_written[u].sem, 1)

            @block.vector
            def _(dve):
                dve.tensor_copy(h[:].rearrange("p (j t) -> p j t", t=SEQ)[:, :, 0],
                                column("cls").to_broadcast([P, PAIRS]))
                dve.wait_ge(loaded.sem, loaded.at(96))
                dve.wait_ge(cleared.sem, cleared.at(1))

                def norm(i, u, k, src, n, table, dst):
                    base = 12 * i + 3 * k
                    for g in range(HALVES):
                        ins = dve.bn_stats(stats[u][:, g, :], src[:, g, 0:n])
                    ins.then_inc(chain[u].sem, 1)
                    dve.wait_ge(chain[u].sem, chain[u].at(base + 1))
                    dve.memset(held[:], 0.0)
                    for g in range(HALVES):
                        ins = dve.bn_aggr(moments[u][:, g, :], stats[u][:, g, :])
                    ins.then_inc(measured[u].sem, 1)
                    dve.wait_ge(rstd_ready[u].sem, rstd_ready[u].at(4 * i + k + 1))
                    for g in range(HALVES):
                        ins = dve.tensor_scalar(normed[u][:, g, 0:n], src[:, g, 0:n], moments[u][:, g, 0:1],
                                                rstd[u][:, g:g + 1], ALU.subtract, ALU.mult)
                    ins.then_inc(chain[u].sem, 1)
                    dve.wait_ge(chain[u].sem, chain[u].at(base + 2))
                    both = lambda m: table[:, m:m + 1, 0:n].to_broadcast([P, HALVES, n])
                    dve.tensor_tensor(scaled_by[u][:, :, 0:n], normed[u][:, :, 0:n], both(0),
                                      ALU.mult).then_inc(chain[u].sem, 1)
                    dve.wait_ge(chain[u].sem, chain[u].at(base + 3))
                    for g in range(HALVES):
                        ins = dve.tensor_tensor(dst(g), shaped(scaled_by[u][:, g, 0:n], k),
                                                shaped(table[:, 1, 0:n], k), ALU.add)
                    return ins

                def shaped(ap, k):
                    return ap if k == 3 else ap.rearrange("p (h w) -> p h w", h=JOINTS)

                with dve.Fori(0, n2) as i:
                    for u in two:
                        dve.wait_ge(landed[u].sem, landed[u].at(16 * i + 16))
                        norm(i, u, 0, x_in[u], 192, ln0, lambda g: pad1[u][:, g, 2:66, 1:4]).then_inc(
                            padded1[u].sem, 1)
                    for u in two:
                        dve.wait_ge(relu1[u].sem, relu1[u].at(i + 1))
                        norm(i, u, 1, act1[u], 192, ln0, lambda g: pad2[u][:, g, 2:66, :]).then_inc(
                            padded2[u].sem, 1)
                    for u in two:
                        dve.wait_ge(relu2[u].sem, relu2[u].at(i + 1))
                        norm(i, u, 2, act2[u], 128, ln1, lambda g: pad3[u][:, g, 2:66, :]).then_inc(
                            padded3[u].sem, 1)
                    for u in two:
                        dve.wait_ge(relu3[u].sem, relu3[u].at(i + 1))
                        norm(i, u, 3, act3[u], 128, ln1, lambda g: last[u][:, g, :]).then_inc(
                            last_ready[u].sem, 1)



THIRD = SEQ // 3
WIDE_HEADS = 3
SLICES = 3


def thirds_attention_phase(tower, h, xn, column):
    nc, n2, two = tower.nc, PAIRS // 2, range(2)
    heads = WIDE_HEADS
    qk = 2 * THIRD
    add_phase(tower, h, xn)
    with phase(tower) as ph:
        we = ph.sb("we", [P, heads, SLICES, P])
        be = ph.sb("be", [P, heads, SLICES])
        bv = ph.sb("bv", [THIRD, heads, SLICES * P])
        wo = ph.sb("wo", [P, SLICES, P])
        xs = [ph.sb(f"xs{u}", [P, SEQ]) for u in two]
        e_s = [ph.sb(f"e{u}", [P, heads, SLICES, qk]) for u in two]
        v_s = [ph.sb(f"v{u}", [THIRD, heads, SLICES, P]) for u in two]
        peak = [ph.sb(f"peak{u}", [THIRD, HALVES, heads]) for u in two]
        total = [ph.sb(f"total{u}", [THIRD, HALVES, heads]) for u in two]
        prob = [ph.sb(f"prob{u}", [THIRD, HALVES, heads, THIRD]) for u in two]
        prob_t = [ph.sb(f"prob_t{u}", [THIRD, HALVES, heads, THIRD]) for u in two]
        o_s = [ph.sb(f"o{u}", [P, SLICES, SEQ]) for u in two]
        e_ps, s_ps, v_ps = [[ph.ps(f"{n}{r}") for r in two] for n in ("e", "s", "v")]
        t_ps, o_ps = ph.ps("t"), ph.ps("o")
        loaded = ph.counts(64)
        copied = ph.counts(2 * n2)
        e_made, e_read = ph.counts(6 * n2), ph.counts(6 * n2)
        s_made, s_peaked, s_read = ph.counts(4 * n2), ph.counts(4 * n2), ph.counts(4 * n2)
        v_made, v_read = ph.counts(6 * n2), ph.counts(6 * n2)
        exped, summed, inverted, prob_ready = [ph.counts(2 * n2) for _ in range(4)]
        turned, turned_read = ph.counts(2 * n2), ph.counts(2 * n2)
        o_made, o_read, y_made, y_read = [ph.counts(2 * n2) for _ in range(4)]

        def cols(i, u):
            return bass.ds((2 * i + u) * SEQ, SEQ)

        def half(g):
            return slice(D * g, D * g + D)

        with nc.Block() as block:
            @block.sync
            def _(sp):
                for buf, name in ((we, "L0_we"), (be, "L0_be"), (bv, "L0_bv"), (wo, "L0_wo")):
                    sp.dma_start(buf[:], tower.dram[name]).then_inc(loaded.sem, 16)

            @block.gpsimd
            def _(pool):
                with pool.Fori(0, n2) as i:
                    for u in two:
                        pool.wait_ge(v_made.sem, v_made.at(6 * i + 3 * u - 3))
                        pool.tensor_copy(xs[u][:], xn[:, cols(i, u)]).then_inc(copied.sem, 1)

            @block.tensor
            def _(pe):
                pe.wait_ge(loaded.sem, loaded.at(64))
                with pe.Fori(0, n2) as i:
                    for u in two:
                        pe.wait_ge(copied.sem, copied.at(2 * i + u + 1))
                        for hd in range(heads):
                            n = 3 * u + hd
                            pe.wait_ge(e_read.sem, e_read.at(6 * i + n - 1))
                            for c in range(SLICES):
                                mm = pe.matmul(e_ps[n % 2][:, c * qk:(c + 1) * qk], we[:, hd, c, :],
                                               xs[u][:, 0:qk], start=True, stop=True)
                            mm.then_inc(e_made.sem, 1)
                    for u in two:
                        pe.wait_ge(e_read.sem, e_read.at(6 * i + 3 * u + 3))
                        for g in range(HALVES):
                            if u == 0:
                                pe.wait_ge(y_read.sem, y_read.at(2 * i))
                            pe.wait_ge(s_read.sem, s_read.at(4 * i + 2 * u + g - 1))
                            for hd in range(heads):
                                for c in range(SLICES):
                                    mm = pe.matmul(s_ps[g][0:qk, hd * THIRD:(hd + 1) * THIRD],
                                                   e_s[u][half(g), hd, c, :],
                                                   e_s[u][half(g), hd, c, THIRD:qk],
                                                   start=c == 0, stop=c == SLICES - 1)
                            mm.then_inc(s_made.sem, 1)
                        for hd in range(heads):
                            n = 3 * u + hd
                            pe.wait_ge(v_read.sem, v_read.at(6 * i + n - 1))
                            pe.matmul(v_ps[n % 2][0:THIRD, 0:SLICES * P], xs[u][:, qk:SEQ],
                                      we[:, hd, :, :].rearrange("p c n -> p (c n)"),
                                      start=True, stop=True).then_inc(v_made.sem, 1)
                    for u in two:
                        pe.wait_ge(prob_ready.sem, prob_ready.at(2 * i + u + 1))
                        pe.wait_ge(turned_read.sem, turned_read.at(2 * i + u))
                        pe.matmul(t_ps[:, 0:2], tower.ident[:], tower.ident[:, 0:2], start=True, stop=True)
                        for g in range(HALVES):
                            for hd in range(heads):
                                at = (g * heads + hd) * THIRD
                                mm = pe.transpose(t_ps[0:THIRD, at:at + THIRD], prob[u][:, g, hd, :],
                                                  tower.ident[0:THIRD, 0:THIRD])
                        mm.then_inc(turned.sem, 1)
                    for u in two:
                        pe.wait_ge(turned_read.sem, turned_read.at(2 * i + u + 1))
                        pe.wait_ge(v_read.sem, v_read.at(6 * i + 3 * u + 3))
                        pe.wait_ge(o_read.sem, o_read.at(2 * i + u))
                        pe.matmul(o_ps[:, 0:2], tower.ident[:], tower.ident[:, 0:2], start=True, stop=True)
                        for g in range(HALVES):
                            for c in range(SLICES):
                                for hd in range(heads):
                                    at = c * SEQ + hd * THIRD
                                    mm = pe.matmul(o_ps[half(g), at:at + THIRD], v_s[u][:, hd, c, half(g)],
                                                   prob_t[u][:, g, hd, :], start=True, stop=True)
                        mm.then_inc(o_made.sem, 1)
                    for u in two:
                        pe.wait_ge(o_read.sem, o_read.at(2 * i + u + 1))
                        for c in range(SLICES):
                            mm = pe.matmul(s_ps[u][:, 0:SEQ], wo[:, c, :], o_s[u][:, c, :],
                                           start=c == 0, stop=c == SLICES - 1)
                        mm.then_inc(y_made.sem, 1)

            @block.scalar
            def _(act):
                with act.Fori(0, n2) as i:
                    for u in two:
                        act.wait_ge(s_read.sem, s_read.at(4 * i + 2 * u + 2))
                        act.activation(prob[u][:], prob[u][:], ACT.Exp, scale=D ** -0.5).then_inc(exped.sem, 1)
                    for u in two:
                        act.wait_ge(turned.sem, turned.at(2 * i + u + 1))
                        act.activation(prob_t[u][:], t_ps[0:THIRD, 0:6 * THIRD]
                                       .rearrange("p (g h n) -> p g h n", g=2, h=heads),
                                       ACT.Copy).then_inc(turned_read.sem, 1)
                    for u in two:
                        act.wait_ge(o_made.sem, o_made.at(2 * i + u + 1))
                        act.activation(o_s[u][:], o_ps[:, 0:SLICES * SEQ].rearrange("p (c n) -> p c n", c=SLICES),
                                       ACT.Copy).then_inc(o_read.sem, 1)

            @block.vector
            def _(dve):
                dve.wait_ge(loaded.sem, loaded.at(64))
                with dve.Fori(0, n2) as i:
                    for u in two:
                        for hd in range(heads):
                            n = 3 * u + hd
                            dve.wait_ge(e_made.sem, e_made.at(6 * i + n + 1))
                            dve.tensor_tensor(e_s[u][:, hd, :, :],
                                              e_ps[n % 2][:, 0:SLICES * qk].rearrange("p (c n) -> p c n", c=SLICES),
                                              be[:, hd, :][:, :, None].to_broadcast([P, SLICES, qk]),
                                              ALU.add).then_inc(e_read.sem, 1)
                    for u in two:
                        for g in range(HALVES):
                            step = 4 * i + 2 * u + g
                            s = s_ps[g][0:THIRD, 0:heads * THIRD].rearrange("p (h n) -> p h n", h=heads)
                            dve.wait_ge(s_made.sem, s_made.at(step + 1))
                            dve.tensor_reduce(peak[u][:, g, :], s, AX, ALU.max).then_inc(s_peaked.sem, 1)
                            dve.wait_ge(s_peaked.sem, s_peaked.at(step + 1))
                            dve.tensor_tensor(prob[u][:, g, :, :], s,
                                              peak[u][:, g, :][:, :, None].to_broadcast([THIRD, heads, THIRD]),
                                              ALU.subtract).then_inc(s_read.sem, 1)
                        for hd in range(heads):
                            n = 3 * u + hd
                            dve.wait_ge(v_made.sem, v_made.at(6 * i + n + 1))
                            dve.tensor_tensor(v_s[u][:, hd, :, :].rearrange("p c n -> p (c n)"),
                                              v_ps[n % 2][0:THIRD, 0:SLICES * P], bv[:, hd, :],
                                              ALU.add).then_inc(v_read.sem, 1)
                    for u in two:
                        step = 2 * i + u + 1
                        dve.wait_ge(exped.sem, exped.at(step))
                        dve.tensor_reduce(total[u][:], prob[u][:], AX, ALU.add).then_inc(summed.sem, 1)
                        dve.wait_ge(summed.sem, summed.at(step))
                        dve.reciprocal(total[u][:], total[u][:]).then_inc(inverted.sem, 1)
                        dve.wait_ge(inverted.sem, inverted.at(step))
                        flat = prob[u][:].rearrange("p g h n -> p (g h) n")
                        dve.tensor_tensor(flat, flat, total[u][:].rearrange("p g h -> p (g h)")[:, :, None]
                                          .to_broadcast([THIRD, 6, THIRD]), ALU.mult).then_inc(prob_ready.sem, 1)
                    for u in two:
                        dve.wait_ge(y_made.sem, y_made.at(2 * i + u + 1))
                        dve.scalar_tensor_tensor(h[:, cols(i, u)], s_ps[u][:, 0:SEQ], column("L0_b_out"),
                                                 h[:, cols(i, u)], ALU.add, ALU.add).then_inc(y_read.sem, 1)


def head_columns(w, head_rows, rows_of):
    out = np.zeros((D, D), np.float32)
    out[:, rows_of] = w[head_rows].T
    return out


def lay_out_attention(a, name, wq, wk, wv, wo, q_at, kv_rows, swap, width):
    heads = len(q_at)
    q = np.zeros((D, heads, D), np.float32)
    o = np.zeros((D, heads, D), np.float32)
    for h, at in enumerate(q_at):
        q[:, h, at] = wq[h * width:(h + 1) * width].T
        o[at, h] = wo[:, h * width:(h + 1) * width].T
    k, v = np.zeros((D, D), np.float32), np.zeros((D, D), np.float32)
    k[:, :kv_rows], v[:, :kv_rows] = wk.T, wv.T
    stack = lambda w: np.stack([diag(w[:, h]) for h in range(heads)], 1)
    a[f"{name}_wq"], a[f"{name}_wk"], a[f"{name}_wo"] = stack(q), diag(k), stack(o)
    a[f"{name}_wv"] = diag(v)
    if swap is not None:
        a[f"{name}_wq_turned"], a[f"{name}_wk_turned"] = stack(q[:, :, swap]), diag(k[:, swap])


def lay_out_network(a, name, w1, b1, w2):
    parts = w1.shape[1] // P
    up, down = np.zeros((P, HALVES, parts, P), np.float32), np.zeros((P, HALVES, parts, P), np.float32)
    bias = np.zeros((P, HALVES, parts), np.float32)
    for g in range(HALVES):
        for k in range(parts):
            at = slice(k * P, (k + 1) * P)
            up[D * g:D * g + D, g, k] = w1[:, at]
            down[:, g, k] = into_half(w2[at], g)
            bias[:, g, k] = b1[at]
    a[f"{name}_up"], a[f"{name}_down"] = up.reshape(P, -1, P), down.reshape(P, -1, P)
    a[f"{name}_up_b"] = bias.reshape(P, -1)


def lay_out_layers(a, t, f):
    two = lambda v: np.concatenate([v, v])
    pos = np.arange(SEQ, dtype=np.float32)[:, None]
    div = np.exp(np.arange(0, D, 2, dtype=np.float32) * np.float32(-np.log(10000.0) / D)).astype(np.float32)
    pe = np.zeros((SEQ, D), np.float32)
    pe[:, 0::2], pe[:, 1::2] = np.sin(pos * div), np.cos(pos * div)
    a["L1_pos"] = two(pe.T)
    a["L1_blocks"] = np.kron(np.eye(16), np.ones((8, 8))) * 8 ** -0.5
    for l in range(4):
        for n in "qkvo":
            a[f"L1_w{n}{l}"] = diag(f(f"L1_attn_W{n}")[l])
        lay_out_network(a, "L1l", f("L1_attn_W1")[l], f("L1_attn_bf1")[l], f("L1_attn_W2")[l])
        for n in ("up", "down", "up_b"):
            a[f"L1_{n}{l}"] = a.pop(f"L1l_{n}")
    a["L1f_wr"] = diag(f("L1_ffn_wr"))
    a["L1f_br"] = two(f("L1_ffn_br"))[:, None]
    lay_out_network(a, "L1f", f("L1_ffn_w1"), f("L1_ffn_b1"), f("L1_ffn_w2"))
    q_at = [np.arange(16 * h, 16 * h + 16) for h in range(4)]
    lay_out_attention(a, "L2a", f("L2_attn_Wq"), f("L2_attn_Wk"), f("L2_attn_Wv"), f("L2_attn_Wo"),
                      q_at, D, None, 16)
    bias = np.zeros((D, 6), np.float32)
    bias[:, 0] = f("L2_attn_bk")
    for h in range(4):
        bias[q_at[h], 1 + h] = f("L2_attn_bq")[q_at[h]]
    bias[:, 5] = f("L2_attn_bv")
    a["L2a_bias"] = two(bias)
    q_at = [np.arange(16 * (h // 2), 16 * (h // 2) + 16) for h in range(4)]
    row = np.arange(D)
    swap = row // 16 * 16 + (row % 16 + 8) % 16
    lay_out_attention(a, "L2f", f("L2_ffn_wq"), f("L2_ffn_wk"), f("L2_ffn_wv"), f("L2_ffn_wo"),
                      q_at, 32, swap, 16)
    freq = (1.0 / 10000.0 ** (np.arange(0, 16, 2, dtype=np.float32) / 16)).astype(np.float32)
    angle = np.outer(np.tile(freq, 8), np.arange(SEQ, dtype=np.float32))
    sign = np.where(row % 16 < 8, -1.0, 1.0)[:, None]
    a["L2f_cos"], a["L2f_sin"] = two(np.cos(angle)), two(sign * np.sin(angle))
    wkv = f("L3_attn_wkv")
    lay_out_attention(a, "L3a", f("L3_attn_wq"), wkv[:D], wkv[D:], f("L3_attn_wo"),
                      [row] * 16, D, row ^ 1, D)
    freq = 10000.0 ** (-2.0 * np.arange(32, dtype=np.float32) / D)
    angle = np.outer(np.repeat(freq, 2), np.arange(SEQ, dtype=np.float32))
    sign = np.where(row % 2 == 0, -1.0, 1.0)[:, None]
    a["L3a_cos"], a["L3a_sin"] = two(np.cos(angle)), two(sign * np.sin(angle))
    a["L3a_norm_w"] = two(np.stack([f("L3_attn_k_norm_w"), f("L3_attn_q_norm_w")], 1))
    w1, w3, w2 = f("L2_ffn_w1"), f("L2_ffn_w3"), f("L2_ffn_w2")
    ups = [np.zeros((P, EXPERTS, SLABS * SLAB), np.float32) for _ in range(2)]
    down = np.zeros((EXPERTS, SLABS * SLAB, P), np.float32)
    for g in range(HALVES):
        at = slice(HIDDEN * g, HIDDEN * (g + 1))
        for up, w in zip(ups, (w1, w3)):
            up[D * g:D * (g + 1), :, at] = w.transpose(2, 0, 1)
        down[:, at, D * g:D * (g + 1)] = w2.transpose(0, 2, 1)
    a["L2m_w1"], a["L2m_w3"] = [up.reshape(P, EXPERTS * SLABS, SLAB) for up in ups]
    a["L2m_w2"] = down.reshape(EXPERTS * SLABS, SLAB, P).transpose(1, 0, 2)
    pick = np.zeros((P, EXPERTS, P))
    for g in range(HALVES):
        for e in range(EXPERTS):
            pick[32 * g + e, e, D * g:D * (g + 1)] = 1.0
    a["L2m_pick"] = pick
    pick = np.zeros((D, 2, HALVES))
    for g in range(HALVES):
        pick[32 * g:32 * g + 8, 0, g] = 1.0
        pick[32 * g + 8:32 * g + 16, 1, g] = 1.0
    a["L3_pick"] = pick
    tap = lambda w: f(w).transpose(1, 2, 3, 0).reshape(P, -1, f(w).shape[0])
    a["tok_c1w"], a["tok_c2w"] = tap("L0_tok_conv1_w"), tap("L0_tok_conv2_w")
    a["tok_c3w"] = tap("L0_tok_conv3_w").reshape(P, 10, 2, P)
    a["tok_ow"] = np.stack([into_half(f("L0_tok_out_w"), g) for g in range(HALVES)], 1)
    for n in range(2):
        both = np.stack([f(f"L0_tok_ln{n}_g"), f(f"L0_tok_ln{n}_b")])
        a[f"tok_ln{n}"] = np.broadcast_to(both, (P,) + both.shape)
    a["tok_x"] = f("x").reshape(HALVES, PAIRS, P, 192).transpose(1, 2, 0, 3)
    we, be = f("L0_attn_W_embed"), f("L0_attn_b_embed")
    a["L0_we"] = np.stack([np.stack([diag(we[n, D * c:D * c + D].T) for c in range(3)], 1) for n in range(3)], 1)
    cut = be.reshape(3, 3, D)
    a["L0_be"] = np.concatenate([cut, cut], 2).transpose(2, 0, 1)
    a["L0_bv"] = np.broadcast_to(np.concatenate([cut, cut], 2).reshape(3, 3 * P), (SEQ // 3, 3, 3 * P))
    a["L0_wo"] = np.stack([diag(f("L0_attn_W_out")[:, D * c:D * c + D].T) for c in range(3)], 1)



SEMAPHORES = 64


def tower_program(nc, dram, out, stages):
    with ExitStack() as stack:
        handles = [nc.alloc_semaphore(name=f"signal{n}") for n in range(SEMAPHORES)]
        tower = Tower(nc, dram, handles)

        def keep(name, shape, dtype=F32):
            return stack.enter_context(nc.sbuf_tensor(name, shape, dtype))

        h = keep("h", [P, COLS])
        xn = keep("xn", [P, COLS])
        tower.ident, tower.center, tower.average = [keep(n, [P, P]) for n in ("ident", "center", "average")]
        tower.rank8 = keep("rank8", [P, EXPERTS])
        tower.head_blocks = keep("head_blocks", [P, P])
        tower.spread2 = keep("spread2", [HALVES, P])
        tower.later = keep("later", [P, SEQ], BF16)
        tower.place = keep("place", [P, SEQ + P], BF16)
        tower.ones2 = keep("ones2", [2, P], BF16)
        wide_later, wide_place = keep("wide_later", [P, SEQ]), keep("wide_place", [P, SEQ + P])
        columns = keep("columns", [P, len(COLUMNS)])
        eps_cols = keep("eps_cols", [P, 3])
        tower.eps = {1e-5: eps_cols[:, 0:1], 1e-6: eps_cols[:, 1:2], 1.1920929e-07: eps_cols[:, 2:3]}

        def column(name):
            n = COLUMNS.index(name)
            return columns[:, n:n + 1]

        loaded = nc.alloc_semaphore(name="constants_loaded")
        stored = nc.alloc_semaphore(name="output_stored")
        with nc.Block() as block:
            @block.sync
            def _(sp):
                consts = [(tower.ident, "ident"), (tower.center, "center"), (tower.average, "average"),
                          (tower.rank8, "rank8"), (columns, "columns"),
                          (tower.spread2, "spread2"), (wide_later, "later"), (wide_place, "place")]
                if "h_in" in dram:
                    consts.append((h, "h_in"))
                for buf, name in consts:
                    sp.dma_start(buf[:], dram[name]).then_inc(loaded, 16)
                for s in handles:
                    sp.sem_inc(s, CREDIT)
                sp.wait_ge(loaded, 16 * len(consts))

            @block.gpsimd
            def _(pool):
                pool.memset(tower.ones2[:], 1.0)
                for n, eps in enumerate((1e-5, 1e-6, 1.1920929e-07)):
                    pool.memset(eps_cols[:, n:n + 1], eps)

        with nc.Block() as block:
            @block.vector
            def _(dve):
                dve.tensor_copy(tower.later[:], wide_later[:])
                dve.tensor_copy(tower.place[:], wide_place[:])

        if "L0_tok" in stages:
            tokenizer_phase(tower, h, column)
        if "L0_attn" in stages:
            norm_phase(tower, h, xn, 1e-5)
            thirds_attention_phase(tower, h, xn, column)
        if "L0_ffn" in stages:
            norm_phase(tower, h, xn, 1e-5)
            with ExitStack() as moe:
                rows_t = moe.enter_context(nc.sbuf_tensor("marks0", [64, COLS], F32))
                aug = [moe.enter_context(nc.sbuf_tensor(f"aug0{g}", [104, COLS], F32)) for g in range(HALVES)]
                gate_phase(tower, xn, "L0_gate_w", "L0_gate_b", 2, False, rows_t)
                spread_phase(tower, xn, rows_t, aug)
                mlp_phase(tower, "L0_up", "L0_down", "L0_up_b", 2 * EXPERTS, ACT.Gelu, 72,
                          lambda b: aug[b % 2], AddTo(h), None, extra=("L0_down_b", 104, aug),
                          up_of=lambda b: b // HALVES)
        if "L1_attn" in stages:
            norm_phase(tower, h, xn, 1e-5)
            linear_tower(tower, nc, h, xn, column)
        if "L1_ffn" in stages:
            norm_phase(tower, h, xn, 1e-5)
            half_ffn(tower, nc, h, xn, column)
        if "L2_attn" in stages:
            norm_phase(tower, h, xn, 1e-5)
            with nc.Block() as block:
                @block.vector
                def _(dve):
                    dve.tensor_scalar(xn[:], xn[:], -10000.0, 10000.0, ALU.max, ALU.min)
            attention_phase(tower, xn, h, ATTENTION["L2a"], column("L2_bo"))
        if "L2_ffn" in stages:
            norm_phase(tower, h, xn, 1e-5)
            routed_block(tower, nc, h, xn, column)
        if "L3_attn" in stages:
            norm_phase(tower, h, xn, 1e-5)
            attention_phase(tower, xn, h, ATTENTION["L3a"])
        if "L3_ffn" in stages:
            norm_phase(tower, h, xn, 1e-5)
            capacity_ffn(tower, nc, h, xn)
        with nc.Block() as block:
            @block.sync
            def _(sp):
                sp.dma_start(out, h[:]).then_inc(stored, 16)
                sp.wait_ge(stored, 16)



COLUMNS = ["cls", "tok_out_b", "L0_b_out"] + \
    [f"L1_{n}{l}" for l in range(4) for n in ("bo", "g1", "b1", "bf2", "g2", "b2")] + \
    ["L1f_b2", "L2_bo", "L2_ln1", "L2_ln2", "tok_c1b", "tok_c2b", "tok_c3b0", "tok_c3b1"]


def diag(w):
    k, m = w.shape
    out = np.zeros((2 * k, 2 * m), np.float32)
    out[:k, :m], out[k:, m:] = w, w
    return out


def into_half(w, g):
    out = np.zeros((w.shape[0], P), np.float32)
    out[:, D * g:D * g + D] = w
    return out


def lay_out(t):
    f = lambda name: np.asarray(t[name])
    two = lambda v: np.concatenate([v, v])
    a = {}
    same = np.kron(np.eye(2), np.ones((D, D))) / D
    a["ident"], a["center"], a["average"] = np.eye(P), np.eye(P) - same, same
    a["spread2"] = np.kron(np.eye(2), np.ones((1, D)))
    a["later"] = np.where(np.arange(SEQ)[None, :] > np.arange(P)[:, None], float(-BIG), 0.0)
    a["place"] = (np.arange(SEQ + P)[None, :] % SEQ == np.arange(P)[:, None]).astype(np.float64)
    a["rank8"] = np.broadcast_to(8.0 - np.arange(8), (P, 8))
    col = {"cls": two(f("cls_tok").reshape(D)), "tok_out_b": two(f("L0_tok_out_b")),
           "L0_b_out": two(f("L0_attn_b_out")), "L1f_b2": two(f("L1_ffn_b2")), "L2_bo": two(f("L2_attn_bo")),
           "L2_ln1": two(f("L2_ffn_ln1_w")), "L2_ln2": two(f("L2_ffn_ln2_w")),
           "tok_c1b": f("L0_tok_conv1_b"), "tok_c2b": f("L0_tok_conv2_b"),
           "tok_c3b0": f("L0_tok_conv3_b")[:P], "tok_c3b1": f("L0_tok_conv3_b")[P:]}
    for l in range(4):
        for n in ("bo", "g1", "b1", "bf2", "g2", "b2"):
            col[f"L1_{n}{l}"] = two(f(f"L1_attn_{n}")[l])
    a["columns"] = np.stack([col[n] for n in COLUMNS], 1)

    for p, w, b in (("L0", f("L0_ffn_Wg"), f("L0_ffn_bg")), ("L2", f("L2_ffn_router_w").T, np.zeros(8)),
                    ("L3", f("L3_ffn_gate_w"), f("L3_ffn_gate_b"))):
        a[f"{p}_gate_w"], a[f"{p}_gate_b"] = diag(w), np.broadcast_to(two(b), (CHUNK, 16))

    for p, w1, b1, w2, b2 in (("L0", "L0_ffn_W1", "L0_ffn_b1", "L0_ffn_W2", "L0_ffn_b2"),
                              ("L3", "L3_ffn_w1", "L3_ffn_b1", "L3_ffn_w2", "L3_ffn_b2")):
        w1, b1, w2, b2 = f(w1), f(b1), f(w2), f(b2)
        parts = w1.shape[2] // P
        up = np.zeros((72, EXPERTS * parts, P), np.float32)
        down = np.zeros((P, EXPERTS * parts, HALVES, P), np.float32)
        for e in range(EXPERTS):
            for k in range(parts):
                n = e * parts + k
                up[0:D, n] = w1[e][:, k * P:(k + 1) * P]
                up[D + e, n] = BIG
                for g in range(HALVES):
                    down[:, n, g] = into_half(w2[e][k * P:(k + 1) * P], g)
        a[f"{p}_up"] = up
        a[f"{p}_down"] = down.reshape(P, -1, P)
        a[f"{p}_up_b"] = b1.reshape(EXPERTS * parts, P).T
        extra = np.zeros((104, HALVES, P), np.float32)
        for g in range(HALVES):
            extra[96:104, g] = into_half(b2, g)
        a[f"{p}_down_b"] = extra
    lay_out_layers(a, t, f)
    return {n: np.ascontiguousarray(v.astype(np.float32) if v.dtype == np.float64 else v) for n, v in a.items()}


def kernel(**inputs):
    import concourse.bacc as _bacc
    from concourse.bass_utils import run_bass_kernel_spmd as _run
    nc = _bacc.Bacc("TRN2", target_bir_lowering=False, num_devices=1)
    arrays = {f"in_{n}": v for n, v in lay_out(inputs).items()}
    dram = {n[3:]: nc.dram_tensor(n, v.shape, mybir.dt.from_np(v.dtype), kind="ExternalInput").ap()
            for n, v in arrays.items()}
    out = nc.dram_tensor("out_0", (P, COLS), F32, kind="ExternalOutput").ap()
    tower_program(nc, dram, out, STAGES)
    got = np.asarray(_run(nc, [arrays], core_ids=[0]).results[0]["out_0"])
    return got.reshape(HALVES, D, PAIRS, SEQ).transpose(0, 2, 3, 1).reshape(HALVES * PAIRS, SEQ, D)


STAGES = ["L0_tok", "L0_attn", "L0_ffn", "L1_attn", "L1_ffn", "L2_attn", "L2_ffn", "L3_attn", "L3_ffn"]
```

```python
from contextlib import ExitStack, contextmanager

import numpy as np

import concourse.bass as bass
from concourse import mybir

F32 = mybir.dt.float32
BF16 = mybir.dt.bfloat16
ALU = mybir.AluOpType
ACT = mybir.ActivationFunctionType
AX = mybir.AxisListType.X

P = 128
D = 64
HALVES = 2
PAIRS = 32
SEQ = 129
COLS = PAIRS * SEQ
TILE = 344
TILES = COLS // TILE
CHUNK = 96
CHUNKS = COLS // CHUNK
EXPERTS = 8
BANK = 512
CREDIT = 8
BIG = 1.0e30


class Signal:

    def __init__(self, handle):
        self.sem, self.base, self.total = handle, CREDIT, 0

    def at(self, k):
        return k + self.base


class Tower:

    def __init__(self, nc, dram, free_handles):
        self.nc, self.dram = nc, dram
        self.free = [Signal(handle) for handle in free_handles]
        self.phases = 0


class Phase:

    def __init__(self, tower, stack):
        self.tower, self.nc, self.stack = tower, tower.nc, stack
        self.tag = f"p{tower.phases}"
        self.used = []
        tower.phases += 1

    def sb(self, name, shape, dtype=F32):
        return self.stack.enter_context(self.nc.sbuf_tensor(f"{self.tag}_{name}", shape, dtype))

    def ps(self, name, shape=(P, BANK), dtype=F32):
        return self.stack.enter_context(self.nc.psum_tensor(f"{self.tag}_{name}_ps", list(shape), dtype))

    def counts(self, total):
        s = self.tower.free.pop(0)
        s.total = total
        self.used.append(s)
        return s


@contextmanager
def phase(tower):
    with ExitStack() as stack:
        ph = Phase(tower, stack)
        yield ph
    for s in ph.used:
        s.base += s.total
        tower.free.append(s)



def norm_phase(tower, src, dst, eps, center=True, gamma=None, beta=None):
    nc, n2 = tower.nc, TILES // 2
    with phase(tower) as ph:
        centered_ps = [ph.ps(f"centered{u}") for u in range(2)]
        var_ps = [ph.ps(f"var{u}") for u in range(2)]
        square = [ph.sb(f"square{u}", [P, TILE]) for u in range(2)]
        rstd = [ph.sb(f"rstd{u}", [P, TILE]) for u in range(2)]
        centered = [ph.counts(n2) for _ in range(2)]
        squared = [ph.counts(n2) for _ in range(2)]
        var_ready = [ph.counts(n2) for _ in range(2)]
        logged = [ph.counts(n2) for _ in range(2)]
        rstd_ready = [ph.counts(n2) for _ in range(2)]
        scaled = [ph.counts(n2) for _ in range(2)]
        written = [ph.counts(n2) for _ in range(2)]
        affine = gamma is not None
        eps_col = tower.eps[eps]

        def cols(i, u):
            return bass.ds((2 * i + u) * TILE, TILE)

        with nc.Block() as block:
            @block.tensor
            def _(pe):
                with pe.Fori(0, n2) as i:
                    if center:
                        for u in range(2):
                            pe.wait_ge(scaled[u].sem, scaled[u].at(i))
                            pe.matmul(centered_ps[u][:, 0:TILE], tower.center[:], src[:, cols(i, u)],
                                      start=True, stop=True).then_inc(centered[u].sem, 1)
                    for u in range(2):
                        pe.wait_ge(squared[u].sem, squared[u].at(i + 1))
                        pe.wait_ge(logged[u].sem, logged[u].at(i))
                        pe.matmul(var_ps[u][:, 0:TILE], tower.average[:], square[u][:],
                                  start=True, stop=True).then_inc(var_ready[u].sem, 1)

            @block.scalar
            def _(act):
                act.preload_act_table_set("natural_log_exp_and_others")
                with act.Fori(0, n2) as i:
                    for u in range(2):
                        act.wait_ge(var_ready[u].sem, var_ready[u].at(i))
                        if center:
                            act.wait_ge(centered[u].sem, centered[u].at(i + 1))
                            act.activation(square[u][:], centered_ps[u][:, 0:TILE],
                                           ACT.Square).then_inc(squared[u].sem, 1)
                        else:
                            act.activation(square[u][:], src[:, cols(i, u)],
                                           ACT.Square).then_inc(squared[u].sem, 1)
                    for u in range(2):
                        act.wait_ge(var_ready[u].sem, var_ready[u].at(i + 1))
                        act.wait_ge(scaled[u].sem, scaled[u].at(i))
                        act.activation(rstd[u][:], var_ps[u][:, 0:TILE], ACT.Ln,
                                       bias=eps_col).then_inc(logged[u].sem, 1)
                    for u in range(2):
                        act.wait_ge(logged[u].sem, logged[u].at(i + 1))
                        act.activation(rstd[u][:], rstd[u][:], ACT.Exp,
                                       scale=-0.5).then_inc(rstd_ready[u].sem, 1)

            @block.vector
            def _(dve):
                with dve.Fori(0, n2) as i:
                    for u in range(2):
                        dve.wait_ge(rstd_ready[u].sem, rstd_ready[u].at(i + 1))
                        x = centered_ps[u][:, 0:TILE] if center else src[:, cols(i, u)]
                        dve.tensor_tensor(dst[:, cols(i, u)], x, rstd[u][:],
                                          ALU.mult).then_inc(scaled[u].sem, 1)
                    for u in range(2 if affine else 0):
                        dve.wait_ge(scaled[u].sem, scaled[u].at(i + 1))
                        if beta is None:
                            dve.tensor_scalar(dst[:, cols(i, u)], dst[:, cols(i, u)], gamma, None,
                                              ALU.mult).then_inc(written[u].sem, 1)
                        else:
                            dve.tensor_scalar(dst[:, cols(i, u)], dst[:, cols(i, u)], gamma, beta,
                                              ALU.mult, ALU.add).then_inc(written[u].sem, 1)
        if not affine:
            for s in written:
                s.total = 0
        if not center:
            for s in centered:
                s.total = 0



def gate_phase(tower, x, gate_w, gate_b, top, weighted, rows_t):
    nc = tower.nc
    per_bank = BANK // (HALVES * EXPERTS)
    groups = [(c, min(5, CHUNKS - c)) for c in range(0, CHUNKS, 5)]
    with phase(tower) as ph:
        gw = ph.sb("gate_w", [P, HALVES * EXPERTS])
        gb = ph.sb("gate_b", [CHUNK, HALVES * EXPERTS])
        logit_ps = [ph.ps(f"logit{u}") for u in range(2)]
        turn_ps = [ph.ps(f"turn{u}", (64, BANK)) for u in range(4)]
        shape = [CHUNK, CHUNKS, HALVES, EXPERTS]
        logit = ph.sb("logit", shape)
        eq = ph.sb("eq", shape)
        mark = ph.sb("mark", shape)
        second = ph.sb("second", shape)
        e_x = ph.sb("e_x", shape)
        best = ph.sb("best", [CHUNK, CHUNKS * HALVES])
        place = ph.sb("place", [CHUNK, CHUNKS * HALVES])
        total = ph.sb("total", [CHUNK, CHUNKS * HALVES])
        wide = ph.sb("wide", [CHUNK, CHUNKS, HALVES, 32])
        loaded = ph.counts(32)
        logits = ph.counts(1)
        v = ph.counts(0)
        exped = ph.counts(1)
        cleared = ph.counts(1)
        marked = ph.counts(1)
        turned = ph.counts(len(groups))
        copied = ph.counts(len(groups))

        def flat(t):
            return t[:].rearrange("p c g e -> p (c g) e")

        def wide_to(t):
            return t[:, :, None].to_broadcast([CHUNK, CHUNKS * HALVES, EXPERTS])

        rank = tower.rank8[0:CHUNK, :]
        rank_all = rank[:, None, :].to_broadcast([CHUNK, CHUNKS * HALVES, EXPERTS])
        with nc.Block() as block:
            @block.sync
            def _(sp):
                sp.dma_start(gw[:], tower.dram[gate_w]).then_inc(loaded.sem, 16)
                sp.dma_start(gb[:], tower.dram[gate_b]).then_inc(loaded.sem, 16)

            @block.gpsimd
            def _(pool):
                pool.memset(wide[:], 0.0).then_inc(cleared.sem, 1)

            @block.tensor
            def _(pe):
                pe.wait_ge(loaded.sem, loaded.at(32))
                for c in range(CHUNKS):
                    at = (c % per_bank) * HALVES * EXPERTS
                    mm = pe.matmul(logit_ps[c // per_bank][0:CHUNK, at:at + HALVES * EXPERTS],
                                   x[:, c * CHUNK:(c + 1) * CHUNK], gw[:], start=True, stop=True)
                mm.then_inc(logits.sem, 1)
                pe.wait_ge(marked.sem, marked.at(1))
                for n, (c0, k) in enumerate(groups):
                    pe.wait_ge(copied.sem, copied.at(n - 3))
                    for c in range(c0, c0 + k):
                        at = (c - c0) * CHUNK
                        mm = pe.transpose(turn_ps[n % 4][0:64, at:at + CHUNK],
                                          wide[:, c, :, :].rearrange("p g e -> p (g e)"),
                                          tower.ident[0:CHUNK, 0:CHUNK])
                    mm.then_inc(turned.sem, 1)

            @block.scalar
            def _(act):
                if top == 1 or weighted:
                    act.wait_ge(v.sem, v.at(5))
                    act.activation(e_x[:], e_x[:], ACT.Exp).then_inc(exped.sem, 1)
                for n, (c0, k) in enumerate(groups):
                    act.wait_ge(turned.sem, turned.at(n + 1))
                    act.activation(rows_t[0:64, c0 * CHUNK:(c0 + k) * CHUNK], turn_ps[n % 4][0:64, 0:k * CHUNK],
                                   ACT.Copy).then_inc(copied.sem, 1)

            @block.vector
            def _(dve):
                done = [0]

                def step(ins):
                    done[0] += 1
                    ins.then_inc(v.sem, 1)
                    dve.wait_ge(v.sem, v.at(done[0]))

                if rows_t.shape[0] > 64:
                    dve.memset(rows_t[64:P, :], 0.0)
                dve.wait_ge(logits.sem, logits.at(1))
                for k in range(2):
                    n = min(per_bank, CHUNKS - k * per_bank)
                    step(dve.tensor_tensor(
                        logit[:, k * per_bank:k * per_bank + n, :, :].rearrange("p c g e -> p c (g e)"),
                        logit_ps[k][0:CHUNK, 0:n * 16].rearrange("p (c e) -> p c e", e=16),
                        gb[:, None, :].to_broadcast([CHUNK, n, 16]), ALU.add))

                def mark_first(out, values):
                    step(dve.tensor_reduce(best[:], flat(values), AX, ALU.max))
                    step(dve.tensor_tensor(flat(eq), flat(values), wide_to(best), ALU.is_equal))
                    if values is logit:
                        step(dve.tensor_tensor(flat(e_x), flat(values), wide_to(best), ALU.subtract))
                    step(dve.tensor_tensor(flat(eq), flat(eq), rank_all, ALU.mult))
                    step(dve.tensor_reduce(place[:], flat(eq), AX, ALU.max))
                    step(dve.tensor_tensor(flat(out), rank_all, wide_to(place), ALU.is_equal))

                mark_first(mark, logit)
                if top == 2:
                    step(dve.scalar_tensor_tensor(second[:], mark[:], -BIG, logit[:], ALU.mult, ALU.add))
                    mark_first(logit, second)
                    step(dve.tensor_tensor(mark[:], mark[:], logit[:], ALU.add))
                dve.wait_ge(cleared.sem, cleared.at(1))
                if weighted:
                    dve.wait_ge(exped.sem, exped.at(1))
                    for eps in (0.0, 1e-9):
                        step(dve.tensor_reduce(total[:], flat(e_x), AX, ALU.add))
                        step(dve.tensor_scalar(total[:], total[:], eps, None, ALU.add))
                        step(dve.reciprocal(total[:], total[:]))
                        if eps:
                            last = dve.tensor_tensor(wide[:, :, :, 0:8].rearrange("p c g e -> p (c g) e"),
                                                     flat(e_x), wide_to(total), ALU.mult)
                        else:
                            step(dve.tensor_tensor(flat(e_x), flat(e_x), wide_to(total), ALU.mult))
                            step(dve.tensor_tensor(e_x[:], e_x[:], mark[:], ALU.mult))
                    last.then_inc(marked.sem, 1)
                else:
                    if top == 1:
                        dve.wait_ge(exped.sem, exped.at(1))
                        step(dve.tensor_reduce(total[:], flat(e_x), AX, ALU.add))
                        step(dve.reciprocal(total[:], total[:]))
                        step(dve.tensor_tensor(wide[:, :, :, 8:16].rearrange("p c g e -> p (c g) e"),
                                               flat(mark), wide_to(total), ALU.mult))
                    dve.tensor_copy(wide[:, :, :, 0:8].rearrange("p c g e -> p (c g) e"),
                                    flat(mark)).then_inc(marked.sem, 1)
                v.total = done[0]
        if not (top == 1 or weighted):
            exped.total = 0


def spread_phase(tower, x, rows_t, aug):
    nc = tower.nc
    with phase(tower) as ph:
        cleared = ph.counts(1)
        with nc.Block() as block:
            @block.gpsimd
            def _(pool):
                pool.memset(aug[0][64:96, :], 0.0)
                pool.memset(aug[1][64:96, :], 0.0).then_inc(cleared.sem, 1)

            @block.scalar
            def _(act):
                for g in range(HALVES):
                    act.activation(aug[g][0:64, :], x[64 * g:64 * g + 64, :], ACT.Copy)

            @block.vector
            def _(dve):
                for g in range(HALVES):
                    dve.tensor_copy(aug[g][96:104, :], rows_t[32 * g:32 * g + 8, :])
                dve.wait_ge(cleared.sem, cleared.at(1))
                for g in range(HALVES):
                    dve.tensor_scalar(aug[g][64:72, :], rows_t[32 * g:32 * g + 8, :], -1.0, None, ALU.add)



def mlp_phase(tower, up, down, bias, blocks, func, rows, x_of, finish, load, extra=None,
              up_of=lambda b: b):
    nc, n2, ring = tower.nc, TILES // 2, 4
    lag = 2
    with phase(tower) as ph:
        n_up = tower.dram[up].shape[1]
        w_up = ph.sb("w_up", [rows, n_up, P])
        w_down = ph.sb("w_down", [P, blocks, P])
        b_up = ph.sb("b_up", [P, n_up])
        w_extra = ph.sb("w_extra", [extra[1], HALVES, P]) if extra else None
        hid_ps = [ph.ps(f"hid{r}") for r in range(ring)]
        y_ps = [ph.ps(f"y{u}") for u in range(2)]
        aux_ps = [ph.ps(f"aux{u}") for u in range(2)]
        hid = [ph.sb(f"hidden{r}", [P, TILE]) for r in range(ring)]
        n_load = 4 if extra else 3
        loaded = ph.counts(16 * n_load)
        up_done = ph.counts(2 * blocks * n2)
        act_done = ph.counts(2 * blocks * n2)
        down_done = ph.counts(2 * blocks * n2)
        y_done = [ph.counts(n2) for _ in range(2)]
        y_read = [ph.counts(n2) for _ in range(2)]
        per = 2 * blocks
        state = load(ph) if load else None
        aux_sb = [ph.sb(f"aux_sb{u}", [P, TILE]) for u in range(2)] if finish.broadcast else None
        aux_ready = [ph.counts(n2 if finish.broadcast else 0) for _ in range(2)]

        def cols(i, u):
            return bass.ds((2 * i + u) * TILE, TILE)

        with nc.Block() as block:
            @block.sync
            def _(sp):
                sp.dma_start(w_up[:], tower.dram[up]).then_inc(loaded.sem, 16)
                sp.dma_start(b_up[:], tower.dram[bias]).then_inc(loaded.sem, 16)
                sp.dma_start(w_down[:], tower.dram[down]).then_inc(loaded.sem, 16)
                if extra:
                    sp.dma_start(w_extra[:], tower.dram[extra[0]]).then_inc(loaded.sem, 16)

            @block.tensor
            def _(pe):
                pe.wait_ge(loaded.sem, loaded.at(16 * n_load))
                with pe.Fori(0, n2) as i:
                    for n in range(per + lag):
                        if n < per:
                            b, u = n % blocks, n // blocks
                            pe.wait_ge(act_done.sem, act_done.at(i * per + n - ring + 1))
                            pe.matmul(hid_ps[n % ring][:, 0:TILE], w_up[:, up_of(b), :],
                                      x_of(b)[0:rows, cols(i, u)],
                                      start=True, stop=True).then_inc(up_done.sem, 1)
                        if n >= lag:
                            m = n - lag
                            b, u = m % blocks, m // blocks
                            if b == 0:
                                pe.wait_ge(y_read[u].sem, y_read[u].at(i))
                            pe.wait_ge(act_done.sem, act_done.at(i * per + m + 1))
                            last = b == blocks - 1 and not extra
                            mm = pe.matmul(y_ps[u][:, 0:TILE], w_down[:, b, :], hid[m % ring][:],
                                           start=b == 0, stop=last)
                            mm.then_inc(down_done.sem, 1)
                            if b == blocks - 1:
                                if extra:
                                    for g in range(HALVES):
                                        mm = pe.matmul(y_ps[u][:, 0:TILE], w_extra[:, g, :],
                                                       extra[2][g][0:extra[1], cols(i, u)],
                                                       start=False, stop=g == 1)
                                if finish.broadcast:
                                    mm = finish.broadcast(pe, aux_ps[u], state, cols(i, u), u)
                                if extra or finish.broadcast:
                                    mm.then_inc(y_done[u].sem, 1)

            @block.scalar
            def _(act):
                act.wait_ge(loaded.sem, loaded.at(16 * n_load))
                with act.Fori(0, n2) as i:
                    for n in range(per):
                        act.wait_ge(up_done.sem, up_done.at(i * per + n + 1))
                        act.wait_ge(down_done.sem, down_done.at(i * per + n - ring + 1))
                        b = up_of(n % blocks)
                        act.activation(hid[n % ring][:], hid_ps[n % ring][:, 0:TILE], func,
                                       bias=b_up[:, b:b + 1]).then_inc(act_done.sem, 1)
                        if finish.broadcast and n % blocks == blocks - 1:
                            u = n // blocks
                            act.wait_ge(y_done[u].sem, y_done[u].at(i + 1))
                            act.wait_ge(y_read[u].sem, y_read[u].at(i))
                            act.activation(aux_sb[u][:], aux_ps[u][:, 0:TILE],
                                           ACT.Copy).then_inc(aux_ready[u].sem, 1)

            @block.vector
            def _(dve):
                with dve.Fori(0, n2) as i:
                    for u in range(2):
                        if extra or finish.broadcast:
                            dve.wait_ge(y_done[u].sem, y_done[u].at(i + 1))
                        else:
                            dve.wait_ge(down_done.sem, down_done.at(i * per + (u + 1) * blocks))
                        if finish.broadcast:
                            dve.wait_ge(aux_ready[u].sem, aux_ready[u].at(i + 1))
                        finish.vector(dve, y_ps[u][:, 0:TILE], aux_sb and aux_sb[u], state, cols(i, u), i, u).then_inc(
                            y_read[u].sem, 1)
        if not (extra or finish.broadcast):
            for s in y_done:
                s.total = 0


class AddTo:
    broadcast = None

    def __init__(self, acc, bias=None):
        self.acc, self.bias = acc, bias

    def vector(self, dve, y, aux, state, cols, i, u):
        if self.bias is None:
            return dve.tensor_tensor(self.acc[:, cols], y, self.acc[:, cols], ALU.add)
        return dve.scalar_tensor_tensor(self.acc[:, cols], y, self.bias, self.acc[:, cols], ALU.add, ALU.add)



class Attend:

    def __init__(self, name, heads, scale, causal=False, rope=False, norm=False, bias=False, bf16_out=False):
        self.name, self.heads, self.scale = name, heads, scale
        self.causal, self.rope, self.norm, self.bias, self.bf16_out = causal, rope, norm, bias, bf16_out


ATTENTION = {
    "L2a": Attend("L2a", heads=4, scale=16 ** -0.5, bias=True, bf16_out=True),
    "L2f": Attend("L2f", heads=4, scale=16 ** -0.5, causal=True, rope=True),
    "L3a": Attend("L3a", heads=16, scale=64 ** -0.5, causal=True, rope=True, norm=True),
}


RING = 4


def attention_phase(tower, src, acc, a, out_bias=None):
    nc = tower.nc
    seen = P if a.causal else SEQ
    per_bank = 4 if a.causal else 2
    banks = a.heads // per_bank
    quads = a.heads // 4
    tiles = a.heads + 1
    groups = a.heads + 1
    steps = quads + 1
    both = HALVES * steps
    at_once = not a.norm
    unroll = 4 if a.norm else 8
    with phase(tower) as ph:
        def w(name, shape, dtype=F32):
            buf = ph.sb(name, shape, dtype)
            loads.append((buf[:], f"{a.name}_{name}"))
            return buf

        loads = []
        wq, wk = w("wq", [P, a.heads, P]), w("wk", [P, P])
        wv, wo = w("wv", [P, P]), w("wo", [P, a.heads, P])
        if a.rope:
            wq_turned, wk_turned = w("wq_turned", [P, a.heads, P]), w("wk_turned", [P, P])
            cos_sin = ph.sb("cos_sin", [P, 2, SEQ])
            loads.append((cos_sin[:, 0, :], f"{a.name}_cos"))
            loads.append((cos_sin[:, 1, :], f"{a.name}_sin"))
        if a.norm:
            norm_w = w("norm_w", [P, 2])
        if a.bias:
            bias = w("bias", [P, a.heads + 2])
        if a.causal:
            later, place = tower.later, tower.place
        ones = tower.ones

        xs = ph.sb("xs", [P, SEQ])
        k_t = [[ph.sb(f"k_t{r}{g}", [P, SEQ]) for g in range(HALVES)] for r in range(2)]
        q_t = [ph.sb(f"q_t{r}", [P, a.heads, SEQ]) for r in range(2)]
        products = [ph.sb(f"products{r}", [P, 2, SEQ]) for r in range(2)]
        turned = [ph.sb(f"turned{r}", [P, SEQ]) for r in range(RING)]
        square = [ph.sb(f"square{r}", [P, SEQ]) for r in range(RING)]
        rstd = [ph.sb(f"rstd{r}", [P, SEQ]) for r in range(RING)]
        val = [ph.sb(f"val{g}", [P, P]) for g in range(HALVES)]
        val_last = [ph.sb(f"val_last{g}", [1, P]) for g in range(HALVES)]
        peak = ph.sb("peak", [P, HALVES, tiles])
        peak_t = [ph.sb(f"peak_t{g}", [tiles, 2, P], BF16) for g in range(HALVES)]
        peak_row = [ph.sb(f"peak_row{g}", [P, tiles * P], BF16) for g in range(HALVES)]
        prob = [ph.sb(f"prob{r}", [P, BANK]) for r in range(3)]
        prob_last = [ph.sb(f"prob_last{r}", [1, BANK]) for r in range(3)]
        inv = [ph.sb(f"inv{r}", [P, BANK]) for r in range(2)]
        mixed = ph.sb("mixed", [P, a.heads, SEQ])
        narrow = ph.sb("narrow", [P, BANK], BF16) if a.bf16_out else None
        raw = ph.sb("raw", [P, BANK]) if a.bf16_out else None

        b = [ph.ps(f"bank{n}") for n in range(8)]
        front_ps, score_ps = b[0:2], b[0:2]
        out_ps, st_ps = b[2:4], b[6:8]
        turn_ps = b[7]
        value_ps, avg_ps = b[4], b[4]
        last_ps = b[5]
        y_ps = b[6]

        made = PAIRS + 1
        per_half = banks + 1
        loaded = ph.counts(16 * len(loads))
        filled = ph.counts(4)
        copied = ph.counts(made)
        projected = ph.counts(made * groups)
        squared = ph.counts(made * groups * a.norm)
        averaged = ph.counts(made * groups * a.norm)
        logged = ph.counts(made * groups * a.norm)
        rstd_ready = ph.counts(made * groups * a.norm)
        multiplied = ph.counts(made * groups * a.rope)
        rotated = ph.counts(made * groups * a.norm)
        written = ph.counts(made * groups)
        values_made = ph.counts(PAIRS)
        values_ready = ph.counts(PAIRS)
        scored = ph.counts(PAIRS * HALVES * per_half)
        peaked = ph.counts(PAIRS * HALVES * per_half)
        peak_turned = ph.counts(PAIRS * HALVES)
        peak_high = ph.counts(PAIRS * HALVES)
        peak_split = ph.counts(PAIRS * HALVES)
        rows_landed = [ph.counts(PAIRS * 32) for _ in range(HALVES)]
        st_ready = ph.counts(PAIRS * both)
        exped = ph.counts(PAIRS * both)
        out_ready = ph.counts(PAIRS * both)
        sum_logged = ph.counts(PAIRS * both)
        inv_ready = ph.counts(PAIRS * both)
        rounding = ph.counts(PAIRS * both * 2 * a.bf16_out)
        out_read = ph.counts(PAIRS * both)
        y_ready = ph.counts(PAIRS)
        y_read = ph.counts(PAIRS)

        def half(g):
            return slice(D * g, D * g + D)

        def other(g):
            return half(1 - g)

        def heads_of(x):
            return slice(4 * x - 4, 4 * x)

        def queries(buf, x):
            return buf[:, heads_of(x), 0:P] if x else buf[:, :, P]

        def size(x):
            return BANK if x else a.heads

        def rows_of(x):
            return slice((x - 1) * BANK, x * BANK) if x else slice(a.heads * P, a.heads * P + a.heads)

        def shaped(ap, x):
            return ap.rearrange("p (h t) -> p h t", t=P) if x else ap

        def last_row(n):
            x = n % steps
            return last_ps[0:1, 0:BANK] if x else st_ps[n % 2][0:1, D:D + a.heads]

        def masked(x):
            return a.causal and x > 0

        def bank_of(r, h):
            return (r * groups + h) % 2

        def beside(n):
            if at_once:
                return [None, None]
            each = -(-groups // both)
            return [h if h < groups and k < each else None for k in range(2) for h in [n * each + k]]

        def waiting(n):
            return beside(n - 1)[1] if n else None

        with nc.Block() as block:
            @block.sync
            def _(sp):
                for buf, name in loads:
                    sp.dma_start(buf, tower.dram[name]).then_inc(loaded.sem, 16)
                with sp.Fori(0, PAIRS) as j:
                    for g in range(HALVES):
                        sp.wait_ge(peak_split.sem, peak_split.at(j * HALVES + g + 1))
                        for part in range(2):
                            sp.dma_start(peak_row[g][part:part + 1, :].rearrange("a (i r) -> a i r", r=P),
                                         peak_t[g][:, part, :]).then_inc(rows_landed[g].sem, 16)

            @block.gpsimd
            def _(pool):
                for g in range(HALVES):
                    pool.memset(val[g][:], 1.0)
                    pool.memset(val_last[g][:], 1.0).then_inc(filled.sem, 1)
                pool.memset(peak[:], 0.0).then_inc(filled.sem, 1)
                for g in range(HALVES):
                    ins = pool.memset(peak_row[g][:], 0.0)
                ins.then_inc(filled.sem, 1)
                with pool.Fori(0, PAIRS) as j:
                    pool.wait_ge(values_made.sem, values_made.at(j))
                    pool.tensor_copy(xs[:], src[:, bass.ds(j * SEQ, SEQ)]).then_inc(copied.sem, 1)
                pool.wait_ge(values_made.sem, values_made.at(PAIRS))
                pool.tensor_copy(xs[:], src[:, 0:SEQ]).then_inc(copied.sem, 1)

            @block.tensor
            def _(pe):
                pe.wait_ge(loaded.sem, loaded.at(16 * len(loads)))
                pe.wait_ge(filled.sem, filled.at(4))

                def project(j, r, h):
                    step, to = j * groups + h, front_ps[bank_of(r, h)]
                    if h == 0:
                        pe.wait_ge(copied.sem, copied.at(j + 1))
                        pe.wait_ge(peaked.sem, peaked.at(j * HALVES * per_half))
                    read = multiplied if a.rope else written
                    pe.wait_ge(read.sem, read.at(step - 1))
                    mm = pe.matmul(to[:, 0:SEQ], wq[:, h - 1, :] if h else wk[:], xs[:], start=True, stop=True)
                    if a.rope:
                        mm = pe.matmul(to[:, SEQ:2 * SEQ], wq_turned[:, h - 1, :] if h else wk_turned[:], xs[:],
                                       start=True, stop=True)
                    mm.then_inc(projected.sem, 1)

                def average(j, r, h):
                    if not a.norm:
                        return
                    step = j * groups + h
                    pe.wait_ge(squared.sem, squared.at(step + 1))
                    pe.wait_ge(logged.sem, logged.at(step))
                    pe.matmul(avg_ps[:, 0:SEQ], tower.average[:],
                              square[h % RING][:], start=True, stop=True).then_inc(averaged.sem, 1)

                def score(j, r, g, m):
                    pe.wait_ge(peaked.sem, peaked.at((j * HALVES + g) * per_half + m - 1))
                    if a.causal:
                        pe.matmul(score_ps[m % 2][:], place[:], later[:, None, 0:P].to_broadcast([P, per_bank, P]),
                                  start=True, stop=False)
                    for i in range(per_bank):
                        to = score_ps[m % 2][:, i * seen:(i + 1) * seen]
                        mm = pe.matmul(to, q_t[r][:, m * per_bank + i, 0:P], k_t[r][g][:, 0:seen],
                                       start=not a.causal, stop=not a.causal or i == per_bank - 1)
                    mm.then_inc(scored.sem, 1)

                def score_last(j, r, g):
                    pe.wait_ge(peaked.sem, peaked.at((j * HALVES + g) * per_half))
                    pe.matmul(last_ps[0:a.heads, 0:SEQ], q_t[r][:, :, P], k_t[r][g][:],
                              start=True, stop=True).then_inc(scored.sem, 1)

                def turn_peak(j, g):
                    pe.wait_ge(peaked.sem, peaked.at((j * HALVES + g + 1) * per_half))
                    pe.wait_ge(peak_split.sem, peak_split.at(j * HALVES + g))
                    pe.transpose(turn_ps[0:tiles, 0:P], peak[:, g, :], tower.ident[:]).then_inc(
                        peak_turned.sem, 1)

                def scores_t(j, r, n):
                    g, x = n // steps, n % steps
                    if x == 0:
                        pe.wait_ge(rows_landed[g].sem, rows_landed[g].at(j * 32 + 32))
                    pe.wait_ge(exped.sem, exped.at(j * both + n - 1))
                    if n == 0:
                        pe.wait_ge(y_read.sem, y_read.at(j))
                    if n == 1:
                        pe.wait_ge(peak_split.sem, peak_split.at((j + 1) * HALVES))
                    to = st_ps[n % 2][:, 0:size(x)]
                    pe.matmul(to, k_t[r][g][:, 0:P], queries(q_t[r], x), start=True, stop=False)
                    mm = pe.matmul(to, ones[:], peak_row[g][:, rows_of(x)], start=False, stop=not masked(x))
                    if masked(x):
                        mm = pe.matmul(to, later[:, 0:P], place[:, None, 0:P].to_broadcast([P, 4, P]),
                                       start=False, stop=True)
                    else:
                        if x:
                            pe.wait_ge(exped.sem, exped.at(j * both + n))
                        to = last_row(n)
                        pe.matmul(to, k_t[r][g][:, P:SEQ], queries(q_t[r], x), start=True, stop=False)
                        mm = pe.matmul(to, ones[:, 0:1], peak_row[g][:, rows_of(x)], start=False, stop=True)
                    mm.then_inc(st_ready.sem, 1)

                def mix(j, n):
                    g, x = n // steps, n % steps
                    pe.wait_ge(exped.sem, exped.at(j * both + n + 1))
                    pe.wait_ge(out_read.sem, out_read.at(j * both + n - 1))
                    to = out_ps[n % 2][:, 0:size(x)]
                    mm = pe.matmul(to, val[g][:], prob[n % 3][:, 0:size(x)], start=True, stop=masked(x))
                    if not masked(x):
                        mm = pe.matmul(to, val_last[g][:], prob_last[n % 3][:, 0:size(x)],
                                       start=False, stop=True)
                    mm.then_inc(out_ready.sem, 1)

                def output(j):
                    pe.wait_ge(out_read.sem, out_read.at((j + 1) * both))
                    for head in range(a.heads):
                        mm = pe.matmul(y_ps[:, 0:SEQ], wo[:, head, :], mixed[:, head, :],
                                       start=head == 0, stop=head == a.heads - 1)
                    mm.then_inc(y_ready.sem, 1)

                def pair(j, r, first_pair):
                    pe.wait_ge(written.sem, written.at(j * groups + groups))
                    for m in range(banks):
                        score(j, r, 0, m)
                    score_last(j, r, 0)
                    pe.matmul(value_ps[:, 0:P], xs[:, 0:P], wv[:], start=True, stop=True)
                    pe.matmul(value_ps[0:1, P:2 * P], xs[:, P:SEQ], wv[:],
                              start=True, stop=True).then_inc(values_made.sem, 1)
                    turn_peak(j, 0)
                    if not first_pair:
                        output(j - 1)
                    for m in range(banks):
                        score(j, r, 1, m)
                    score_last(j, r, 1)
                    if at_once:
                        turn_peak(j, 1)
                        for h in range(groups):
                            project(j + 1, 1 - r, h)
                    scores_t(j, r, 0)
                    for n in range(both + 1):
                        first, second = beside(n)
                        if first is not None:
                            project(j + 1, 1 - r, first)
                        if n == 0 and not at_once:
                            turn_peak(j, 1)
                        if waiting(n) is not None:
                            average(j + 1, 1 - r, waiting(n))
                        if 0 < n < both:
                            scores_t(j, r, n)
                        if first is not None:
                            average(j + 1, 1 - r, first)
                        if second is not None:
                            project(j + 1, 1 - r, second)
                        if n:
                            mix(j, n - 1)

                for h in range(groups + 1):
                    if h < groups:
                        project(0, 0, h)
                    if h:
                        average(0, 0, h - 1)
                with pe.Fori(0, PAIRS // unroll) as i:
                    for r in range(unroll):
                        pair(unroll * i + r, r % 2, r == 0)
                    output(unroll * i + unroll - 1)

            @block.scalar
            def _(act):
                act.preload_act_table_set("natural_log_exp_and_others")
                eps = tower.eps[1.1920929e-07]
                act.wait_ge(filled.sem, filled.at(4))

                def squares(j, r, h):
                    if a.norm:
                        act.wait_ge(rotated.sem, rotated.at(j * groups + h + 1))
                        act.activation(square[h % RING][:], turned[h % RING][:],
                                       ACT.Square).then_inc(squared.sem, 1)

                def inverse_norm(j, r, h):
                    if a.norm:
                        step, to = j * groups + h, rstd[h % RING]
                        act.wait_ge(averaged.sem, averaged.at(step + 1))
                        act.activation(to[:], avg_ps[:, 0:SEQ], ACT.Ln,
                                       bias=eps).then_inc(logged.sem, 1)
                        act.wait_ge(logged.sem, logged.at(step + 1))
                        act.activation(to[:], to[:], ACT.Exp, scale=-0.5).then_inc(rstd_ready.sem, 1)

                def exponentials(j, n):
                    x = n % steps
                    act.wait_ge(st_ready.sem, st_ready.at(j * both + n + 1))
                    ins = act.activation(prob[n % 3][:, 0:size(x)], st_ps[n % 2][:, 0:size(x)],
                                         ACT.Exp, scale=a.scale)
                    if not masked(x):
                        ins = act.activation(prob_last[n % 3][:, 0:size(x)], last_row(n),
                                             ACT.Exp, scale=a.scale)
                    ins.then_inc(exped.sem, 1)

                def inverse_sum(j, n):
                    g, x = n // steps, n % steps
                    act.wait_ge(out_ready.sem, out_ready.at(j * both + n + 1))
                    act.wait_ge(out_read.sem, out_read.at(j * both + n - 1))
                    act.activation(inv[n % 2][half(g), 0:size(x)], out_ps[n % 2][other(g), 0:size(x)],
                                   ACT.Ln).then_inc(sum_logged.sem, 1)
                    act.wait_ge(sum_logged.sem, sum_logged.at(j * both + n + 1))
                    act.activation(inv[n % 2][half(g), 0:size(x)], inv[n % 2][half(g), 0:size(x)], ACT.Exp,
                                   scale=-1.0).then_inc(inv_ready.sem, 1)

                def pair(j, r):
                    act.wait_ge(values_made.sem, values_made.at(j + 1))
                    for g in range(HALVES):
                        act.activation(val[g][:, half(g)], value_ps[:, D * g:D * g + D], ACT.Copy)
                        ins = act.activation(val_last[g][:, half(g)], value_ps[0:1, P + D * g:P + D * g + D],
                                             ACT.Copy)
                    ins.then_inc(values_ready.sem, 1)
                    for n in range(both + 1):
                        first, second = beside(n)
                        if waiting(n) is not None:
                            inverse_norm(j + 1, 1 - r, waiting(n))
                        if first is not None:
                            squares(j + 1, 1 - r, first)
                        if n < both:
                            exponentials(j, n)
                        if first is not None:
                            inverse_norm(j + 1, 1 - r, first)
                        if second is not None:
                            squares(j + 1, 1 - r, second)
                        if n:
                            inverse_sum(j, n - 1)

                for h in range(groups + 1):
                    if h < groups:
                        squares(0, 0, h)
                    if h:
                        inverse_norm(0, 0, h - 1)
                with act.Fori(0, PAIRS // unroll) as i:
                    for r in range(unroll):
                        pair(unroll * i + r, r % 2)

            @block.vector
            def _(dve):
                for r in range(2):
                    for g in range(HALVES):
                        dve.memset(k_t[r][g][other(g), :], 0.0)
                dve.wait_ge(loaded.sem, loaded.at(16 * len(loads)))
                dve.wait_ge(filled.sem, filled.at(4))

                def parts(r, h):
                    if h:
                        return [(q_t[r][:, h - 1, :], slice(0, P))]
                    return [(k_t[r][g][half(g), :], half(g)) for g in range(HALVES)]

                def take(j, r, h):
                    step, ps = j * groups + h, front_ps[bank_of(r, h)]
                    dve.wait_ge(projected.sem, projected.at(step + 1))
                    if not a.rope:
                        for dst, rows in parts(r, h):
                            ins = dve.tensor_scalar(dst, ps[rows, 0:SEQ], bias[rows, h:h + 1], None, ALU.add)
                        ins.then_inc(written.sem, 1)
                        return
                    both_products = products[bank_of(r, h)]
                    dve.tensor_tensor(both_products[:], ps[:, 0:2 * SEQ].rearrange("p (k t) -> p k t", k=2),
                                      cos_sin[:], ALU.mult).then_inc(multiplied.sem, 1)
                    dve.wait_ge(multiplied.sem, multiplied.at(step + 1))
                    if a.norm:
                        dve.tensor_tensor(turned[h % RING][:], both_products[:, 0, :],
                                          both_products[:, 1, :], ALU.add).then_inc(rotated.sem, 1)
                    else:
                        for dst, rows in parts(r, h):
                            ins = dve.tensor_tensor(dst, both_products[rows, 0, :], both_products[rows, 1, :],
                                                    ALU.add)
                        ins.then_inc(written.sem, 1)

                def scale(j, r, h):
                    if a.norm:
                        step, col = j * groups + h, 1 if h else 0
                        dve.wait_ge(rotated.sem, rotated.at(step + 1))
                        dve.wait_ge(rstd_ready.sem, rstd_ready.at(step + 1))
                        for dst, rows in parts(r, h):
                            ins = dve.scalar_tensor_tensor(dst, turned[h % RING][rows, :],
                                                           norm_w[rows, col:col + 1],
                                                           rstd[h % RING][rows, :], ALU.mult, ALU.mult)
                        ins.then_inc(written.sem, 1)

                def peaks(j, g, m):
                    dve.wait_ge(scored.sem, scored.at((j * HALVES + g) * per_half + m + 1))
                    if m < banks:
                        ins = dve.tensor_reduce(peak[:, g, per_bank * m:per_bank * (m + 1)],
                                                score_ps[m % 2][:, 0:per_bank * seen]
                                                .rearrange("p (i s) -> p i s", s=seen), AX, ALU.max)
                    else:
                        ins = dve.tensor_reduce(peak[0:a.heads, g, a.heads:tiles],
                                                last_ps[0:a.heads, 0:SEQ], AX, ALU.max)
                    ins.then_inc(peaked.sem, 1)

                def split_peak(j, g):
                    step = j * HALVES + g
                    dve.wait_ge(peak_turned.sem, peak_turned.at(step + 1))
                    dve.wait_ge(rows_landed[g].sem, rows_landed[g].at(j * 32))
                    dve.tensor_scalar(peak_t[g][:, 0, :], turn_ps[0:tiles, 0:P], -1.0, None,
                                      ALU.mult).then_inc(peak_high.sem, 1)
                    dve.wait_ge(peak_high.sem, peak_high.at(step + 1))
                    dve.scalar_tensor_tensor(peak_t[g][:, 1, :], turn_ps[0:tiles, 0:P], -1.0,
                                             peak_t[g][:, 0, :], ALU.mult, ALU.subtract).then_inc(
                        peak_split.sem, 1)

                def normalise(j, n):
                    g, x = n // steps, n % steps
                    step = j * both + n
                    dst = queries(mixed[half(g)], x)
                    dve.wait_ge(inv_ready.sem, inv_ready.at(step + 1))
                    sums, over = out_ps[n % 2][half(g), 0:size(x)], inv[n % 2][half(g), 0:size(x)]
                    if not a.bf16_out:
                        dve.tensor_tensor(dst, shaped(sums, x), shaped(over, x), ALU.mult).then_inc(
                            out_read.sem, 1)
                        return
                    dve.tensor_tensor(raw[half(g), 0:size(x)], sums, over, ALU.mult).then_inc(rounding.sem, 1)
                    dve.wait_ge(rounding.sem, rounding.at(2 * step + 1))
                    col = a.heads + 1
                    dve.tensor_scalar(narrow[half(g), 0:size(x)], raw[half(g), 0:size(x)],
                                      bias[half(g), col:col + 1], None, ALU.add).then_inc(rounding.sem, 1)
                    dve.wait_ge(rounding.sem, rounding.at(2 * step + 2))
                    dve.tensor_copy(dst, shaped(narrow[half(g), 0:size(x)], x)).then_inc(out_read.sem, 1)

                def add_output(j):
                    dve.wait_ge(y_ready.sem, y_ready.at(j + 1))
                    at = bass.ds(j * SEQ, SEQ)
                    if out_bias is None:
                        ins = dve.tensor_tensor(acc[:, at], y_ps[:, 0:SEQ], acc[:, at], ALU.add)
                    else:
                        ins = dve.scalar_tensor_tensor(acc[:, at], y_ps[:, 0:SEQ], out_bias, acc[:, at],
                                                       ALU.add, ALU.add)
                    ins.then_inc(y_read.sem, 1)

                def pair(j, r, first_pair):
                    peaks(j, 0, 0)
                    if not first_pair:
                        normalise(j - 1, both - 1)
                    for m in range(1, per_half):
                        peaks(j, 0, m)
                    split_peak(j, 0)
                    if not first_pair:
                        add_output(j - 1)
                    for m in range(per_half):
                        peaks(j, 1, m)
                    if at_once:
                        split_peak(j, 1)
                        for h in range(groups):
                            take(j + 1, 1 - r, h)
                    for n in range(both + 1):
                        first, second = beside(n)
                        if first is not None:
                            take(j + 1, 1 - r, first)
                        if n == 0 and not at_once:
                            split_peak(j, 1)
                        if n >= 2:
                            normalise(j, n - 2)
                        if waiting(n) is not None:
                            scale(j + 1, 1 - r, waiting(n))
                        if second is not None:
                            take(j + 1, 1 - r, second)
                        if first is not None:
                            scale(j + 1, 1 - r, first)

                for h in range(groups + 1):
                    if h < groups:
                        take(0, 0, h)
                    if h:
                        scale(0, 0, h - 1)
                with dve.Fori(0, PAIRS // unroll) as i:
                    for r in range(unroll):
                        pair(unroll * i + r, r % 2, r == 0)
                    normalise(unroll * i + unroll - 1, both - 1)
                    add_output(unroll * i + unroll - 1)



def add_phase(tower, acc, x):
    with tower.nc.Block() as block:
        @block.vector
        def _(dve):
            dve.tensor_tensor(acc[:], acc[:], x[:], ALU.add)



GROUP = 8
WINDOW = 288
GROUPS = WINDOW // GROUP


def linear_attention_phase(tower, hn, acc, names, out_bias):
    nc, n2 = tower.nc, PAIRS // 2
    cut = [slice(0, 65), slice(65, SEQ)]
    size = [65, 64]
    with phase(tower) as ph:
        wq, wk, wv, wo = [ph.sb(n, [P, P]) for n in ("wq", "wk", "wv", "wo")]
        raw_q, turned_q, q = [ph.sb(n, [P, WINDOW]) for n in ("raw_q", "turned_q", "q")]
        stat = ph.sb("stat", [P, GROUPS])
        grouped = turned_q[:].rearrange("p (n e) -> p n e", e=GROUP)
        spread = stat[:, :, None].to_broadcast([P, GROUPS, GROUP])
        two = range(2)
        xs = [ph.sb(f"xs{u}", [P, SEQ]) for u in two]
        low = [ph.sb(f"low{u}", [P, 1]) for u in two]
        ek = [ph.sb(f"ek{u}", [P, SEQ]) for u in two]
        total = [ph.sb(f"total{u}", [P, 1]) for u in two]
        inv = [ph.sb(f"inv{u}", [P, 1]) for u in two]
        ek_t = [ph.sb(f"ek_t{u}", [65, 2, P]) for u in two]
        vt = [ph.sb(f"vt{u}", [65, 2, P]) for u in two]
        ctx = [ph.sb(f"ctx{u}", [P, P]) for u in two]
        at_s = [ph.sb(f"at{u}", [P, SEQ]) for u in two]
        k_ps = [ph.ps(f"k{u}") for u in two]
        v_ps = [ph.ps(f"v{u}") for u in two]
        t_ps = [ph.ps(f"t{u}") for u in two]
        c_ps = [ph.ps(f"c{u}") for u in two]
        q_ps = k_ps[1][:, SEQ:3 * SEQ]
        sig = lambda k=1: [ph.counts(n2 * k) for _ in two]
        loaded = ph.counts(64)
        filled, q_made, q_copied, q_exped, q_ready = [ph.counts(k) for k in (1, n2 + 1, n2 + 1, n2, n2)]
        q_turned, q_top, q_lowered = [ph.counts(n2 + 1) for _ in range(3)]
        q_summed, q_inverted, q_scaled = [ph.counts(n2) for _ in range(3)]
        copied, k_made, v_made, lowest, exped, v_copied = sig(), sig(), sig(), sig(), sig(), sig()
        ek_turned, ek_copied, inverted, ctx_made, ctx_ready = sig(), sig(), sig(), sig(), sig()
        at_made, at_copied, y_made, y_read = sig(), sig(), sig(), sig()

        def cols(i, u):
            return bass.ds((2 * i + u) * SEQ, SEQ)

        with nc.Block() as block:
            @block.sync
            def _(sp):
                for buf, name in zip((wq, wk, wv, wo), names):
                    sp.dma_start(buf[:], tower.dram[name]).then_inc(loaded.sem, 16)

            @block.gpsimd
            def _(pool):
                pool.memset(raw_q[:, 2 * SEQ:WINDOW], 0.0).then_inc(filled.sem, 1)
                with pool.Fori(0, n2) as i:
                    for u in two:
                        pool.wait_ge(v_made[u].sem, v_made[u].at(i))
                        pool.tensor_copy(xs[u][:], hn[:, cols(i, u)]).then_inc(copied[u].sem, 1)

            @block.tensor
            def _(pe):
                pe.wait_ge(loaded.sem, loaded.at(64))

                def queries(i):
                    pe.matmul(q_ps, wq[:], hn[:, bass.ds(i * 2 * SEQ, 2 * SEQ)],
                              start=True, stop=True).then_inc(q_made.sem, 1)

                queries(0)
                pe.wait_ge(q_copied.sem, q_copied.at(1))
                with pe.Fori(0, n2) as i:
                    for u in two:
                        pe.wait_ge(copied[u].sem, copied[u].at(i + 1))
                        pe.wait_ge(at_copied[u].sem, at_copied[u].at(i))
                        if u == 1:
                            queries(i + 1)
                        pe.matmul(k_ps[u][:, 0:SEQ], wk[:], xs[u][:], start=True, stop=True).then_inc(
                            k_made[u].sem, 1)
                        pe.wait_ge(y_read[u].sem, y_read[u].at(i))
                        for c in two:
                            mm = pe.matmul(v_ps[u][0:size[c], c * P:(c + 1) * P], xs[u][:, cut[c]], wv[:],
                                           start=True, stop=True)
                        mm.then_inc(v_made[u].sem, 1)
                    for u in two:
                        pe.wait_ge(exped[u].sem, exped[u].at(i + 1))
                        pe.wait_ge(ek_copied[u].sem, ek_copied[u].at(i))
                        for c in two:
                            mm = pe.transpose(t_ps[u][0:size[c], c * P:(c + 1) * P], ek[u][:, cut[c]],
                                              tower.ident[:])
                        mm.then_inc(ek_turned[u].sem, 1)
                    for u in two:
                        pe.wait_ge(ek_copied[u].sem, ek_copied[u].at(i + 1))
                        pe.wait_ge(v_copied[u].sem, v_copied[u].at(i + 1))
                        pe.wait_ge(ctx_ready[u].sem, ctx_ready[u].at(i))
                        for c in two:
                            mm = pe.matmul(c_ps[u][:, 0:P], ek_t[u][0:size[c], c, :], vt[u][0:size[c], c, :],
                                           start=c == 0, stop=c == 1)
                        mm.then_inc(ctx_made[u].sem, 1)
                    for u in two:
                        pe.wait_ge(ctx_ready[u].sem, ctx_ready[u].at(i + 1))
                        pe.wait_ge(q_ready.sem, q_ready.at(i + 1))
                        pe.wait_ge(q_copied.sem, q_copied.at(i + 2))
                        pe.matmul(k_ps[u][:, 0:SEQ], ctx[u][:], q[:, u * SEQ:(u + 1) * SEQ],
                                  start=True, stop=True).then_inc(at_made[u].sem, 1)
                    for u in two:
                        pe.wait_ge(at_copied[u].sem, at_copied[u].at(i + 1))
                        pe.matmul(v_ps[u][:, 0:SEQ], wo[:], at_s[u][:], start=True, stop=True).then_inc(
                            y_made[u].sem, 1)

            @block.scalar
            def _(act):
                def copy_queries(i):
                    act.wait_ge(q_made.sem, q_made.at(i + 1))
                    act.wait_ge(q_turned.sem, q_turned.at(i))
                    act.activation(raw_q[:, 0:2 * SEQ], q_ps, ACT.Copy).then_inc(q_copied.sem, 1)

                copy_queries(0)
                with act.Fori(0, n2) as i:
                    act.wait_ge(q_lowered.sem, q_lowered.at(i + 1))
                    act.activation(turned_q[:], turned_q[:], ACT.Exp).then_inc(q_exped.sem, 1)
                    for u in two:
                        act.wait_ge(v_made[u].sem, v_made[u].at(i + 1))
                        for c in two:
                            ins = act.activation(vt[u][0:size[c], c, :], v_ps[u][0:size[c], c * P:(c + 1) * P],
                                                 ACT.Copy)
                        ins.then_inc(v_copied[u].sem, 1)
                        act.wait_ge(lowest[u].sem, lowest[u].at(i + 1))
                        act.activation(ek[u][:], k_ps[u][:, 0:SEQ], ACT.Exp, bias=low[u][:, 0:1],
                                       accum_out=total[u][:, 0:1]).then_inc(exped[u].sem, 1)
                    copy_queries(i + 1)
                    for u in two:
                        act.wait_ge(at_made[u].sem, at_made[u].at(i + 1))
                        act.activation(at_s[u][:], k_ps[u][:, 0:SEQ], ACT.Copy).then_inc(at_copied[u].sem, 1)

            @block.vector
            def _(dve):
                dve.wait_ge(filled.sem, filled.at(1))

                def lower_queries(i):
                    dve.wait_ge(q_copied.sem, q_copied.at(i + 1))
                    dve.wait_ge(q_ready.sem, q_ready.at(i))
                    dve.transpose(turned_q[:], raw_q[:]).then_inc(q_turned.sem, 1)
                    dve.wait_ge(q_turned.sem, q_turned.at(i + 1))
                    dve.tensor_reduce(stat[:], grouped, AX, ALU.max).then_inc(q_top.sem, 1)
                    dve.wait_ge(q_top.sem, q_top.at(i + 1))
                    dve.tensor_tensor(grouped, grouped, spread, ALU.subtract).then_inc(q_lowered.sem, 1)

                lower_queries(0)
                with dve.Fori(0, n2) as i:
                    for u in two:
                        dve.wait_ge(k_made[u].sem, k_made[u].at(i + 1))
                        dve.tensor_reduce(low[u][:], k_ps[u][:, 0:SEQ], AX, ALU.max,
                                          negate=True).then_inc(lowest[u].sem, 1)
                    dve.wait_ge(q_exped.sem, q_exped.at(i + 1))
                    dve.tensor_reduce(stat[:], grouped, AX, ALU.add).then_inc(q_summed.sem, 1)
                    dve.wait_ge(q_summed.sem, q_summed.at(i + 1))
                    dve.reciprocal(stat[:], stat[:]).then_inc(q_inverted.sem, 1)
                    dve.wait_ge(q_inverted.sem, q_inverted.at(i + 1))
                    dve.tensor_tensor(grouped, grouped, spread, ALU.mult).then_inc(q_scaled.sem, 1)
                    for u in two:
                        dve.wait_ge(ek_turned[u].sem, ek_turned[u].at(i + 1))
                        for c in two:
                            ins = dve.tensor_copy(ek_t[u][0:size[c], c, :], t_ps[u][0:size[c], c * P:(c + 1) * P])
                        ins.then_inc(ek_copied[u].sem, 1)
                        dve.reciprocal(inv[u][:], total[u][:]).then_inc(inverted[u].sem, 1)
                    dve.wait_ge(q_scaled.sem, q_scaled.at(i + 1))
                    for u in two:
                        dve.wait_ge(at_made[u].sem, at_made[u].at(i))
                    dve.transpose(q[:], turned_q[:]).then_inc(q_ready.sem, 1)
                    for u in two:
                        dve.wait_ge(ctx_made[u].sem, ctx_made[u].at(i + 1))
                        dve.wait_ge(inverted[u].sem, inverted[u].at(i + 1))
                        dve.scalar_tensor_tensor(ctx[u][:], c_ps[u][:, 0:P], inv[u][:, 0:1],
                                                 tower.head_blocks[:], ALU.mult, ALU.mult).then_inc(
                            ctx_ready[u].sem, 1)
                    lower_queries(i + 1)
                    for u in two:
                        dve.wait_ge(y_made[u].sem, y_made[u].at(i + 1))
                        dve.scalar_tensor_tensor(acc[:, cols(i, u)], v_ps[u][:, 0:SEQ], out_bias,
                                                 acc[:, cols(i, u)], ALU.add, ALU.add).then_inc(
                            y_read[u].sem, 1)


def linear_tower(tower, nc, h, x, column):
    with ExitStack() as stack:
        wide_hn = stack.enter_context(nc.sbuf_tensor("lin_hn", [P, COLS + 2 * SEQ], F32))
        hn = wide_hn[:, 0:COLS]
        with phase(tower) as ph:
            pos = ph.sb("pos", [P, SEQ])
            loaded = ph.counts(32)
            with nc.Block() as block:
                @block.sync
                def _(sp):
                    sp.dma_start(pos[:], tower.dram["L1_pos"]).then_inc(loaded.sem, 16)
                    sp.dma_start(tower.head_blocks[:], tower.dram["L1_blocks"]).then_inc(loaded.sem, 16)

                @block.vector
                def _(dve):
                    dve.memset(wide_hn[:, COLS:COLS + 2 * SEQ], 0.0)
                    dve.wait_ge(loaded.sem, loaded.at(32))
                    xj = x[:].rearrange("p (j t) -> p j t", t=SEQ)
                    dve.tensor_tensor(xj, xj, pos[:, None, :].to_broadcast([P, PAIRS, SEQ]), ALU.add)
        for l in range(4):
            norm_phase(tower, x, hn, 1e-5, gamma=column(f"L1_g1{l}"), beta=column(f"L1_b1{l}"))
            linear_attention_phase(tower, wide_hn, x, [f"L1_wq{l}", f"L1_wk{l}", f"L1_wv{l}", f"L1_wo{l}"],
                                   column(f"L1_bo{l}"))
            norm_phase(tower, x, hn, 1e-5, gamma=column(f"L1_g2{l}"), beta=column(f"L1_b2{l}"))
            mlp_phase(tower, f"L1_up{l}", f"L1_down{l}", f"L1_up_b{l}", 4, ACT.Gelu, P,
                      lambda b: hn, AddTo(x, column(f"L1_bf2{l}")), None)
        add_phase(tower, h, x)



KEPT = max(1, int(0.5 * SEQ)) - 1


LARGEST = 3.4028234663852886e38


class WeightedAddTo:

    def __init__(self, tower, acc, bias, weight_rows, rows, finite=False):
        self.acc, self.bias, self.weights, self.rows = acc, bias, weight_rows, rows
        self.tower, self.finite = tower, finite

    def load(self, ph):
        self.tmp = [ph.sb(f"weighted{u}", [P, TILE]) for u in range(2)]
        self.made = ph.counts(TILES)
        if self.finite:
            self.ends = [ph.sb(f"ends{u}", [P, 2, TILE]) for u in range(2)]
            self.is_finite = [ph.sb(f"is_finite{u}", [P, TILE], mybir.dt.int32) for u in range(2)]
            self.nothing = [ph.sb(f"nothing{u}", [P, TILE]) for u in range(2)]
            self.zeroed = ph.counts(TILES)
            self.compared = ph.counts(TILES)
            self.joined = ph.counts(TILES)
            self.guarded = ph.counts(TILES)

    def broadcast(self, pe, aux, state, cols, u):
        return pe.matmul(aux[:, 0:TILE], self.tower.spread2[0:self.rows, :], self.weights[0:self.rows, cols],
                         start=True, stop=True)

    def vector(self, dve, y, aux, state, cols, i, u):
        step, tmp = 2 * i + u + 1, self.tmp[u]
        dve.scalar_tensor_tensor(tmp[:], y, self.bias, aux[:], ALU.add,
                                 ALU.mult).then_inc(self.made.sem, 1)
        dve.wait_ge(self.made.sem, self.made.at(step))
        if not self.finite:
            return dve.tensor_tensor(self.acc[:, cols], self.acc[:, cols], tmp[:], ALU.add)
        ends = self.ends[u]
        dve.tensor_scalar(ends[:, 0, :], tmp[:], LARGEST, 10000.0, ALU.is_gt, ALU.mult)
        dve.tensor_scalar(ends[:, 1, :], tmp[:], -LARGEST, -10000.0, ALU.is_lt, ALU.mult)
        dve.tensor_scalar(self.nothing[u][:], tmp[:], 0.0, None, ALU.mult).then_inc(self.zeroed.sem, 1)
        dve.wait_ge(self.zeroed.sem, self.zeroed.at(step))
        dve.tensor_scalar(self.is_finite[u][:], self.nothing[u][:], 0.0, None,
                          ALU.is_equal).then_inc(self.compared.sem, 1)
        dve.wait_ge(self.compared.sem, self.compared.at(step))
        dve.tensor_tensor(ends[:, 0, :], ends[:, 0, :], ends[:, 1, :], ALU.add).then_inc(self.joined.sem, 1)
        dve.wait_ge(self.joined.sem, self.joined.at(step))
        dve.memset(self.nothing[u][0:1, 0:1], 0.0)
        dve.copy_predicated(ends[:, 0, :], self.is_finite[u][:], tmp[:]).then_inc(self.guarded.sem, 1)
        dve.wait_ge(self.guarded.sem, self.guarded.at(step))
        return dve.tensor_tensor(self.acc[:, cols], self.acc[:, cols], ends[:, 0, :], ALU.add)


def half_ffn(tower, nc, h, x, column):
    add_phase(tower, h, x)
    with ExitStack() as stack:
        rows = stack.enter_context(nc.sbuf_tensor("mod_rows", [HALVES, COLS], F32))
        with phase(tower) as ph:
            wr = ph.sb("wr", [P, HALVES])
            br = ph.sb("br", [HALVES, 1])
            weight = ph.sb("weight", [D, SEQ])
            race = ph.sb("race", [D, SEQ])
            top = ph.sb("top", [D, 8])
            w_ps = [ph.ps(f"w{r}") for r in range(4)]
            loaded = ph.counts(32)
            made = ph.counts(TILES)
            copied = ph.counts(TILES)
            turned = ph.counts(32)
            back = ph.counts(32)
            rounds = -(-KEPT // 8)
            v = ph.counts(2 * rounds + 3)
            with nc.Block() as block:
                @block.sync
                def _(sp):
                    sp.dma_start(wr[:], tower.dram["L1f_wr"]).then_inc(loaded.sem, 16)
                    sp.dma_start(br[:], tower.dram["L1f_br"]).then_inc(loaded.sem, 16)
                    sp.wait_ge(copied.sem, copied.at(TILES))
                    for g in range(HALVES):
                        sp.dma_start(weight[PAIRS * g:PAIRS * (g + 1), :],
                                     rows[g:g + 1, :].rearrange("a (j t) -> a j t", t=SEQ)).then_inc(
                            turned.sem, 16)
                    sp.wait_ge(v.sem, v.at(2 * rounds + 3))
                    for g in range(HALVES):
                        sp.dma_start(rows[g:g + 1, :].rearrange("a (j t) -> a j t", t=SEQ),
                                     race[PAIRS * g:PAIRS * (g + 1), :]).then_inc(back.sem, 16)
                    sp.wait_ge(back.sem, back.at(32))

                @block.tensor
                def _(pe):
                    pe.wait_ge(loaded.sem, loaded.at(32))
                    for n in range(TILES):
                        pe.wait_ge(copied.sem, copied.at(n - 3))
                        pe.matmul(w_ps[n % 4][0:HALVES, 0:TILE], wr[:], x[:, n * TILE:(n + 1) * TILE],
                                  start=True, stop=True).then_inc(made.sem, 1)

                @block.scalar
                def _(act):
                    for n in range(TILES):
                        act.wait_ge(made.sem, made.at(n + 1))
                        act.activation(rows[:, n * TILE:(n + 1) * TILE], w_ps[n % 4][0:HALVES, 0:TILE],
                                       ACT.Identity, bias=br[:, 0:1]).then_inc(copied.sem, 1)

                @block.vector
                def _(dve):
                    done = [0]

                    def step(ins):
                        done[0] += 1
                        ins.then_inc(v.sem, 1)
                        dve.wait_ge(v.sem, v.at(done[0]))

                    dve.wait_ge(turned.sem, turned.at(32))
                    step(dve.tensor_copy(race[:], weight[:]))
                    for r in range(rounds):
                        step(dve.max(top[:], race[:]))
                        if r == rounds - 1:
                            step(dve.memset(top[:, KEPT - 8 * r:8], 3.0e38))
                        step(dve.match_replace(race[:], top[:], race[:], -3.0e38))
                    step(dve.scalar_tensor_tensor(race[:], race[:], -3.0e38, weight[:], ALU.is_equal, ALU.mult))
                    v.total = done[0]
                    assert done[0] == 2 * rounds + 3
        finish = WeightedAddTo(tower, h, column("L1f_b2"), rows, HALVES)
        mlp_phase(tower, "L1f_up", "L1f_down", "L1f_up_b", 4, ACT.Gelu_apprx_tanh, P,
                  lambda b: x, finish, finish.load)



HIDDEN = int(8 / 3 * D)
SLAB = 2 * HIDDEN // 3 + 1
SLABS = 3


def gated_experts_phase(tower, hn, rows_t, acc):
    nc = tower.nc
    blocks = EXPERTS * SLABS
    lag = 2
    with phase(tower) as ph:
        w1 = ph.sb("w1", [P, blocks, SLAB])
        w3 = ph.sb("w3", [P, blocks, SLAB])
        w2 = ph.sb("w2", [SLAB, blocks, P])
        pick = ph.sb("pick", [P, EXPERTS, P])
        a_ps, c_ps = [[ph.ps(f"{n}{r}") for r in range(2)] for n in "ac"]
        weight_ps = [ph.ps(f"weight{r}") for r in range(2)]
        y_ps = [ph.ps(f"y{u}") for u in range(2)]
        weighted = [ph.sb(f"weighted{r}", [P, TILE]) for r in range(2)]
        silu = [ph.sb(f"silu{r}", [SLAB, TILE]) for r in range(2)]
        hid = [ph.sb(f"hid{r}", [SLAB, TILE]) for r in range(3)]
        n2 = TILES // 2
        per, per_e = 2 * blocks, 2 * EXPERTS
        loaded = ph.counts(64)
        weight_made = ph.counts(n2 * per_e)
        weighted_ready = ph.counts(n2 * per_e)
        up_made = ph.counts(n2 * per)
        silu_ready = ph.counts(n2 * per)
        hid_ready = ph.counts(n2 * per)
        down_made = ph.counts(n2 * per)
        y_read = [ph.counts(n2) for _ in range(2)]

        def cols(i, u):
            return bass.ds((2 * i + u) * TILE, TILE)

        with nc.Block() as block:
            @block.sync
            def _(sp):
                for buf, name in ((pick, "L2m_pick"), (w1, "L2m_w1"), (w3, "L2m_w3"), (w2, "L2m_w2")):
                    sp.dma_start(buf[:], tower.dram[name]).then_inc(loaded.sem, 16)

            @block.tensor
            def _(pe):
                pe.wait_ge(loaded.sem, loaded.at(64))

                def spread(i, x):
                    pe.wait_ge(weighted_ready.sem, weighted_ready.at(i * per_e + x - 1))
                    pe.matmul(weight_ps[x % 2][:, 0:TILE], pick[:, x % EXPERTS, :],
                              rows_t[:, cols(i, x // EXPERTS)], start=True, stop=True).then_inc(
                        weight_made.sem, 1)

                def up(i, n):
                    x, b, u = n // SLABS, n % blocks, n // blocks
                    pe.wait_ge(hid_ready.sem, hid_ready.at(i * per + n - 1))
                    pe.matmul(a_ps[n % 2][0:SLAB, 0:TILE], w1[:, b, :], hn[:, cols(i, u)],
                              start=True, stop=True)
                    pe.wait_ge(weighted_ready.sem, weighted_ready.at(i * per_e + x + 1))
                    pe.matmul(c_ps[n % 2][0:SLAB, 0:TILE], w3[:, b, :], weighted[x % 2][:],
                              start=True, stop=True).then_inc(up_made.sem, 1)

                def down(i, m):
                    b, u = m % blocks, m // blocks
                    if b == 0:
                        pe.wait_ge(y_read[u].sem, y_read[u].at(i))
                    pe.wait_ge(hid_ready.sem, hid_ready.at(i * per + m + 1))
                    pe.matmul(y_ps[u][:, 0:TILE], w2[:, b, :], hid[m % 3][:], start=b == 0,
                              stop=b == blocks - 1).then_inc(down_made.sem, 1)

                with pe.Fori(0, n2) as i:
                    spread(i, 0)
                    for n in range(per + lag):
                        if n < per and n % SLABS == 0 and n // SLABS + 1 < per_e:
                            spread(i, n // SLABS + 1)
                        if n < per:
                            up(i, n)
                        if n >= lag:
                            down(i, n - lag)

            @block.scalar
            def _(act):
                with act.Fori(0, n2) as i:
                    for n in range(per):
                        act.wait_ge(up_made.sem, up_made.at(i * per + n + 1))
                        act.wait_ge(hid_ready.sem, hid_ready.at(i * per + n - 1))
                        act.activation(silu[n % 2][:], a_ps[n % 2][0:SLAB, 0:TILE],
                                       ACT.Silu).then_inc(silu_ready.sem, 1)

            @block.vector
            def _(dve):
                def weigh(i, x):
                    dve.wait_ge(weight_made.sem, weight_made.at(i * per_e + x + 1))
                    dve.wait_ge(up_made.sem, up_made.at(i * per + (x - 1) * SLABS))
                    dve.tensor_tensor(weighted[x % 2][:], hn[:, cols(i, x // EXPERTS)],
                                      weight_ps[x % 2][:, 0:TILE], ALU.mult).then_inc(weighted_ready.sem, 1)

                def add_y(i, u):
                    dve.wait_ge(down_made.sem, down_made.at(i * per + (u + 1) * blocks))
                    dve.tensor_tensor(acc[:, cols(i, u)], acc[:, cols(i, u)], y_ps[u][:, 0:TILE],
                                      ALU.add).then_inc(y_read[u].sem, 1)

                with dve.Fori(0, n2) as i:
                    weigh(i, 0)
                    for n in range(per):
                        if n % SLABS == 0 and n // SLABS + 1 < per_e:
                            weigh(i, n // SLABS + 1)
                        dve.wait_ge(silu_ready.sem, silu_ready.at(i * per + n + 1))
                        dve.wait_ge(down_made.sem, down_made.at(i * per + n - 2))
                        dve.tensor_tensor(hid[n % 3][:], silu[n % 2][:], c_ps[n % 2][0:SLAB, 0:TILE],
                                          ALU.mult).then_inc(hid_ready.sem, 1)
                        if n == blocks + lag:
                            add_y(i, 0)
                    add_y(i, 1)


def routed_block(tower, nc, h, x, column):
    with ExitStack() as stack:
        hn = stack.enter_context(nc.sbuf_tensor("routed_hn", [P, COLS], F32))
        norm_phase(tower, x, hn, 1e-6, center=False, gamma=column("L2_ln1"))
        attention_phase(tower, hn, x, ATTENTION["L2f"])
        norm_phase(tower, x, hn, 1e-6, center=False, gamma=column("L2_ln2"))
        with ExitStack() as inner:
            rows_t = inner.enter_context(nc.sbuf_tensor("routed_rows", [P, COLS], F32))
            gate_phase(tower, hn, "L2_gate_w", "L2_gate_b", 2, True, rows_t)
            add_phase(tower, h, x)
            gated_experts_phase(tower, hn, rows_t, h)



TOKENS = HALVES * COLS
CAPACITY = max(1, -(-5 * TOKENS // (4 * EXPERTS)))


def capacity_phase(tower, rows_t, scale_rows):
    nc = tower.nc
    with phase(tower) as ph:
        before = ph.sb("before", [64, 1])
        count = ph.sb("count", [64, COLS])
        pick = ph.sb("pick", [64, 2, HALVES])
        kept = [ph.sb(f"kept{r}", [HALVES, TILE]) for r in range(2)]
        kept_ps = [ph.ps(f"kept_ps{r}") for r in range(2)]
        prob_ps = [ph.ps(f"prob_ps{r}") for r in range(2)]
        loaded = ph.counts(16)
        v = ph.counts(5)
        made = ph.counts(TILES)
        copied = ph.counts(TILES)
        scaled = ph.counts(TILES)
        with nc.Block() as block:
            @block.sync
            def _(sp):
                sp.dma_start(pick[:], tower.dram["L3_pick"]).then_inc(loaded.sem, 16)

            @block.vector
            def _(dve):
                dve.memset(before[:], 0.0).then_inc(v.sem, 1)
                dve.tensor_reduce(count[0:8, 0:1], rows_t[0:8, :], AX, ALU.add).then_inc(v.sem, 1)
                dve.wait_ge(v.sem, v.at(2))
                dve.tensor_copy(before[32:40, :], count[0:8, 0:1]).then_inc(v.sem, 1)
                dve.wait_ge(v.sem, v.at(3))
                dve.tensor_tensor_scan(count[:], rows_t[:], rows_t[:], before[:, 0:1], ALU.add,
                                       ALU.bypass).then_inc(v.sem, 1)
                dve.wait_ge(v.sem, v.at(4))
                dve.scalar_tensor_tensor(count[:], count[:], float(CAPACITY), rows_t[:], ALU.is_le,
                                         ALU.mult).then_inc(v.sem, 1)
                for n in range(TILES):
                    dve.wait_ge(copied.sem, copied.at(n + 1))
                    dve.tensor_tensor(scale_rows[:, n * TILE:(n + 1) * TILE], kept[n % 2][:],
                                      prob_ps[n % 2][0:HALVES, 0:TILE], ALU.mult).then_inc(scaled.sem, 1)

            @block.tensor
            def _(pe):
                pe.wait_ge(loaded.sem, loaded.at(16))
                pe.wait_ge(v.sem, v.at(5))
                for n in range(TILES):
                    pe.wait_ge(scaled.sem, scaled.at(n - 1))
                    at = slice(n * TILE, (n + 1) * TILE)
                    pe.matmul(kept_ps[n % 2][0:HALVES, 0:TILE], pick[:, 0, :], count[:, at],
                              start=True, stop=True)
                    pe.matmul(prob_ps[n % 2][0:HALVES, 0:TILE], pick[:, 1, :], rows_t[:, at],
                              start=True, stop=True).then_inc(made.sem, 1)

            @block.scalar
            def _(act):
                for n in range(TILES):
                    act.wait_ge(made.sem, made.at(n + 1))
                    act.wait_ge(scaled.sem, scaled.at(n - 1))
                    act.activation(kept[n % 2][:], kept_ps[n % 2][0:HALVES, 0:TILE],
                                   ACT.Copy).then_inc(copied.sem, 1)


def capacity_ffn(tower, nc, h, x):
    with ExitStack() as stack:
        scale_rows = stack.enter_context(nc.sbuf_tensor("cap_scale", [HALVES, COLS], F32))
        aug = [stack.enter_context(nc.sbuf_tensor(f"cap_aug{g}", [104, COLS], F32)) for g in range(HALVES)]
        with ExitStack() as inner:
            rows_t = inner.enter_context(nc.sbuf_tensor("cap_rows", [64, COLS], F32))
            gate_phase(tower, x, "L3_gate_w", "L3_gate_b", 1, False, rows_t)
            spread_phase(tower, x, rows_t, aug)
            capacity_phase(tower, rows_t, scale_rows)
        finish = WeightedAddTo(tower, h, 0.0, scale_rows, HALVES, finite=True)
        mlp_phase(tower, "L3_up", "L3_down", "L3_up_b", 4 * EXPERTS, ACT.Relu, 72,
                  lambda b: aug[b % 2], finish, finish.load, extra=("L3_down_b", 104, aug),
                  up_of=lambda b: b // HALVES)



JOINTS = 64
TAPS_H = 5
ROWS_PADDED = JOINTS + TAPS_H - 1
TOKENS_IN = SEQ - 1


def tokenizer_phase(tower, h, column):
    nc, n2, two = tower.nc, PAIRS // 2, range(2)
    with phase(tower) as ph:
        c1w, c2w = ph.sb("c1w", [P, 15, P]), ph.sb("c2w", [P, 10, P])
        c3w, ow = ph.sb("c3w", [P, 10, 2, P]), ph.sb("ow", [P, HALVES, P])
        ln0 = ph.sb("ln0", [P, 2, 192])
        ln1 = ph.sb("ln1", [P, 2, 128])
        x_in = [ph.sb(f"x{u}", [P, HALVES, 192]) for u in two]
        pad1 = [ph.sb(f"pad1{u}", [P, HALVES, ROWS_PADDED, 5]) for u in two]
        pad2 = [ph.sb(f"pad2{u}", [P, HALVES, ROWS_PADDED, 3]) for u in two]
        pad3 = [ph.sb(f"pad3{u}", [P, HALVES, ROWS_PADDED, 2]) for u in two]
        act1 = [ph.sb(f"act1{u}", [P, HALVES, 192]) for u in two]
        act2 = [ph.sb(f"act2{u}", [P, HALVES, 128]) for u in two]
        act3 = [ph.sb(f"act3{u}", [P, HALVES, 128]) for u in two]
        normed = [ph.sb(f"normed{u}", [P, HALVES, 192]) for u in two]
        scaled_by = [ph.sb(f"scaled{u}", [P, HALVES, 192]) for u in two]
        last = [ph.sb(f"last{u}", [P, HALVES, 128]) for u in two]
        turned_s = [ph.sb(f"turned{u}", [P, HALVES, 128]) for u in two]
        stats = [ph.sb(f"stats{u}", [P, HALVES, 6]) for u in two]
        moments = [ph.sb(f"moments{u}", [P, HALVES, 2]) for u in two]
        rstd = [ph.sb(f"rstd{u}", [P, HALVES]) for u in two]
        held = ph.sb("held", [P, 1])
        c1_ps, c2_ps, c3_ps, y_ps = [[ph.ps(f"{n}{u}") for u in two] for n in ("c1", "c2", "c3", "y")]
        sig = lambda k=1: [ph.counts(n2 * k) for _ in two]
        loaded = ph.counts(16 * 6)
        cleared = ph.counts(1)
        landed = [ph.counts(n2 * 16) for _ in two]
        conv1, conv2, conv3, relu1, relu2, relu3 = sig(), sig(), sig(), sig(), sig(), sig()
        padded1, padded2, padded3, last_ready = sig(), sig(), sig(), sig()
        measured, rstd_ready, chain = sig(4), sig(4), sig(4 * 3)
        logged = sig(4)
        turned, turned_copied, y_made, y_written = sig(), sig(), sig(), sig()

        with nc.Block() as block:
            @block.sync
            def _(sp):
                for buf, name in ((ln0, "tok_ln0"), (c1w, "tok_c1w"), (c2w, "tok_c2w"), (ln1, "tok_ln1"),
                                  (c3w, "tok_c3w"), (ow, "tok_ow")):
                    sp.dma_start(buf[:], tower.dram[name]).then_inc(loaded.sem, 16)
                with sp.Fori(0, n2) as i:
                    for u in two:
                        sp.wait_ge(padded1[u].sem, padded1[u].at(i))
                        sp.dma_start(x_in[u][:], tower.dram["tok_x"][bass.ds(2 * i + u, 1), :, :, :]
                                     .rearrange("o p g n -> (o p) g n")).then_inc(landed[u].sem, 16)

            @block.gpsimd
            def _(pool):
                for pads in (pad1, pad2, pad3):
                    for u in two:
                        ins = pool.memset(pads[u][:], 0.0)
                ins.then_inc(cleared.sem, 1)

            @block.tensor
            def _(pe):
                pe.wait_ge(loaded.sem, loaded.at(96))

                def taps(to, pad, weights, kw_of, width):
                    n = TAPS_H * kw_of
                    for k in range(n):
                        kh, kw = k // kw_of, k % kw_of
                        mm = pe.matmul(to, weights(k), pad[:, :, kh:kh + JOINTS, kw:kw + width],
                                       start=k == 0, stop=k == n - 1)
                    return mm

                with pe.Fori(0, n2) as i:
                    for u in two:
                        pe.wait_ge(padded1[u].sem, padded1[u].at(i + 1))
                        pe.wait_ge(relu1[u].sem, relu1[u].at(i))
                        taps(c1_ps[u][:, 0:384], pad1[u], lambda k: c1w[:, k, :], 3, 3).then_inc(
                            conv1[u].sem, 1)
                    for u in two:
                        pe.wait_ge(padded2[u].sem, padded2[u].at(i + 1))
                        pe.wait_ge(relu2[u].sem, relu2[u].at(i))
                        taps(c2_ps[u][:, 0:256], pad2[u], lambda k: c2w[:, k, :], 2, 2).then_inc(
                            conv2[u].sem, 1)
                    for u in two:
                        pe.wait_ge(padded3[u].sem, padded3[u].at(i + 1))
                        pe.wait_ge(relu3[u].sem, relu3[u].at(i))
                        for part in range(2):
                            mm = taps(c3_ps[u][:, part * 128:part * 128 + 128], pad3[u],
                                      lambda k: c3w[:, k, part, :], 2, 1)
                        mm.then_inc(conv3[u].sem, 1)
                    for u in two:
                        pe.wait_ge(last_ready[u].sem, last_ready[u].at(i + 1))
                        pe.wait_ge(y_written[u].sem, y_written[u].at(i))
                        for g in range(HALVES):
                            mm = pe.transpose(y_ps[u][:, g * P:(g + 1) * P], last[u][:, g, :], tower.ident[:])
                        mm.then_inc(turned[u].sem, 1)
                    for u in two:
                        pe.wait_ge(turned_copied[u].sem, turned_copied[u].at(i + 1))
                        for g in range(HALVES):
                            mm = pe.matmul(y_ps[u][:, 256:384], ow[:, g, :], turned_s[u][:, g, :],
                                           start=g == 0, stop=g == 1)
                        mm.then_inc(y_made[u].sem, 1)

            @block.scalar
            def _(act):
                act.preload_act_table_set("natural_log_exp_and_others")
                eps = tower.eps[1e-5]

                def inverse(i, u, k):
                    at = 4 * i + k + 1
                    act.wait_ge(measured[u].sem, measured[u].at(at))
                    act.activation(rstd[u][:], moments[u][:, :, 1], ACT.Ln, bias=eps).then_inc(logged[u].sem, 1)
                    act.wait_ge(logged[u].sem, logged[u].at(at))
                    act.activation(rstd[u][:], rstd[u][:], ACT.Exp, scale=-0.5).then_inc(rstd_ready[u].sem, 1)

                with act.Fori(0, n2) as i:
                    for u in two:
                        inverse(i, u, 0)
                    for u in two:
                        act.wait_ge(conv1[u].sem, conv1[u].at(i + 1))
                        act.activation(act1[u][:], c1_ps[u][:, 0:384].rearrange("p (g n) -> p g n", g=2),
                                       ACT.Relu, bias=column("tok_c1b")).then_inc(relu1[u].sem, 1)
                        inverse(i, u, 1)
                    for u in two:
                        act.wait_ge(conv2[u].sem, conv2[u].at(i + 1))
                        act.activation(act2[u][:], c2_ps[u][:, 0:256].rearrange("p (g n) -> p g n", g=2),
                                       ACT.Relu, bias=column("tok_c2b")).then_inc(relu2[u].sem, 1)
                        inverse(i, u, 2)
                    for u in two:
                        act.wait_ge(conv3[u].sem, conv3[u].at(i + 1))
                        for part in range(2):
                            ins = act.activation(act3[u][:, :, part * 64:part * 64 + 64],
                                                 c3_ps[u][:, part * 128:part * 128 + 128]
                                                 .rearrange("p (g n) -> p g n", g=2),
                                                 ACT.Relu, bias=column(f"tok_c3b{part}"))
                        ins.then_inc(relu3[u].sem, 1)
                        inverse(i, u, 3)
                    for u in two:
                        act.wait_ge(turned[u].sem, turned[u].at(i + 1))
                        act.activation(turned_s[u][:], y_ps[u][:, 0:256].rearrange("p (g n) -> p g n", g=2),
                                       ACT.Copy).then_inc(turned_copied[u].sem, 1)
                    for u in two:
                        act.wait_ge(y_made[u].sem, y_made[u].at(i + 1))
                        act.activation(h[:, bass.ds((2 * i + u) * SEQ + 1, TOKENS_IN)], y_ps[u][:, 256:384],
                                       ACT.Identity, bias=column("tok_out_b")).then_inc(y_written[u].sem, 1)

            @block.vector
            def _(dve):
                dve.tensor_copy(h[:].rearrange("p (j t) -> p j t", t=SEQ)[:, :, 0],
                                column("cls").to_broadcast([P, PAIRS]))
                dve.wait_ge(loaded.sem, loaded.at(96))
                dve.wait_ge(cleared.sem, cleared.at(1))

                def norm(i, u, k, src, n, table, dst):
                    base = 12 * i + 3 * k
                    for g in range(HALVES):
                        ins = dve.bn_stats(stats[u][:, g, :], src[:, g, 0:n])
                    ins.then_inc(chain[u].sem, 1)
                    dve.wait_ge(chain[u].sem, chain[u].at(base + 1))
                    dve.memset(held[:], 0.0)
                    for g in range(HALVES):
                        ins = dve.bn_aggr(moments[u][:, g, :], stats[u][:, g, :])
                    ins.then_inc(measured[u].sem, 1)
                    dve.wait_ge(rstd_ready[u].sem, rstd_ready[u].at(4 * i + k + 1))
                    for g in range(HALVES):
                        ins = dve.tensor_scalar(normed[u][:, g, 0:n], src[:, g, 0:n], moments[u][:, g, 0:1],
                                                rstd[u][:, g:g + 1], ALU.subtract, ALU.mult)
                    ins.then_inc(chain[u].sem, 1)
                    dve.wait_ge(chain[u].sem, chain[u].at(base + 2))
                    both = lambda m: table[:, m:m + 1, 0:n].to_broadcast([P, HALVES, n])
                    dve.tensor_tensor(scaled_by[u][:, :, 0:n], normed[u][:, :, 0:n], both(0),
                                      ALU.mult).then_inc(chain[u].sem, 1)
                    dve.wait_ge(chain[u].sem, chain[u].at(base + 3))
                    for g in range(HALVES):
                        ins = dve.tensor_tensor(dst(g), shaped(scaled_by[u][:, g, 0:n], k),
                                                shaped(table[:, 1, 0:n], k), ALU.add)
                    return ins

                def shaped(ap, k):
                    return ap if k == 3 else ap.rearrange("p (h w) -> p h w", h=JOINTS)

                with dve.Fori(0, n2) as i:
                    for u in two:
                        dve.wait_ge(landed[u].sem, landed[u].at(16 * i + 16))
                        norm(i, u, 0, x_in[u], 192, ln0, lambda g: pad1[u][:, g, 2:66, 1:4]).then_inc(
                            padded1[u].sem, 1)
                    for u in two:
                        dve.wait_ge(relu1[u].sem, relu1[u].at(i + 1))
                        norm(i, u, 1, act1[u], 192, ln0, lambda g: pad2[u][:, g, 2:66, :]).then_inc(
                            padded2[u].sem, 1)
                    for u in two:
                        dve.wait_ge(relu2[u].sem, relu2[u].at(i + 1))
                        norm(i, u, 2, act2[u], 128, ln1, lambda g: pad3[u][:, g, 2:66, :]).then_inc(
                            padded3[u].sem, 1)
                    for u in two:
                        dve.wait_ge(relu3[u].sem, relu3[u].at(i + 1))
                        norm(i, u, 3, act3[u], 128, ln1, lambda g: last[u][:, g, :]).then_inc(
                            last_ready[u].sem, 1)



THIRD = SEQ // 3
WIDE_HEADS = 3
SLICES = 3


def thirds_attention_phase(tower, h, xn, column):
    nc, n2, two = tower.nc, PAIRS // 2, range(2)
    heads = WIDE_HEADS
    qk = 2 * THIRD
    add_phase(tower, h, xn)
    with phase(tower) as ph:
        we = ph.sb("we", [P, heads, SLICES, P])
        be = ph.sb("be", [P, heads, SLICES])
        bv = ph.sb("bv", [THIRD, heads, SLICES * P])
        wo = ph.sb("wo", [P, SLICES, P])
        xs = [ph.sb(f"xs{u}", [P, SEQ]) for u in two]
        e_s = [ph.sb(f"e{u}", [P, heads, SLICES, qk]) for u in two]
        v_s = [ph.sb(f"v{u}", [THIRD, heads, SLICES, P]) for u in two]
        peak = [ph.sb(f"peak{u}", [THIRD, HALVES, heads]) for u in two]
        total = [ph.sb(f"total{u}", [THIRD, HALVES, heads]) for u in two]
        prob = [ph.sb(f"prob{u}", [THIRD, HALVES, heads, THIRD]) for u in two]
        prob_t = [ph.sb(f"prob_t{u}", [THIRD, HALVES, heads, THIRD]) for u in two]
        o_s = [ph.sb(f"o{u}", [P, SLICES, SEQ]) for u in two]
        e_ps, s_ps, v_ps = [[ph.ps(f"{n}{r}") for r in two] for n in ("e", "s", "v")]
        t_ps, o_ps = ph.ps("t"), ph.ps("o")
        loaded = ph.counts(64)
        copied = ph.counts(2 * n2)
        e_made, e_read = ph.counts(6 * n2), ph.counts(6 * n2)
        s_made, s_peaked, s_read = ph.counts(4 * n2), ph.counts(4 * n2), ph.counts(4 * n2)
        v_made, v_read = ph.counts(6 * n2), ph.counts(6 * n2)
        exped, summed, inverted, prob_ready = [ph.counts(2 * n2) for _ in range(4)]
        turned, turned_read = ph.counts(2 * n2), ph.counts(2 * n2)
        o_made, o_read, y_made, y_read = [ph.counts(2 * n2) for _ in range(4)]

        def cols(i, u):
            return bass.ds((2 * i + u) * SEQ, SEQ)

        def half(g):
            return slice(D * g, D * g + D)

        with nc.Block() as block:
            @block.sync
            def _(sp):
                for buf, name in ((we, "L0_we"), (be, "L0_be"), (bv, "L0_bv"), (wo, "L0_wo")):
                    sp.dma_start(buf[:], tower.dram[name]).then_inc(loaded.sem, 16)

            @block.gpsimd
            def _(pool):
                with pool.Fori(0, n2) as i:
                    for u in two:
                        pool.wait_ge(v_made.sem, v_made.at(6 * i + 3 * u - 3))
                        pool.tensor_copy(xs[u][:], xn[:, cols(i, u)]).then_inc(copied.sem, 1)

            @block.tensor
            def _(pe):
                pe.wait_ge(loaded.sem, loaded.at(64))
                with pe.Fori(0, n2) as i:
                    for u in two:
                        pe.wait_ge(copied.sem, copied.at(2 * i + u + 1))
                        for hd in range(heads):
                            n = 3 * u + hd
                            pe.wait_ge(e_read.sem, e_read.at(6 * i + n - 1))
                            for c in range(SLICES):
                                mm = pe.matmul(e_ps[n % 2][:, c * qk:(c + 1) * qk], we[:, hd, c, :],
                                               xs[u][:, 0:qk], start=True, stop=True)
                            mm.then_inc(e_made.sem, 1)
                    for u in two:
                        pe.wait_ge(e_read.sem, e_read.at(6 * i + 3 * u + 3))
                        for g in range(HALVES):
                            if u == 0:
                                pe.wait_ge(y_read.sem, y_read.at(2 * i))
                            pe.wait_ge(s_read.sem, s_read.at(4 * i + 2 * u + g - 1))
                            for hd in range(heads):
                                for c in range(SLICES):
                                    mm = pe.matmul(s_ps[g][0:qk, hd * THIRD:(hd + 1) * THIRD],
                                                   e_s[u][half(g), hd, c, :],
                                                   e_s[u][half(g), hd, c, THIRD:qk],
                                                   start=c == 0, stop=c == SLICES - 1)
                            mm.then_inc(s_made.sem, 1)
                        for hd in range(heads):
                            n = 3 * u + hd
                            pe.wait_ge(v_read.sem, v_read.at(6 * i + n - 1))
                            pe.matmul(v_ps[n % 2][0:THIRD, 0:SLICES * P], xs[u][:, qk:SEQ],
                                      we[:, hd, :, :].rearrange("p c n -> p (c n)"),
                                      start=True, stop=True).then_inc(v_made.sem, 1)
                    for u in two:
                        pe.wait_ge(prob_ready.sem, prob_ready.at(2 * i + u + 1))
                        pe.wait_ge(turned_read.sem, turned_read.at(2 * i + u))
                        pe.matmul(t_ps[:, 0:2], tower.ident[:], tower.ident[:, 0:2], start=True, stop=True)
                        for g in range(HALVES):
                            for hd in range(heads):
                                at = (g * heads + hd) * THIRD
                                mm = pe.transpose(t_ps[0:THIRD, at:at + THIRD], prob[u][:, g, hd, :],
                                                  tower.ident[0:THIRD, 0:THIRD])
                        mm.then_inc(turned.sem, 1)
                    for u in two:
                        pe.wait_ge(turned_read.sem, turned_read.at(2 * i + u + 1))
                        pe.wait_ge(v_read.sem, v_read.at(6 * i + 3 * u + 3))
                        pe.wait_ge(o_read.sem, o_read.at(2 * i + u))
                        pe.matmul(o_ps[:, 0:2], tower.ident[:], tower.ident[:, 0:2], start=True, stop=True)
                        for g in range(HALVES):
                            for c in range(SLICES):
                                for hd in range(heads):
                                    at = c * SEQ + hd * THIRD
                                    mm = pe.matmul(o_ps[half(g), at:at + THIRD], v_s[u][:, hd, c, half(g)],
                                                   prob_t[u][:, g, hd, :], start=True, stop=True)
                        mm.then_inc(o_made.sem, 1)
                    for u in two:
                        pe.wait_ge(o_read.sem, o_read.at(2 * i + u + 1))
                        for c in range(SLICES):
                            mm = pe.matmul(s_ps[u][:, 0:SEQ], wo[:, c, :], o_s[u][:, c, :],
                                           start=c == 0, stop=c == SLICES - 1)
                        mm.then_inc(y_made.sem, 1)

            @block.scalar
            def _(act):
                with act.Fori(0, n2) as i:
                    for u in two:
                        act.wait_ge(s_read.sem, s_read.at(4 * i + 2 * u + 2))
                        act.activation(prob[u][:], prob[u][:], ACT.Exp, scale=D ** -0.5).then_inc(exped.sem, 1)
                    for u in two:
                        act.wait_ge(turned.sem, turned.at(2 * i + u + 1))
                        act.activation(prob_t[u][:], t_ps[0:THIRD, 0:6 * THIRD]
                                       .rearrange("p (g h n) -> p g h n", g=2, h=heads),
                                       ACT.Copy).then_inc(turned_read.sem, 1)
                    for u in two:
                        act.wait_ge(o_made.sem, o_made.at(2 * i + u + 1))
                        act.activation(o_s[u][:], o_ps[:, 0:SLICES * SEQ].rearrange("p (c n) -> p c n", c=SLICES),
                                       ACT.Copy).then_inc(o_read.sem, 1)

            @block.vector
            def _(dve):
                dve.wait_ge(loaded.sem, loaded.at(64))
                with dve.Fori(0, n2) as i:
                    for u in two:
                        for hd in range(heads):
                            n = 3 * u + hd
                            dve.wait_ge(e_made.sem, e_made.at(6 * i + n + 1))
                            dve.tensor_tensor(e_s[u][:, hd, :, :],
                                              e_ps[n % 2][:, 0:SLICES * qk].rearrange("p (c n) -> p c n", c=SLICES),
                                              be[:, hd, :][:, :, None].to_broadcast([P, SLICES, qk]),
                                              ALU.add).then_inc(e_read.sem, 1)
                    for u in two:
                        for g in range(HALVES):
                            step = 4 * i + 2 * u + g
                            s = s_ps[g][0:THIRD, 0:heads * THIRD].rearrange("p (h n) -> p h n", h=heads)
                            dve.wait_ge(s_made.sem, s_made.at(step + 1))
                            dve.tensor_reduce(peak[u][:, g, :], s, AX, ALU.max).then_inc(s_peaked.sem, 1)
                            dve.wait_ge(s_peaked.sem, s_peaked.at(step + 1))
                            dve.tensor_tensor(prob[u][:, g, :, :], s,
                                              peak[u][:, g, :][:, :, None].to_broadcast([THIRD, heads, THIRD]),
                                              ALU.subtract).then_inc(s_read.sem, 1)
                        for hd in range(heads):
                            n = 3 * u + hd
                            dve.wait_ge(v_made.sem, v_made.at(6 * i + n + 1))
                            dve.tensor_tensor(v_s[u][:, hd, :, :].rearrange("p c n -> p (c n)"),
                                              v_ps[n % 2][0:THIRD, 0:SLICES * P], bv[:, hd, :],
                                              ALU.add).then_inc(v_read.sem, 1)
                    for u in two:
                        step = 2 * i + u + 1
                        dve.wait_ge(exped.sem, exped.at(step))
                        dve.tensor_reduce(total[u][:], prob[u][:], AX, ALU.add).then_inc(summed.sem, 1)
                        dve.wait_ge(summed.sem, summed.at(step))
                        dve.reciprocal(total[u][:], total[u][:]).then_inc(inverted.sem, 1)
                        dve.wait_ge(inverted.sem, inverted.at(step))
                        flat = prob[u][:].rearrange("p g h n -> p (g h) n")
                        dve.tensor_tensor(flat, flat, total[u][:].rearrange("p g h -> p (g h)")[:, :, None]
                                          .to_broadcast([THIRD, 6, THIRD]), ALU.mult).then_inc(prob_ready.sem, 1)
                    for u in two:
                        dve.wait_ge(y_made.sem, y_made.at(2 * i + u + 1))
                        dve.scalar_tensor_tensor(h[:, cols(i, u)], s_ps[u][:, 0:SEQ], column("L0_b_out"),
                                                 h[:, cols(i, u)], ALU.add, ALU.add).then_inc(y_read.sem, 1)


def head_columns(w, head_rows, rows_of):
    out = np.zeros((D, D), np.float32)
    out[:, rows_of] = w[head_rows].T
    return out


def lay_out_attention(a, name, wq, wk, wv, wo, q_at, kv_rows, swap, width):
    heads = len(q_at)
    q = np.zeros((D, heads, D), np.float32)
    o = np.zeros((D, heads, D), np.float32)
    for h, at in enumerate(q_at):
        q[:, h, at] = wq[h * width:(h + 1) * width].T
        o[at, h] = wo[:, h * width:(h + 1) * width].T
    k, v = np.zeros((D, D), np.float32), np.zeros((D, D), np.float32)
    k[:, :kv_rows], v[:, :kv_rows] = wk.T, wv.T
    stack = lambda w: np.stack([diag(w[:, h]) for h in range(heads)], 1)
    a[f"{name}_wq"], a[f"{name}_wk"], a[f"{name}_wo"] = stack(q), diag(k), stack(o)
    a[f"{name}_wv"] = diag(v)
    if swap is not None:
        a[f"{name}_wq_turned"], a[f"{name}_wk_turned"] = stack(q[:, :, swap]), diag(k[:, swap])


def lay_out_network(a, name, w1, b1, w2):
    parts = w1.shape[1] // P
    up, down = np.zeros((P, HALVES, parts, P), np.float32), np.zeros((P, HALVES, parts, P), np.float32)
    bias = np.zeros((P, HALVES, parts), np.float32)
    for g in range(HALVES):
        for k in range(parts):
            at = slice(k * P, (k + 1) * P)
            up[D * g:D * g + D, g, k] = w1[:, at]
            down[:, g, k] = into_half(w2[at], g)
            bias[:, g, k] = b1[at]
    a[f"{name}_up"], a[f"{name}_down"] = up.reshape(P, -1, P), down.reshape(P, -1, P)
    a[f"{name}_up_b"] = bias.reshape(P, -1)


def lay_out_layers(a, t, f):
    two = lambda v: np.concatenate([v, v])
    pos = np.arange(SEQ, dtype=np.float32)[:, None]
    div = np.exp(np.arange(0, D, 2, dtype=np.float32) * np.float32(-np.log(10000.0) / D)).astype(np.float32)
    pe = np.zeros((SEQ, D), np.float32)
    pe[:, 0::2], pe[:, 1::2] = np.sin(pos * div), np.cos(pos * div)
    a["L1_pos"] = two(pe.T)
    a["L1_blocks"] = np.kron(np.eye(16), np.ones((8, 8))) * 8 ** -0.5
    for l in range(4):
        for n in "qkvo":
            a[f"L1_w{n}{l}"] = diag(f(f"L1_attn_W{n}")[l])
        lay_out_network(a, "L1l", f("L1_attn_W1")[l], f("L1_attn_bf1")[l], f("L1_attn_W2")[l])
        for n in ("up", "down", "up_b"):
            a[f"L1_{n}{l}"] = a.pop(f"L1l_{n}")
    a["L1f_wr"] = diag(f("L1_ffn_wr"))
    a["L1f_br"] = two(f("L1_ffn_br"))[:, None]
    lay_out_network(a, "L1f", f("L1_ffn_w1"), f("L1_ffn_b1"), f("L1_ffn_w2"))
    q_at = [np.arange(16 * h, 16 * h + 16) for h in range(4)]
    lay_out_attention(a, "L2a", f("L2_attn_Wq"), f("L2_attn_Wk"), f("L2_attn_Wv"), f("L2_attn_Wo"),
                      q_at, D, None, 16)
    bias = np.zeros((D, 6), np.float32)
    bias[:, 0] = f("L2_attn_bk")
    for h in range(4):
        bias[q_at[h], 1 + h] = f("L2_attn_bq")[q_at[h]]
    bias[:, 5] = f("L2_attn_bv")
    a["L2a_bias"] = two(bias)
    q_at = [np.arange(16 * (h // 2), 16 * (h // 2) + 16) for h in range(4)]
    row = np.arange(D)
    swap = row // 16 * 16 + (row % 16 + 8) % 16
    lay_out_attention(a, "L2f", f("L2_ffn_wq"), f("L2_ffn_wk"), f("L2_ffn_wv"), f("L2_ffn_wo"),
                      q_at, 32, swap, 16)
    freq = (1.0 / 10000.0 ** (np.arange(0, 16, 2, dtype=np.float32) / 16)).astype(np.float32)
    angle = np.outer(np.tile(freq, 8), np.arange(SEQ, dtype=np.float32))
    sign = np.where(row % 16 < 8, -1.0, 1.0)[:, None]
    a["L2f_cos"], a["L2f_sin"] = two(np.cos(angle)), two(sign * np.sin(angle))
    wkv = f("L3_attn_wkv")
    lay_out_attention(a, "L3a", f("L3_attn_wq"), wkv[:D], wkv[D:], f("L3_attn_wo"),
                      [row] * 16, D, row ^ 1, D)
    freq = 10000.0 ** (-2.0 * np.arange(32, dtype=np.float32) / D)
    angle = np.outer(np.repeat(freq, 2), np.arange(SEQ, dtype=np.float32))
    sign = np.where(row % 2 == 0, -1.0, 1.0)[:, None]
    a["L3a_cos"], a["L3a_sin"] = two(np.cos(angle)), two(sign * np.sin(angle))
    a["L3a_norm_w"] = two(np.stack([f("L3_attn_k_norm_w"), f("L3_attn_q_norm_w")], 1))
    w1, w3, w2 = f("L2_ffn_w1"), f("L2_ffn_w3"), f("L2_ffn_w2")
    ups = [np.zeros((P, EXPERTS, SLABS * SLAB), np.float32) for _ in range(2)]
    down = np.zeros((EXPERTS, SLABS * SLAB, P), np.float32)
    for g in range(HALVES):
        at = slice(HIDDEN * g, HIDDEN * (g + 1))
        for up, w in zip(ups, (w1, w3)):
            up[D * g:D * (g + 1), :, at] = w.transpose(2, 0, 1)
        down[:, at, D * g:D * (g + 1)] = w2.transpose(0, 2, 1)
    a["L2m_w1"], a["L2m_w3"] = [up.reshape(P, EXPERTS * SLABS, SLAB) for up in ups]
    a["L2m_w2"] = down.reshape(EXPERTS * SLABS, SLAB, P).transpose(1, 0, 2)
    pick = np.zeros((P, EXPERTS, P))
    for g in range(HALVES):
        for e in range(EXPERTS):
            pick[32 * g + e, e, D * g:D * (g + 1)] = 1.0
    a["L2m_pick"] = pick
    pick = np.zeros((D, 2, HALVES))
    for g in range(HALVES):
        pick[32 * g:32 * g + 8, 0, g] = 1.0
        pick[32 * g + 8:32 * g + 16, 1, g] = 1.0
    a["L3_pick"] = pick
    tap = lambda w: f(w).transpose(1, 2, 3, 0).reshape(P, -1, f(w).shape[0])
    a["tok_c1w"], a["tok_c2w"] = tap("L0_tok_conv1_w"), tap("L0_tok_conv2_w")
    a["tok_c3w"] = tap("L0_tok_conv3_w").reshape(P, 10, 2, P)
    a["tok_ow"] = np.stack([into_half(f("L0_tok_out_w"), g) for g in range(HALVES)], 1)
    for n in range(2):
        both = np.stack([f(f"L0_tok_ln{n}_g"), f(f"L0_tok_ln{n}_b")])
        a[f"tok_ln{n}"] = np.broadcast_to(both, (P,) + both.shape)
    a["tok_x"] = f("x").reshape(HALVES, PAIRS, P, 192).transpose(1, 2, 0, 3)
    we, be = f("L0_attn_W_embed"), f("L0_attn_b_embed")
    a["L0_we"] = np.stack([np.stack([diag(we[n, D * c:D * c + D].T) for c in range(3)], 1) for n in range(3)], 1)
    cut = be.reshape(3, 3, D)
    a["L0_be"] = np.concatenate([cut, cut], 2).transpose(2, 0, 1)
    a["L0_bv"] = np.broadcast_to(np.concatenate([cut, cut], 2).reshape(3, 3 * P), (SEQ // 3, 3, 3 * P))
    a["L0_wo"] = np.stack([diag(f("L0_attn_W_out")[:, D * c:D * c + D].T) for c in range(3)], 1)



SEMAPHORES = 64


def tower_program(nc, dram, out, stages):
    with ExitStack() as stack:
        handles = [nc.alloc_semaphore(name=f"signal{n}") for n in range(SEMAPHORES)]
        tower = Tower(nc, dram, handles)

        def keep(name, shape, dtype=F32):
            return stack.enter_context(nc.sbuf_tensor(name, shape, dtype))

        h = keep("h", [P, COLS])
        xn = keep("xn", [P, COLS])
        tower.ident, tower.center, tower.average = [keep(n, [P, P]) for n in ("ident", "center", "average")]
        tower.rank8 = keep("rank8", [P, EXPERTS])
        tower.head_blocks = keep("head_blocks", [P, P])
        tower.spread2 = keep("spread2", [HALVES, P])
        tower.later = keep("later", [P, SEQ], BF16)
        tower.place = keep("place", [P, P], BF16)
        tower.ones = keep("ones", [P, P], BF16)
        wide_later, wide_place = keep("wide_later", [P, SEQ]), keep("wide_place", [P, P])
        columns = keep("columns", [P, len(COLUMNS)])
        eps_cols = keep("eps_cols", [P, 3])
        tower.eps = {1e-5: eps_cols[:, 0:1], 1e-6: eps_cols[:, 1:2], 1.1920929e-07: eps_cols[:, 2:3]}

        def column(name):
            n = COLUMNS.index(name)
            return columns[:, n:n + 1]

        loaded = nc.alloc_semaphore(name="constants_loaded")
        stored = nc.alloc_semaphore(name="output_stored")
        with nc.Block() as block:
            @block.sync
            def _(sp):
                consts = [(tower.ident, "ident"), (tower.center, "center"), (tower.average, "average"),
                          (tower.rank8, "rank8"), (columns, "columns"),
                          (tower.spread2, "spread2"), (wide_later, "later"), (wide_place, "place")]
                if "h_in" in dram:
                    consts.append((h, "h_in"))
                for buf, name in consts:
                    sp.dma_start(buf[:], dram[name]).then_inc(loaded, 16)
                for s in handles:
                    sp.sem_inc(s, CREDIT)
                sp.wait_ge(loaded, 16 * len(consts))

            @block.gpsimd
            def _(pool):
                pool.memset(tower.ones[:], 1.0)
                for n, eps in enumerate((1e-5, 1e-6, 1.1920929e-07)):
                    pool.memset(eps_cols[:, n:n + 1], eps)

        with nc.Block() as block:
            @block.vector
            def _(dve):
                dve.tensor_copy(tower.later[:], wide_later[:])
                dve.tensor_copy(tower.place[:], wide_place[:])

        if "L0_tok" in stages:
            tokenizer_phase(tower, h, column)
        if "L0_attn" in stages:
            norm_phase(tower, h, xn, 1e-5)
            thirds_attention_phase(tower, h, xn, column)
        if "L0_ffn" in stages:
            norm_phase(tower, h, xn, 1e-5)
            with ExitStack() as moe:
                rows_t = moe.enter_context(nc.sbuf_tensor("marks0", [64, COLS], F32))
                aug = [moe.enter_context(nc.sbuf_tensor(f"aug0{g}", [104, COLS], F32)) for g in range(HALVES)]
                gate_phase(tower, xn, "L0_gate_w", "L0_gate_b", 2, False, rows_t)
                spread_phase(tower, xn, rows_t, aug)
                mlp_phase(tower, "L0_up", "L0_down", "L0_up_b", 2 * EXPERTS, ACT.Gelu, 72,
                          lambda b: aug[b % 2], AddTo(h), None, extra=("L0_down_b", 104, aug),
                          up_of=lambda b: b // HALVES)
        if "L1_attn" in stages:
            norm_phase(tower, h, xn, 1e-5)
            linear_tower(tower, nc, h, xn, column)
        if "L1_ffn" in stages:
            norm_phase(tower, h, xn, 1e-5)
            half_ffn(tower, nc, h, xn, column)
        if "L2_attn" in stages:
            norm_phase(tower, h, xn, 1e-5)
            with nc.Block() as block:
                @block.vector
                def _(dve):
                    dve.tensor_scalar(xn[:], xn[:], -10000.0, 10000.0, ALU.max, ALU.min)
            attention_phase(tower, xn, h, ATTENTION["L2a"], column("L2_bo"))
        if "L2_ffn" in stages:
            norm_phase(tower, h, xn, 1e-5)
            routed_block(tower, nc, h, xn, column)
        if "L3_attn" in stages:
            norm_phase(tower, h, xn, 1e-5)
            attention_phase(tower, xn, h, ATTENTION["L3a"])
        if "L3_ffn" in stages:
            norm_phase(tower, h, xn, 1e-5)
            capacity_ffn(tower, nc, h, xn)
        with nc.Block() as block:
            @block.sync
            def _(sp):
                sp.dma_start(out, h[:]).then_inc(stored, 16)
                sp.wait_ge(stored, 16)



COLUMNS = ["cls", "tok_out_b", "L0_b_out"] + \
    [f"L1_{n}{l}" for l in range(4) for n in ("bo", "g1", "b1", "bf2", "g2", "b2")] + \
    ["L1f_b2", "L2_bo", "L2_ln1", "L2_ln2", "tok_c1b", "tok_c2b", "tok_c3b0", "tok_c3b1"]


def diag(w):
    k, m = w.shape
    out = np.zeros((2 * k, 2 * m), np.float32)
    out[:k, :m], out[k:, m:] = w, w
    return out


def into_half(w, g):
    out = np.zeros((w.shape[0], P), np.float32)
    out[:, D * g:D * g + D] = w
    return out


def lay_out(t):
    f = lambda name: np.asarray(t[name])
    two = lambda v: np.concatenate([v, v])
    a = {}
    same = np.kron(np.eye(2), np.ones((D, D))) / D
    a["ident"], a["center"], a["average"] = np.eye(P), np.eye(P) - same, same
    a["spread2"] = np.kron(np.eye(2), np.ones((1, D)))
    a["later"] = np.where(np.arange(SEQ)[None, :] > np.arange(P)[:, None], float(-BIG), 0.0)
    a["place"] = np.eye(P)
    a["rank8"] = np.broadcast_to(8.0 - np.arange(8), (P, 8))
    col = {"cls": two(f("cls_tok").reshape(D)), "tok_out_b": two(f("L0_tok_out_b")),
           "L0_b_out": two(f("L0_attn_b_out")), "L1f_b2": two(f("L1_ffn_b2")), "L2_bo": two(f("L2_attn_bo")),
           "L2_ln1": two(f("L2_ffn_ln1_w")), "L2_ln2": two(f("L2_ffn_ln2_w")),
           "tok_c1b": f("L0_tok_conv1_b"), "tok_c2b": f("L0_tok_conv2_b"),
           "tok_c3b0": f("L0_tok_conv3_b")[:P], "tok_c3b1": f("L0_tok_conv3_b")[P:]}
    for l in range(4):
        for n in ("bo", "g1", "b1", "bf2", "g2", "b2"):
            col[f"L1_{n}{l}"] = two(f(f"L1_attn_{n}")[l])
    a["columns"] = np.stack([col[n] for n in COLUMNS], 1)

    for p, w, b in (("L0", f("L0_ffn_Wg"), f("L0_ffn_bg")), ("L2", f("L2_ffn_router_w").T, np.zeros(8)),
                    ("L3", f("L3_ffn_gate_w"), f("L3_ffn_gate_b"))):
        a[f"{p}_gate_w"], a[f"{p}_gate_b"] = diag(w), np.broadcast_to(two(b), (CHUNK, 16))

    for p, w1, b1, w2, b2 in (("L0", "L0_ffn_W1", "L0_ffn_b1", "L0_ffn_W2", "L0_ffn_b2"),
                              ("L3", "L3_ffn_w1", "L3_ffn_b1", "L3_ffn_w2", "L3_ffn_b2")):
        w1, b1, w2, b2 = f(w1), f(b1), f(w2), f(b2)
        parts = w1.shape[2] // P
        up = np.zeros((72, EXPERTS * parts, P), np.float32)
        down = np.zeros((P, EXPERTS * parts, HALVES, P), np.float32)
        for e in range(EXPERTS):
            for k in range(parts):
                n = e * parts + k
                up[0:D, n] = w1[e][:, k * P:(k + 1) * P]
                up[D + e, n] = BIG
                for g in range(HALVES):
                    down[:, n, g] = into_half(w2[e][k * P:(k + 1) * P], g)
        a[f"{p}_up"] = up
        a[f"{p}_down"] = down.reshape(P, -1, P)
        a[f"{p}_up_b"] = b1.reshape(EXPERTS * parts, P).T
        extra = np.zeros((104, HALVES, P), np.float32)
        for g in range(HALVES):
            extra[96:104, g] = into_half(b2, g)
        a[f"{p}_down_b"] = extra
    lay_out_layers(a, t, f)
    return {n: np.ascontiguousarray(v.astype(np.float32) if v.dtype == np.float64 else v) for n, v in a.items()}


def kernel(**inputs):
    import concourse.bacc as _bacc
    from concourse.bass_utils import run_bass_kernel_spmd as _run
    nc = _bacc.Bacc("TRN2", target_bir_lowering=False, num_devices=1)
    arrays = {f"in_{n}": v for n, v in lay_out(inputs).items()}
    dram = {n[3:]: nc.dram_tensor(n, v.shape, mybir.dt.from_np(v.dtype), kind="ExternalInput").ap()
            for n, v in arrays.items()}
    out = nc.dram_tensor("out_0", (P, COLS), F32, kind="ExternalOutput").ap()
    tower_program(nc, dram, out, STAGES)
    got = np.asarray(_run(nc, [arrays], core_ids=[0]).results[0]["out_0"])
    return got.reshape(HALVES, D, PAIRS, SEQ).transpose(0, 2, 3, 1).reshape(HALVES * PAIRS, SEQ, D)


STAGES = ["L0_tok", "L0_attn", "L0_ffn", "L1_attn", "L1_ffn", "L2_attn", "L2_ffn", "L3_attn", "L3_ffn"]
```
